# Optimizing a Trainium2 kernel written in Bass

```python
import numpy as np
import jax
import jax.numpy as jnp

def _softmax(x, axis=-1):
    return jax.nn.softmax(x, axis=axis)

def _gelu(x):
    return jax.nn.gelu(x, approximate=True)

def _silu(x):
    return jax.nn.silu(x)

def _sigmoid(x):
    return jax.nn.sigmoid(x)

def _layernorm(x, axis=-1, eps=1e-05):
    m = jnp.mean(x, axis=axis, keepdims=True)
    v = jnp.var(x, axis=axis, keepdims=True)
    return (x - m) / jnp.sqrt(v + eps)

def _scatter_add(tgt, idx, src, axis=0):
    return tgt.at[idx].add(src)

def _segment_sum(src, seg, n):
    return jax.ops.segment_sum(src, seg, n)
kernel_name = 'mk_gnn_resnorm_d4_gnn_r16_7b1b7b'

def setup_inputs(seed: int=0):
    np.random.seed(seed)
    _w = jnp.asarray

    def _rec_inputs():
        import jax
        import jax.numpy as jnp
        _gk = jax.random.key(seed)
        x = -8.776e-05 + 1 * jax.random.normal(jax.random.fold_in(_gk, 1), (3125, 128), jnp.float32)
        src = jax.random.randint(jax.random.fold_in(_gk, 2), (100000,), 0, 3125, jnp.int32)
        dst = jnp.minimum((3125 * jax.random.uniform(jax.random.fold_in(_gk, 3), (100000,)) ** 2.0).astype(jnp.int32), 49999)
        _o = jnp.argsort(dst, stable=True)
        src = src[_o]
        dst = dst[_o]
        edge_attr_16 = -5.3897e-05 + 0.999841 * jax.random.normal(jax.random.fold_in(_gk, 11), (100000, 16), jnp.float32)
        edge_type_9 = jax.random.randint(jax.random.fold_in(_gk, 14), (100000,), 0, 9, jnp.int32)
        return (x, src, dst, edge_attr_16, edge_type_9)
    x, src, dst, edge_attr_16, edge_type_9 = _rec_inputs()

    def _L0_gnn_setup():
        import jax, jax.numpy as jnp
        import numpy as np
        N_NODES = 2500
        N_EDGES = 40000
        IN_DIM, HID_DIM, OUT_DIM = (128, 256, 128)
        key = jax.random.key(seed)
        ks = jax.random.split(key, 8)
        x = jax.random.normal(ks[0], (N_NODES, IN_DIM), dtype=jnp.float32)
        edge_index = jax.random.randint(ks[1], (2, N_EDGES), 0, N_NODES, dtype=jnp.int64)

        def glorot(k, fan_in, fan_out):
            lim = 1.0 / np.sqrt(fan_in)
            return jax.random.uniform(k, (fan_in, fan_out), dtype=jnp.float32, minval=-lim, maxval=lim)
        W0 = glorot(ks[2], IN_DIM, HID_DIM)
        W1 = glorot(ks[3], HID_DIM, HID_DIM)
        W2 = glorot(ks[4], HID_DIM, OUT_DIM)
        b0 = jnp.zeros((HID_DIM,), dtype=jnp.float32)
        b1 = jnp.zeros((HID_DIM,), dtype=jnp.float32)
        b2 = jnp.zeros((OUT_DIM,), dtype=jnp.float32)
        return {'x': x, 'edge_index': edge_index, 'W0': W0, 'b0': b0, 'W1': W1, 'b1': b1, 'W2': W2, 'b2': b2}
    _L0_gnn_all = _L0_gnn_setup()
    _L0_gnn_in = {k: v for k, v in _L0_gnn_all.items() if k in ('W0', 'b0', 'W1', 'b1', 'W2', 'b2')}
    del _L0_gnn_all

    def _L1_gnn_setup():
        import jax, jax.numpy as jnp
        import numpy as np
        N_NODES = 3125
        N_EDGES = 50000
        H = 128
        T = 2
        key = jax.random.key(seed)
        ks = jax.random.split(key, 8)
        s = 0.05
        return {'h': jax.random.normal(ks[0], (N_NODES, H), jnp.float32), 'edges': jax.random.randint(ks[1], (N_EDGES, 2), 0, N_NODES, jnp.int64), 'W_msg': jax.random.normal(ks[2], (T, 2 * H, 2 * H), jnp.float32) * s, 'b_msg': jax.random.normal(ks[3], (T, 2 * H), jnp.float32) * s, 'W_ih': jax.random.normal(ks[4], (T, 3 * H, 2 * H), jnp.float32) * s, 'W_hh': jax.random.normal(ks[5], (T, 3 * H, H), jnp.float32) * s, 'b_ih': jax.random.normal(ks[6], (T, 3 * H), jnp.float32) * s, 'b_hh': jax.random.normal(ks[7], (T, 3 * H), jnp.float32) * s}
    _L1_gnn_all = _L1_gnn_setup()
    _L1_gnn_in = {k: v for k, v in _L1_gnn_all.items() if k in ('W_msg', 'b_msg', 'W_ih', 'W_hh', 'b_ih', 'b_hh')}
    del _L1_gnn_all

    def _L2_gnn_setup():
        import jax, jax.numpy as jnp
        import numpy as np
        NUM_EDGE_TYPES = 8
        HIDDEN = 128
        N_NODES = 3125
        N_EDGES = 37500

        def _gru_cell(x, h, W_ih, W_hh, b_ih, b_hh):
            H = h.shape[-1]
            gi = x @ W_ih.T + b_ih
            gh = h @ W_hh.T + b_hh
            i_r, i_z, i_n = (gi[:, :H], gi[:, H:2 * H], gi[:, 2 * H:])
            h_r, h_z, h_n = (gh[:, :H], gh[:, H:2 * H], gh[:, 2 * H:])
            r = jax.nn.sigmoid(i_r + h_r)
            z = jax.nn.sigmoid(i_z + h_z)
            n = jnp.tanh(i_n + r * h_n)
            return (1.0 - z) * n + z * h
        key = jax.random.key(seed)
        ks = jax.random.split(key, 10)
        H = HIDDEN
        h = jax.random.normal(ks[0], (N_NODES, H), dtype=jnp.float32)
        edge_index = jax.random.randint(ks[1], (2, N_EDGES), 0, N_NODES, dtype=jnp.int32)
        edge_type = jax.random.randint(ks[2], (N_EDGES,), 0, NUM_EDGE_TYPES + 1, dtype=jnp.int32)
        s = 1.0 / np.sqrt(H)
        W_msg = jax.random.uniform(ks[3], (H, H), jnp.float32, -s, s)
        b_msg = jax.random.uniform(ks[4], (H,), jnp.float32, -s, s)
        edge_embed = jax.random.normal(ks[5], (NUM_EDGE_TYPES + 1, H), dtype=jnp.float32)
        W_ih = jax.random.uniform(ks[6], (3 * H, H), jnp.float32, -s, s)
        W_hh = jax.random.uniform(ks[7], (3 * H, H), jnp.float32, -s, s)
        b_ih = jax.random.uniform(ks[8], (3 * H,), jnp.float32, -s, s)
        b_hh = jax.random.uniform(ks[9], (3 * H,), jnp.float32, -s, s)
        return {'h': h, 'edge_index': edge_index, 'edge_type': edge_type, 'num_nodes': N_NODES, 'W_msg': W_msg, 'b_msg': b_msg, 'edge_embed': edge_embed, 'W_ih': W_ih, 'W_hh': W_hh, 'b_ih': b_ih, 'b_hh': b_hh}
    _L2_gnn_all = _L2_gnn_setup()
    _L2_gnn_in = {k: v for k, v in _L2_gnn_all.items() if k in ('W_msg', 'b_msg', 'edge_embed', 'W_ih', 'W_hh', 'b_ih', 'b_hh')}
    del _L2_gnn_all

    def _L3_gnn_setup():
        import jax, jax.numpy as jnp
        import numpy as np
        import math
        N = 6250
        E = 100000
        IN = 128
        H, C = (4, 32)
        ED = 16
        key = jax.random.key(seed)
        ks = jax.random.split(key, 12)
        s = 0.02
        return {'x': jax.random.normal(ks[0], (N, IN), jnp.float32), 'edge_attr': jax.random.normal(ks[1], (E, ED), jnp.float32), 'edge_index': jax.random.randint(ks[2], (2, E), 0, N, dtype=jnp.int32), 'Wq': jax.random.normal(ks[3], (IN, H * C), jnp.float32) * s, 'bq': jnp.zeros((H * C,), jnp.float32), 'Wk': jax.random.normal(ks[4], (IN, H * C), jnp.float32) * s, 'bk': jnp.zeros((H * C,), jnp.float32), 'Wv': jax.random.normal(ks[5], (IN, H * C), jnp.float32) * s, 'bv': jnp.zeros((H * C,), jnp.float32), 'We': jax.random.normal(ks[6], (ED, H * C), jnp.float32) * s, 'Wskip': jax.random.normal(ks[7], (IN, H * C), jnp.float32) * s, 'bskip': jnp.zeros((H * C,), jnp.float32), 'Wbeta': jax.random.normal(ks[8], (3 * H * C, 1), jnp.float32) * s}
    _L3_gnn_all = _L3_gnn_setup()
    _L3_gnn_in = {k: v for k, v in _L3_gnn_all.items() if k in ('Wq', 'bq', 'Wk', 'bk', 'Wv', 'bv', 'We', 'Wskip', 'bskip', 'Wbeta')}
    del _L3_gnn_all
    return {'x': x, 'src': src, 'dst': dst, 'edge_attr_16': edge_attr_16, 'edge_type_9': edge_type_9, 'L0_gnn_W0': _L0_gnn_in['W0'], 'L0_gnn_b0': _L0_gnn_in['b0'], 'L0_gnn_W1': _L0_gnn_in['W1'], 'L0_gnn_b1': _L0_gnn_in['b1'], 'L0_gnn_W2': _L0_gnn_in['W2'], 'L0_gnn_b2': _L0_gnn_in['b2'], 'L1_gnn_W_msg': _L1_gnn_in['W_msg'], 'L1_gnn_b_msg': _L1_gnn_in['b_msg'], 'L1_gnn_W_ih': _L1_gnn_in['W_ih'], 'L1_gnn_W_hh': _L1_gnn_in['W_hh'], 'L1_gnn_b_ih': _L1_gnn_in['b_ih'], 'L1_gnn_b_hh': _L1_gnn_in['b_hh'], 'L2_gnn_W_msg': _L2_gnn_in['W_msg'], 'L2_gnn_b_msg': _L2_gnn_in['b_msg'], 'L2_gnn_edge_embed': _L2_gnn_in['edge_embed'], 'L2_gnn_W_ih': _L2_gnn_in['W_ih'], 'L2_gnn_W_hh': _L2_gnn_in['W_hh'], 'L2_gnn_b_ih': _L2_gnn_in['b_ih'], 'L2_gnn_b_hh': _L2_gnn_in['b_hh'], 'L3_gnn_Wq': _L3_gnn_in['Wq'], 'L3_gnn_bq': _L3_gnn_in['bq'], 'L3_gnn_Wk': _L3_gnn_in['Wk'], 'L3_gnn_bk': _L3_gnn_in['bk'], 'L3_gnn_Wv': _L3_gnn_in['Wv'], 'L3_gnn_bv': _L3_gnn_in['bv'], 'L3_gnn_We': _L3_gnn_in['We'], 'L3_gnn_Wskip': _L3_gnn_in['Wskip'], 'L3_gnn_bskip': _L3_gnn_in['bskip'], 'L3_gnn_Wbeta': _L3_gnn_in['Wbeta']}

def reference(x, src, dst, edge_attr_16, edge_type_9, L0_gnn_W0, L0_gnn_b0, L0_gnn_W1, L0_gnn_b1, L0_gnn_W2, L0_gnn_b2, L1_gnn_W_msg, L1_gnn_b_msg, L1_gnn_W_ih, L1_gnn_W_hh, L1_gnn_b_ih, L1_gnn_b_hh, L2_gnn_W_msg, L2_gnn_b_msg, L2_gnn_edge_embed, L2_gnn_W_ih, L2_gnn_W_hh, L2_gnn_b_ih, L2_gnn_b_hh, L3_gnn_Wq, L3_gnn_bq, L3_gnn_Wk, L3_gnn_bk, L3_gnn_Wv, L3_gnn_bv, L3_gnn_We, L3_gnn_Wskip, L3_gnn_bskip, L3_gnn_Wbeta):
    import jax
    import jax.numpy as jnp

    def _L0_gnn_ref(x, edge_index, W0, b0, W1, b1, W2, b2):
        import jax, jax.numpy as jnp
        import numpy as np
        N_NODES = 2500
        N_EDGES = 40000
        IN_DIM, HID_DIM, OUT_DIM = (128, 256, 128)
        N = x.shape[0]
        loops = jnp.arange(N, dtype=edge_index.dtype)
        row = jnp.concatenate([edge_index[0], loops])
        col = jnp.concatenate([edge_index[1], loops])
        deg = jax.ops.segment_sum(jnp.ones(col.shape[0], dtype=x.dtype), col, num_segments=N)
        dinv = jnp.where(deg > 0, jax.lax.rsqrt(deg), 0.0)
        norm = (dinv[row] * dinv[col])[:, None]

        def gcn_layer(h, W, b):
            hW = h @ W
            msg = norm * hW[row]
            out = jax.ops.segment_sum(msg, col, num_segments=N)
            return out + b
        h = jax.nn.relu(gcn_layer(x, W0, b0))
        h = jax.nn.relu(gcn_layer(h, W1, b1))
        h = gcn_layer(h, W2, b2)
        return h

    def _L1_gnn_ref(h, edges, W_msg, b_msg, W_ih, W_hh, b_ih, b_hh):
        import jax, jax.numpy as jnp
        import numpy as np
        N_NODES = 3125
        N_EDGES = 50000
        H = 128
        T = 2
        n_nodes, hd = h.shape
        src, dst = (edges[:, 0], edges[:, 1])
        deg = jax.ops.segment_sum(jnp.ones(edges.shape[0], h.dtype), dst, num_segments=n_nodes)
        has_msg = (deg > 0)[:, None]
        for t in range(W_msg.shape[0]):
            m_in = jnp.concatenate([h[src], h[dst]], axis=-1)
            m = m_in @ W_msg[t].T + b_msg[t]
            agg = jax.ops.segment_sum(m, dst, num_segments=n_nodes)
            gi = agg @ W_ih[t].T + b_ih[t]
            gh = h @ W_hh[t].T + b_hh[t]
            ir, iz, inn = (gi[:, :hd], gi[:, hd:2 * hd], gi[:, 2 * hd:])
            hr, hz, hn = (gh[:, :hd], gh[:, hd:2 * hd], gh[:, 2 * hd:])
            r = jax.nn.sigmoid(ir + hr)
            z = jax.nn.sigmoid(iz + hz)
            n = jnp.tanh(inn + r * hn)
            h_new = (1.0 - z) * n + z * h
            h = jnp.where(has_msg, h_new, h)
        return h

    def _L2_gnn_ref(h, edge_index, edge_type, num_nodes, W_msg, b_msg, edge_embed, W_ih, W_hh, b_ih, b_hh):
        import jax, jax.numpy as jnp
        import numpy as np
        NUM_EDGE_TYPES = 8
        HIDDEN = 128
        N_NODES = 3125
        N_EDGES = 37500

        def _gru_cell(x, h, W_ih, W_hh, b_ih, b_hh):
            H = h.shape[-1]
            gi = x @ W_ih.T + b_ih
            gh = h @ W_hh.T + b_hh
            i_r, i_z, i_n = (gi[:, :H], gi[:, H:2 * H], gi[:, 2 * H:])
            h_r, h_z, h_n = (gh[:, :H], gh[:, H:2 * H], gh[:, 2 * H:])
            r = jax.nn.sigmoid(i_r + h_r)
            z = jax.nn.sigmoid(i_z + h_z)
            n = jnp.tanh(i_n + r * h_n)
            return (1.0 - z) * n + z * h
        src = edge_index[0]
        dst = edge_index[1]
        src_h = h[src] @ W_msg.T + b_msg
        emb = edge_embed[jnp.clip(edge_type, 0, NUM_EDGE_TYPES)]
        msg = src_h + emb
        messages = jax.ops.segment_sum(msg, dst, num_segments=num_nodes)
        h_new = _gru_cell(messages, h[:num_nodes], W_ih, W_hh, b_ih, b_hh)
        result = jnp.zeros_like(h).at[:num_nodes].set(h_new)
        return result

    def _L3_gnn_ref(x, edge_attr, edge_index, Wq, bq, Wk, bk, Wv, bv, We, Wskip, bskip, Wbeta):
        import jax, jax.numpy as jnp
        import numpy as np
        import math
        N = 6250
        E = 100000
        IN = 128
        H, C = (4, 32)
        ED = 16
        n = x.shape[0]
        q = (x @ Wq + bq).reshape(n, H, C)
        k = (x @ Wk + bk).reshape(n, H, C)
        v = (x @ Wv + bv).reshape(n, H, C)
        row, col = (edge_index[0], edge_index[1])
        k_j = k[col] + (edge_attr @ We).reshape(-1, H, C)
        alpha = jnp.einsum('ehc,ehc->eh', q[row], k_j) / math.sqrt(C)
        m = jnp.zeros((n, H), alpha.dtype).at[row].set(alpha)
        ex = jnp.exp(alpha - m[row])
        denom = jax.ops.segment_sum(ex, row, num_segments=n)
        alpha = ex / (denom[row] + 1e-16)
        msgs = v[col] * alpha[..., None]
        out = jax.ops.segment_sum(msgs, row, num_segments=n)
        out = out.reshape(n, H * C)
        x_skip = x @ Wskip + bskip
        beta = jax.nn.sigmoid(jnp.concatenate([out, x_skip, out - x_skip], axis=-1) @ Wbeta)
        return beta * x_skip + (1.0 - beta) * out
    edge_index = jnp.stack([src, dst])
    edge_index_t = jnp.stack([src, dst], axis=1)
    x = _layernorm(x + _L0_gnn_ref(x, edge_index, L0_gnn_W0, L0_gnn_b0, L0_gnn_W1, L0_gnn_b1, L0_gnn_W2, L0_gnn_b2), axis=-1)
    x = _layernorm(x + _L1_gnn_ref(x, edge_index_t, L1_gnn_W_msg, L1_gnn_b_msg, L1_gnn_W_ih, L1_gnn_W_hh, L1_gnn_b_ih, L1_gnn_b_hh), axis=-1)
    x = _layernorm(x + _L2_gnn_ref(x, edge_index, edge_type_9, 3125, L2_gnn_W_msg, L2_gnn_b_msg, L2_gnn_edge_embed, L2_gnn_W_ih, L2_gnn_W_hh, L2_gnn_b_ih, L2_gnn_b_hh), axis=-1)
    x = _layernorm(x + _L3_gnn_ref(x, edge_attr_16, edge_index, L3_gnn_Wq, L3_gnn_bq, L3_gnn_Wk, L3_gnn_bk, L3_gnn_Wv, L3_gnn_bv, L3_gnn_We, L3_gnn_Wskip, L3_gnn_bskip, L3_gnn_Wbeta), axis=-1)
    return x

_drawn_inputs = setup_inputs


def setup_inputs(seed=0):
    import zlib

    import numpy as np

    out = dict(_drawn_inputs(seed))
    spreads = {'L0_gnn_b0': (0.0, 0.1),
     'L0_gnn_b1': (0.0, 0.1),
     'L0_gnn_b2': (0.0, 0.1),
     'L3_gnn_bq': (0.0, 0.1),
     'L3_gnn_bk': (0.0, 0.1),
     'L3_gnn_bv': (0.0, 0.1),
     'L3_gnn_bskip': (0.0, 0.1)}
    factors = {}
    for name, (base, spread) in spreads.items():
        noise = np.random.default_rng([zlib.crc32(name.encode()), seed]).standard_normal(out[name].shape)
        drawn = base * np.exp(spread * noise) if base else spread * noise
        out[name] = jnp.asarray(drawn.astype(out[name].dtype))
    for name, factor in factors.items():
        out[name] = (out[name] * factor).astype(out[name].dtype)
    return out
```

```python
from contextlib import ExitStack

import concourse.bass as bass
import concourse.mybir as mybir
import numpy as np

ALU = mybir.AluOpType
ACT = mybir.ActivationFunctionType
AX = mybir.AxisListType
F32, BF16, F16 = mybir.dt.float32, mybir.dt.bfloat16, mybir.dt.float16
I32, U8 = mybir.dt.int32, mybir.dt.uint8

P = 128
N, E, D = 3125, 100000, 128
NTYPE = 9
DE = 16
W = 112
NB = -(-N // W)
NP = NB * W
LASTROWS = N - (NB - 1) * W
BPC = 4
CH = BPC * W
NCH = NP // CH
ECOLS = -(-E // P)
ETAIL = E - (P - 1) * ECOLS
TG = 6
GE = TG * P
NG = P * ECOLS // GE + NB
REC = 20
R_SRC, R_DSTI, R_DSTC, R_TYPE = 16, 17, 18, 19
NO_SRC, NO_TYPE = float(W + 3), 100.0
CENTER = NP // 2
MAGIC = 1.5 * 2.0 ** 23
HEADS, HD = 4, 32
QW = D + HEADS * DE + HEADS
MW = D + HEADS
EPS_LN = 1e-5

B_L0_0, B_L0_1, B_L0_2 = 0, 2, 4
B_L1 = 5
B_L2 = 17
NBIAS = 23


class Progress:

    def __init__(self, sem):
        self.sem, self.n = sem, 0

    def mark(self, ins):
        self.n += 1
        ins.then_inc(self.sem, 1)
        return (self.sem, self.n)


class Slot:

    def __init__(self, sem):
        self.sem, self.n = sem, 0

    def mark(self, ins):
        self.n += 16
        ins.then_inc(self.sem, 16)
        return (self.sem, self.n)


NOT_YET = "not issued yet"


def need(engine, *tokens):
    for t in tokens:
        if t is not None:
            assert t is not NOT_YET, "the producer comes later in the program"
            engine.wait_ge(t[0], t[1])


class Ctx:

    def __init__(self, nc, ctx, io):
        self.nc, self.ctx, self.io = nc, ctx, io
        self.pe, self.dve, self.act, self.pool, self.sp = nc.tensor, nc.vector, nc.scalar, nc.gpsimd, nc.sync
        self.PE, self.DVE, self.ACT, self.POOL = (
            Progress(ctx.enter_context(nc.semaphore(n))) for n in ("pe_done", "dve_done", "act_done", "pool_done"))

    def slot(self, name):
        return Slot(self.ctx.enter_context(self.nc.semaphore(name)))

    def dram(self, name, shape, dt):
        return self.nc.dram_tensor(name, shape, dt, kind="Internal").ap()


def edge_rows(ap, cols=1):
    whole = ap[0:(P - 1) * ECOLS * cols].rearrange("(p j) -> p j", j=ECOLS * cols)
    tail = ap[(P - 1) * ECOLS * cols:E * cols].rearrange("(p j) -> p j", p=1)
    return [(0, 112, whole[0:112, :]), (112, P - 1, whole[112:P - 1, :]), (P - 1, P, tail)]


def sort_edges(c, bins, flags):
    nc, sp, act, dve, pool, pe = c.nc, c.sp, c.act, c.dve, c.pool, c.pe
    with ExitStack() as st:
        def sb(name, shape, dt=F32):
            return st.enter_context(nc.sbuf_tensor(name, shape, dt))

        rec = sb("rec", [P, ECOLS, REC])
        fill = sb("fill", [P, NG * TG, REC])
        EC = 98
        stage = sb("stage", [P, 2, EC * DE])
        srci, dsti, typi = (sb(n, [P, ECOLS], I32) for n in ("srci", "dsti", "typi"))
        srcf, blk, rank, pos, ones_e = (sb(n, [P, ECOLS]) for n in ("srcf", "blk", "rank", "pos", "ones_e"))
        posi = sb("posi", [P, ECOLS], I32)
        mask = sb("mask", [P, NB, ECOLS], U8)
        cnt, gcnt, gend, gstart, off = (sb(n, [P, NB]) for n in ("cnt", "gcnt", "gend", "gstart", "off"))
        ones_b = sb("ones_b", [P, NB])
        ones_pp, below = sb("ones_pp", [P, P]), sb("below", [P, P])
        iota_g = sb("iota_g", [P, NG])
        rounded = sb("rounded", [P, NB])
        tot = st.enter_context(nc.psum_tensor("tot", [P, NB], F32))
        pre = st.enter_context(nc.psum_tensor("pre", [P, NB], F32))
        s_int = [c.slot(f"s_int{i}") for i in range(3)]
        s_stage = [[c.slot(f"s_stage{i}_{k}") for k in range(3)] for i in range(2)]
        s_fill, s_scatter = c.slot("s_fill"), c.slot("s_scatter")

        t_f = c.POOL.mark(pool.memset(fill[:, :, :], 0.0))
        need(pool, t_f)
        c.POOL.mark(pool.memset(fill[:, :, R_SRC:R_SRC + 1], NO_SRC))
        t_f = c.POOL.mark(pool.memset(fill[:, :, R_TYPE:R_TYPE + 1], NO_TYPE))
        need(sp, t_f)
        t_fill = s_fill.mark(sp.dma_start(bins.rearrange("(p s) r -> p s r", p=P), fill[:, :, :]))

        t_ints = []
        for tile, name, pad in ((srci, "src", NP + 3), (dsti, "dst", 0), (typi, "edge_type_9", 0)):
            t_pad = c.DVE.mark(dve.memset(tile[:, ETAIL:ECOLS], pad))
            need(act, t_pad)
            s = s_int[len(t_ints)]
            for a, b, piece in edge_rows(c.io[name]):
                t = s.mark(act.dma_start(tile[a:b, 0:piece.shape[1]], piece))
            t_ints.append(t)

        t_one = c.DVE.mark(dve.memset(ones_e[:, :], 1.0))
        t_one = c.DVE.mark(dve.memset(ones_b[:, :], 1.0))
        t_pp = c.DVE.mark(dve.memset(ones_pp[:, :], 1.0))
        t_io = c.POOL.mark(pool.iota(iota_g[:, :], [[1, NG]], base=0, channel_multiplier=0,
                                     allow_small_or_imprecise_dtypes=True))
        need(pool, t_pp)
        t_below = c.POOL.mark(pool.affine_select(out=below[:, :], in_=ones_pp[:, :], compare_op=ALU.is_gt, fill=0.0,
                                                 base=0, pattern=[[1, P]], channel_multiplier=-1))

        need(dve, t_ints[0])
        t = c.DVE.mark(dve.tensor_copy(srcf[:, :], srci[:, :]))
        need(dve, t)
        t = c.DVE.mark(dve.tensor_scalar(blk[:, :], srcf[:, :], -(W - 1) / 2, 1.0 / W, ALU.add, ALU.mult))
        need(dve, t)
        t = c.DVE.mark(dve.tensor_scalar(blk[:, :], blk[:, :], MAGIC, None, ALU.add))
        need(dve, t)
        t = c.DVE.mark(dve.tensor_scalar(blk[:, :], blk[:, :], -MAGIC, float(NB - 1), ALU.add, ALU.min))
        need(dve, t)
        for b in range(NB):
            t_cnt = c.DVE.mark(dve.tensor_scalar(mask[:, b, :], blk[:, :], float(b), None, ALU.is_equal, ALU.add,
                                                 accum_out=cnt[:, b:b + 1]))
        need(pe, t_cnt, t_pp, t_below)
        t_tot = c.PE.mark(pe.matmul(tot[:, :], ones_pp[:, :], cnt[:, :], start=True, stop=True))
        t_pre = c.PE.mark(pe.matmul(pre[:, :], below[:, :], cnt[:, :], start=True, stop=True))
        need(dve, t_tot)
        t = c.DVE.mark(dve.tensor_scalar(rounded[:, :], tot[:, :], -(GE - 1) / 2, 1.0 / GE, ALU.add, ALU.mult))
        need(dve, t)
        t = c.DVE.mark(dve.tensor_scalar(rounded[:, :], rounded[:, :], MAGIC, None, ALU.add))
        need(dve, t)
        t = c.DVE.mark(dve.tensor_scalar(gcnt[:, :], rounded[:, :], -MAGIC, 1.0, ALU.add, ALU.add))
        need(dve, t, t_one)
        t = c.DVE.mark(dve.tensor_tensor_scan(gend[:, :], ones_b[:, :], gcnt[:, :], 0.0, ALU.mult, ALU.add))
        need(dve, t)
        t = c.DVE.mark(dve.tensor_tensor(gstart[:, :], gend[:, :], gcnt[:, :], ALU.subtract))
        need(dve, t, t_pre)
        t = c.DVE.mark(dve.scalar_tensor_tensor(out=off[:, :], in0=gstart[:, :], scalar=float(GE), in1=pre[:, :],
                                                op0=ALU.mult, op1=ALU.add))
        need(dve, t)
        t = c.DVE.mark(dve.tensor_scalar(off[:, :], off[:, :], -1.0, None, ALU.add))
        need(dve, t)
        t_pos = None
        for b in range(NB):
            need(dve, t_pos)
            t = c.DVE.mark(dve.tensor_tensor_scan(rank[:, :], ones_e[:, :], mask[:, b, :], off[:, b:b + 1],
                                                  ALU.mult, ALU.add))
            need(dve, t)
            t_pos = c.DVE.mark(dve.copy_predicated(pos[:, :], mask[:, b, :], rank[:, :]))
        need(dve, t_pos)
        t_pos = c.DVE.mark(dve.tensor_copy(posi[:, :], pos[:, :]))

        need(dve, t_ints[1], t_ints[2], t_pos)
        t = c.DVE.mark(dve.scalar_tensor_tensor(out=rec[:, :, R_SRC], in0=blk[:, :], scalar=-float(W), in1=srcf[:, :],
                                                op0=ALU.mult, op1=ALU.add))
        t = c.DVE.mark(dve.tensor_copy(rec[:, :, R_DSTI].bitcast(I32), dsti[:, :]))
        t = c.DVE.mark(dve.tensor_scalar(rec[:, :, R_DSTC], dsti[:, :], -float(CENTER), None, ALU.add))
        t = c.DVE.mark(dve.tensor_scalar(pos[:, :], srcf[:, :], float(NP), NO_TYPE, ALU.is_ge, ALU.mult))
        t = c.DVE.mark(dve.tensor_scalar(rank[:, :], typi[:, :], 0.0, float(NTYPE - 1), ALU.max, ALU.min))
        need(dve, t)
        t_rec = c.DVE.mark(dve.tensor_tensor(rec[:, :, R_TYPE], rank[:, :], pos[:, :], ALU.add))

        need(dve, t_io)
        blkg, same, last = flags["blk"], flags["same"], flags["last"]
        t = c.DVE.mark(dve.memset(blkg[:, :], 0.0))
        for b in range(NB - 1):
            need(dve, t)
            t = c.DVE.mark(dve.scalar_tensor_tensor(out=blkg[:, :], in0=iota_g[:, :], scalar=gend[:, b:b + 1],
                                                    in1=blkg[:, :], op0=ALU.is_ge, op1=ALU.add))
        t_m = c.DVE.mark(dve.memset(same[:, 0:1], 0.0))
        t_m = c.DVE.mark(dve.memset(last[:, NG - 1:NG], 1.0))
        need(dve, t)
        c.DVE.mark(dve.tensor_tensor(same[:, 1:NG], blkg[:, 1:NG], blkg[:, 0:NG - 1], ALU.is_equal))
        t = c.DVE.mark(dve.tensor_tensor(last[:, 0:NG - 1], blkg[:, 1:NG], blkg[:, 0:NG - 1], ALU.not_equal))
        need(dve, t)
        c.DVE.mark(dve.tensor_copy(flags["blki"][:, :], blkg[0:1, :]))
        flags["ready"] = c.DVE.mark(dve.tensor_copy(flags["lasti"][:, :], last[0:1, :]))

        npieces = -(-ECOLS // EC)
        t_stage_pad = []
        for k in range(2):
            t_stage_pad.append(c.POOL.mark(pool.memset(stage[:, k, :], 0.0)))
        t_copied = [None, None]
        t_ea = []
        ea = c.io["edge_attr_16"].rearrange("e k -> (e k)")
        for k in range(npieces):
            j0, j1 = k * EC, min(ECOLS, (k + 1) * EC)
            need(sp, t_stage_pad[k % 2], t_copied[k % 2])
            for i, (a, b, piece) in enumerate(edge_rows(ea, DE)):
                end = min(j1 * DE, piece.shape[1])
                if end > j0 * DE:
                    t = s_stage[k % 2][i].mark(sp.dma_start(stage[a:b, k % 2, 0:end - j0 * DE],
                                                            piece[:, j0 * DE:end]))
                    need(act, t)
            t_copied[k % 2] = c.ACT.mark(act.activation(
                rec[:, j0:j1, 0:DE], stage[:, k % 2, 0:(j1 - j0) * DE].rearrange("p (j k) -> p j k", k=DE), ACT.Copy))
            t_ea.append(t_copied[k % 2])

        need(pool, t_fill, t_pos, t_rec)
        for j in range(ECOLS):
            if j % EC == 0:
                need(pool, t_ea[j // EC])
            t = s_scatter.mark(pool.indirect_dma_start(
                bins, bass.IndirectOffsetOnAxis(ap=posi[:, j:j + 1].bitcast(mybir.dt.uint32), axis=0),
                rec[:, j, :], None))
        return t


def build_counts(c, recs, flags, at, t_recs, lastslot):
    nc, sp, act, dve, pool, pe = c.nc, c.sp, c.act, c.dve, c.pool, c.pe
    NH = 4
    with ExitStack() as st:
        def sb(name, shape, dt=F32):
            return st.enter_context(nc.sbuf_tensor(name, shape, dt))

        iota_w = sb("iota_w", [P, W], F16)
        iota_t = sb("iota_t", [P, NTYPE], F16)
        iota_n = sb("iota_n", [P, NP], F16)
        order = sb("order", [P, TG, P])
        gbase = sb("gbase", [P, NG])
        ident = sb("ident_b", [P, P], BF16)
        src1 = sb("src1", [P, 2, TG, P], BF16)
        dst1 = sb("dst1", [P, NH, NP], BF16)
        acc = sb("acc", [P, 2, NP])
        lastg = sb("lastg", [P, NG])
        junk = sb("junk", [P, GE])
        lastrun = sb("lastrun", [P, NG])
        seen = sb("seen", [P, NG])
        ps = st.enter_context(nc.psum_tensor("ps_cnt", [P, NCH, 512], F32))
        psT = st.enter_context(nc.psum_tensor("psT", [P, 1024], BF16))
        s_at = [c.slot(f"s_at{i}") for i in range(2)]

        c.POOL.mark(pool.iota(iota_w[:, :], [[1, W]], base=0, channel_multiplier=0, allow_small_or_imprecise_dtypes=True))
        c.POOL.mark(pool.iota(iota_t[:, :], [[1, NTYPE]], base=0, channel_multiplier=0, allow_small_or_imprecise_dtypes=True))
        c.POOL.mark(pool.iota(iota_n[:, :], [[1, NP]], base=-CENTER, channel_multiplier=0, allow_small_or_imprecise_dtypes=True))
        c.POOL.mark(pool.iota(order[:, :, :], [[1, TG], [TG, P]], base=1, channel_multiplier=0, allow_small_or_imprecise_dtypes=True))
        c.POOL.mark(pool.iota(gbase[:, :], [[GE, NG]], base=0, channel_multiplier=0, allow_small_or_imprecise_dtypes=True))
        c.POOL.mark(pool.memset(src1[:, :, :, :], 0.0))
        t = c.POOL.mark(pool.memset(ident[:, :], 0.0))
        need(pool, t)
        t_cst = c.POOL.mark(pool.affine_select(out=ident[:, :], in_=ident[:, :], compare_op=ALU.not_equal, fill=1.0,
                                               base=0, pattern=[[-1, P]], channel_multiplier=1))
        need(pool, t_cst, t_recs)
        need(dve, t_cst, t_recs)
        need(pe, t_cst)
        need(sp, flags["ready"])

        t_src1, t_pe_group, t_order, t_at = [], [], [], [None, None]
        t_tile = []
        t_evac = [None] * NCH
        t_acc = None
        for g in range(NG):
            if g >= 2:
                need(pool, t_pe_group[g - 2])
            for t in range(TG):
                c.POOL.mark(pool.tensor_scalar(src1[:, g % 2, t, 0:W], iota_w[:, :], recs[:, g, t, R_SRC:R_SRC + 1], None, ALU.is_equal))
                tok = c.POOL.mark(pool.tensor_scalar(src1[:, g % 2, t, W:W + NTYPE], iota_t[:, :], recs[:, g, t, R_TYPE:R_TYPE + 1], None, ALU.is_equal))
            t_src1.append(tok)

            for t in range(TG):
                i = g * TG + t
                if i >= NH:
                    need(dve, t_tile[i - NH])
                tok = c.DVE.mark(dve.tensor_scalar(dst1[:, i % NH, :], iota_n[:, :], recs[:, g, t, R_DSTC:R_DSTC + 1], None, ALU.is_equal))
                if t == 0:
                    need(pe, t_src1[g])
                need(pe, tok)
                for ch in range(NCH):
                    if t == 0:
                        need(pe, t_evac[ch])
                    mm = pe.matmul(ps[:, ch, 0:CH], src1[:, g % 2, t, :], dst1[:, i % NH, ch * CH:(ch + 1) * CH],
                                   start=(t == 0), stop=(t == TG - 1))
                t_tile.append(c.PE.mark(mm))
            need(pe, t_order[g - 1] if g else None)
            for t in range(TG):
                tr = pe.transpose(psT[:, t * P:(t + 1) * P], src1[:, g % 2, t, :], ident[:, :])
            t_pe_group.append(c.PE.mark(tr))

            need(dve, t_tile[-1], t_acc, t_at[g % 2])
            for ch in range(NCH):
                cols = slice(ch * CH, (ch + 1) * CH)
                if g == 0:
                    ins = dve.tensor_copy(acc[:, 0, cols], ps[:, ch, 0:CH])
                else:
                    ins = dve.scalar_tensor_tensor(out=acc[:, g % 2, cols], in0=acc[:, (g - 1) % 2, cols],
                                                   scalar=flags["same"][:, g:g + 1], in1=ps[:, ch, 0:CH],
                                                   op0=ALU.mult, op1=ALU.add)
                t_evac[ch] = c.DVE.mark(ins)
            t_acc = t_evac[NCH - 1]
            need(dve, t_pe_group[g])
            t_order.append(c.DVE.mark(dve.tensor_tensor_reduce(
                junk[:, :], psT[:, 0:GE], order[:, :, :].rearrange("p t k -> p (t k)"), 1.0, 0.0, ALU.mult, ALU.max, lastg[:, g:g + 1])))
            b = sp.value_load(flags["blki"][0:1, g:g + 1], min_val=0, max_val=NB - 1)
            is_last = sp.value_load(flags["lasti"][0:1, g:g + 1], min_val=0, max_val=1)
            need(sp, t_acc)
            t_at[g % 2] = s_at[g % 2].mark(sp.dma_start(at[bass.ds(b * P, P), :], acc[:, g % 2, :], cond=is_last))

        need(dve, t_order[-1])
        t = c.DVE.mark(dve.tensor_scalar(seen[:, :], lastg[:, :], 0.0, None, ALU.is_gt))
        need(dve, t)
        t = c.DVE.mark(dve.tensor_tensor(seen[:, :], seen[:, :], gbase[:, :], ALU.mult))
        need(dve, t)
        t = c.DVE.mark(dve.tensor_tensor(lastg[:, :], lastg[:, :], seen[:, :], ALU.add))
        need(dve, t)
        t_run = c.DVE.mark(dve.tensor_tensor_scan(lastrun[:, :], flags["same"][:, :], lastg[:, :], 0.0, ALU.mult, ALU.max))
        need(dve, t_run)
        t_sel = c.DVE.mark(dve.tensor_tensor(lastrun[:, :], lastrun[:, :], flags["last"][:, :], ALU.mult))
        need(dve, t_sel)
        for b in range(NB):
            t = c.DVE.mark(dve.tensor_scalar(seen[:, :], flags["blk"][:, :], float(b), None, ALU.is_equal))
            need(dve, t)
            t = c.DVE.mark(dve.tensor_tensor(junk[:, 0:NG], seen[:, :], lastrun[:, :], ALU.mult))
            need(dve, t)
            t = c.DVE.mark(dve.tensor_reduce(lastslot["f"][:, b:b + 1], junk[:, 0:NG], AX.X, ALU.max))
            need(dve, t)
        t = c.DVE.mark(dve.tensor_scalar(lastslot["f"][:, :], lastslot["f"][:, :], -1.0, 0.0, ALU.add, ALU.max))
        need(dve, t)
        lastslot["ready"] = c.DVE.mark(dve.tensor_copy(lastslot["i"][:, :], lastslot["f"][:, :]))
        need(dve, lastslot["ready"])
        return t_at


def layers(c, at, t_at, x3_out):
    nc, sp, act, dve, pool, pe, io = c.nc, c.sp, c.act, c.dve, c.pool, c.pe, c.io
    NRING = 3
    with ExitStack() as st:
        def sb(name, shape, dt=F32):
            return st.enter_context(nc.sbuf_tensor(name, shape, dt))

        ps = st.enter_context(nc.psum_tensor("ps", [P, 8, 512], F32))
        ring = sb("ring", [P, NRING, NP])
        resT, degT, zT, hT = (sb(n, [P, NP]) for n in ("resT", "degT", "zT", "hT"))
        dinvT = x3_out
        wideT = sb("wideT", [P, 2, NP])
        xn = sb("xn", [P, NB, 2 * D])
        tmp = sb("tmp", [P, 2, 6, CH])
        dinvn = sb("dinvn", [P, NB])
        ident, ones, mean_w = sb("ident", [P, P]), sb("ones", [P, P]), sb("mean_w", [P, P])
        eps = sb("eps", [P, 1])
        bias = sb("bias", [P, NBIAS])
        gbias = sb("gbias", [P, 3, 4])
        w0, w1, w2 = sb("w0", [P, 2 * D]), sb("w1", [P, 2, 2 * D]), sb("w2", [P, 2, D])
        l1_msg, l1_ih, l1_hh = sb("l1_msg", [P, 2, 2, 2 * D]), sb("l1_ih", [P, 2, 2, 3 * D]), sb("l1_hh", [P, 2, 3 * D])
        l2_msg, l2_ih, l2_hh = sb("l2_msg", [P, D]), sb("l2_ih", [P, 3 * D]), sb("l2_hh", [P, 3 * D])
        rowb = sb("rowb", [1, 5 * D])

        s_w, s_x, s_types, s_emb = c.slot("s_w"), c.slot("s_x"), c.slot("s_types"), c.slot("s_emb")
        s_ring = [c.slot(f"s_ring{i}") for i in range(NRING)]

        for out, in_ in ((w0[:, :], io["w0"]), (w1[:, :, :], io["w1"].rearrange("(k p) n -> p k n", p=P)),
                         (w2[:, :, :], io["w2"].rearrange("(k p) n -> p k n", p=P)),
                         (l1_hh[:, :, :], io["l1_hh"].rearrange("t p n -> p t n")),
                         (l2_msg[:, :], io["l2_msg"]), (l2_ih[:, :], io["l2_ih"]), (l2_hh[:, :], io["l2_hh"]),
                         (bias[:, :], io["bias"]), (rowb[:, :], io["rowb"])):
            s_w.mark(act.dma_start(out, in_))
        for t in range(2):
            s_w.mark(act.dma_start(l1_msg[:, t, :, :], io["l1_msg"][t, :, :].rearrange("(k p) n -> p k n", p=P)))
            t_w = s_w.mark(act.dma_start(l1_ih[:, t, :, :], io["l1_ih"][t, :, :].rearrange("(k p) n -> p k n", p=P)))

        xin = xn[:, :, 0:D]
        t0 = c.DVE.mark(dve.memset(xn[:, NB - 1, :], 0.0))
        t1 = c.DVE.mark(dve.memset(ones[:, :], 1.0))
        t2 = c.DVE.mark(dve.memset(mean_w[:, :], 1.0 / D))
        t2 = c.DVE.mark(dve.memset(eps[:, :], EPS_LN))
        t3 = c.POOL.mark(pool.memset(ident[:, :], 0.0))
        need(pool, t3)
        t_ident = c.POOL.mark(pool.affine_select(out=ident[:, :], in_=ident[:, :], compare_op=ALU.not_equal, fill=1.0,
                                                 base=0, pattern=[[-1, P]], channel_multiplier=1))
        need(act, t0)
        s_x.mark(act.dma_start(xin[0:W, 0:NB - 1, :], io["x"][0:(NB - 1) * W, :].rearrange("(b p) f -> p b f", p=W)))
        t_x = s_x.mark(act.dma_start(xin[0:LASTROWS, NB - 1, :], io["x"][(NB - 1) * W:N, :]))

        HB = NB // 2
        need(sp, *t_at)
        for b in range(NB):
            r = (b % HB) * NTYPE
            t_ty = s_types.mark(sp.dma_start(ring[r:r + NTYPE, b // HB, :], at[b * P + W:b * P + W + NTYPE, :]))
        KT = HB * NTYPE

        bank_free = [None] * 8
        need(pe, t_ty, t1, t_ident, t_x, t_w)
        need(dve, t_w, t_x)
        need(act, t1, t2, t_w)

        def cols(ch):
            return slice(ch * CH, (ch + 1) * CH)

        def block_cols(b):
            return slice(b * W, (b + 1) * W)

        t_deg = []
        for ch in range(NCH):
            for h in range(2):
                mm = pe.matmul(ps[:, ch, 0:CH], ones[0:KT, :], ring[0:KT, h, cols(ch)], start=(h == 0), stop=(h == 1))
            t = c.PE.mark(mm)
            need(act, t)
            bank_free[ch] = c.ACT.mark(act.activation(degT[:, cols(ch)], ps[:, ch, 0:CH], ACT.Copy))
            t_deg.append(bank_free[ch])
        for b in range(NB):
            for h in range(2):
                mm = pe.matmul(ps[0:W, 7, b:b + 1], ring[0:KT, h, block_cols(b)], ones[0:KT, 0:1], start=(h == 0), stop=(h == 1))
        t_degn = c.PE.mark(mm)
        ring_free = [t_degn] * NRING

        def one_over_root(out, in_, *tokens):
            need(dve, *tokens)
            t = c.DVE.mark(dve.tensor_scalar(out, in_, 1.0, None, ALU.add))
            need(act, t)
            t = c.ACT.mark(act.activation(out, out, ACT.Sqrt))
            need(dve, t)
            return c.DVE.mark(dve.reciprocal(out, out))

        t_dinvn = bank_free[7] = one_over_root(dinvn[0:W, :], ps[0:W, 7, 0:NB], t_degn)
        t_dinv = [one_over_root(dinvT[:, cols(ch)], degT[:, cols(ch)], t_deg[ch]) for ch in range(NCH)]

        t_res = []
        for ch in range(NCH):
            need(pe, bank_free[ch])
            for b in range(ch * BPC, (ch + 1) * BPC):
                mm = pe.transpose(ps[:, ch, (b % BPC) * W:(b % BPC + 1) * W], xin[0:W, b, :], ident[0:W, 0:W])
            t = c.PE.mark(mm)
            need(act, t)
            bank_free[ch] = c.ACT.mark(act.activation(resT[:, cols(ch)], ps[:, ch, 0:CH], ACT.Copy))
            t_res.append(bank_free[ch])
        need(dve, t_res[-1], t_dinvn)
        t = c.DVE.mark(dve.tensor_tensor(xin[0:W, :, :], xin[0:W, :, :], dinvn[0:W, :].unsqueeze(2).to_broadcast([W, NB, D]), ALU.mult))
        t_xn = [t] * NB

        state = {"block": 0}

        def times_counts(f0, rows, t_xn, self_loops=False):
            for ch in range(NCH):
                need(pe, bank_free[ch])
            for b in range(NB):
                r = state["block"] % NRING
                state["block"] += 1
                need(sp, ring_free[r])
                t = s_ring[r].mark(sp.dma_start(ring[:, r, :], at[b * P:(b + 1) * P, :]))
                need(pe, t, t_xn[b])
                for ch in range(NCH):
                    mm = pe.matmul(ps[:, ch, 0:CH], xn[0:rows, b, f0:f0 + D], ring[0:rows, r, cols(ch)],
                                   start=(b == 0), stop=(b == NB - 1))
                ring_free[r] = c.PE.mark(mm)
                if b == NB - 2 and self_loops:
                    need(pe, t_xn[NB - 1])
                    for i in range(NB):
                        pe.matmul(ps[:, i // BPC, (i % BPC) * W:(i % BPC + 1) * W], xn[0:W, i, f0:f0 + D], ident[0:W, 0:W],
                                  start=False, stop=False, skip_group_check=True)
            return [ring_free[r]] * NCH

        bank_turn = {"n": 0}

        def next_bank():
            bank_turn["n"] = (bank_turn["n"] + 1) % 8
            need(pe, bank_free[bank_turn["n"]])
            return bank_turn["n"]

        def to_nodes(srcs, weights, width, t_src, evac, bias_row=None, rows_free=None):
            out = []
            for b in range(NB):
                k7 = next_bank()
                need(pe, *t_src[b // BPC])
                if bias_row is not None:
                    pe.matmul(ps[0:W, k7, 0:width], ones[0:1, 0:W], bias_row, start=True, stop=False)
                for k, (s, w) in enumerate(zip(srcs, weights)):
                    mm = pe.matmul(ps[0:W, k7, 0:width], s[:, block_cols(b)], w, start=(k == 0 and bias_row is None),
                                   stop=(k == len(srcs) - 1))
                t = c.PE.mark(mm)
                bank_free[k7] = evac(k7, b, t)
                out.append(bank_free[k7])
            return out

        def norm(y, out, t_y):
            res = []
            for ch in range(NCH):
                k7 = next_bank()
                need(pe, t_y[ch])
                t = c.PE.mark(pe.matmul(ps[:, k7, 0:CH], mean_w[:, :], y[:, cols(ch)], start=True, stop=True))
                need(dve, t)
                t_c = bank_free[k7] = c.DVE.mark(dve.tensor_tensor(y[:, cols(ch)], y[:, cols(ch)], ps[:, k7, 0:CH], ALU.subtract))
                sq = tmp[:, ch % 2, 0, :]
                need(act, t_c, t_tmp[ch % 2])
                t = c.ACT.mark(act.activation(sq, y[:, cols(ch)], ACT.Square))
                k7 = next_bank()
                need(pe, t)
                t = c.PE.mark(pe.matmul(ps[:, k7, 0:CH], mean_w[:, :], sq, start=True, stop=True))
                rstd = tmp[:, ch % 2, 1, :]
                need(act, t)
                t = bank_free[k7] = c.ACT.mark(act.activation(rstd, ps[:, k7, 0:CH], ACT.Sqrt, bias=eps[:, 0:1]))
                need(dve, t)
                t = c.DVE.mark(dve.reciprocal(rstd, rstd))
                need(dve, t)
                t_tmp[ch % 2] = c.DVE.mark(dve.tensor_tensor(out[:, cols(ch)], y[:, cols(ch)], rstd, ALU.mult))
                res.append(t_tmp[ch % 2])
            return res

        t_tmp = [None, None]

        t_ps = times_counts(0, W, t_xn, self_loops=True)
        t_z = []
        for ch in range(NCH):
            need(dve, t_ps[ch], t_dinv[ch])
            bank_free[ch] = c.DVE.mark(dve.tensor_tensor(zT[:, cols(ch)], ps[:, ch, 0:CH], dinvT[:, cols(ch)], ALU.mult))
            t_z.append(bank_free[ch])
        t_wide = []
        for ch in range(NCH):
            for half in range(2):
                k7 = next_bank()
                need(pe, t_z[ch])
                t = c.PE.mark(pe.matmul(ps[:, k7, 0:CH], w0[:, half * D:(half + 1) * D], zT[:, cols(ch)], start=True, stop=True))
                need(act, t)
                bank_free[k7] = c.ACT.mark(act.activation(wideT[:, half, cols(ch)], ps[:, k7, 0:CH], ACT.Relu,
                                                          bias=bias[:, B_L0_0 + half:B_L0_0 + half + 1]))
            t_wide.append((bank_free[k7],))

        def scaled(width):
            def evac(k7, b, t):
                need(dve, t)
                return c.DVE.mark(dve.tensor_scalar(xn[0:W, b, 0:width], ps[0:W, k7, 0:width], dinvn[0:W, b:b + 1], None, ALU.mult))
            return evac

        t_xn = to_nodes([wideT[:, 0, :], wideT[:, 1, :]], [w1[:, 0, :], w1[:, 1, :]], 2 * D, t_wide, scaled(2 * D))
        t_wide = [None] * NCH
        for half in range(2):
            t_ps = times_counts(half * D, W, t_xn, self_loops=True)
            for ch in range(NCH):
                need(dve, t_ps[ch])
                t = bank_free[ch] = c.DVE.mark(dve.tensor_tensor(wideT[:, half, cols(ch)], ps[:, ch, 0:CH], dinvT[:, cols(ch)], ALU.mult))
                need(act, t)
                t = c.ACT.mark(act.activation(wideT[:, half, cols(ch)], wideT[:, half, cols(ch)], ACT.Relu,
                                              bias=bias[:, B_L0_1 + half:B_L0_1 + half + 1]))
                t_wide[ch] = (t,)

        t_xn = to_nodes([wideT[:, 0, :], wideT[:, 1, :]], [w2[:, 0, :], w2[:, 1, :]], D, t_wide, scaled(D))
        t_ps = times_counts(0, W, t_xn, self_loops=True)
        t_y = []
        for ch in range(NCH):
            need(dve, t_ps[ch])
            t = bank_free[ch] = c.DVE.mark(dve.tensor_tensor(zT[:, cols(ch)], ps[:, ch, 0:CH], dinvT[:, cols(ch)], ALU.mult))
            need(dve, t)
            t_y.append(c.DVE.mark(dve.scalar_tensor_tensor(out=zT[:, cols(ch)], in0=zT[:, cols(ch)], scalar=bias[:, B_L0_2:B_L0_2 + 1],
                                                           in1=resT[:, cols(ch)], op0=ALU.add, op1=ALU.add)))
        t_res = norm(zT, resT, t_y)

        for k, b0 in enumerate((B_L1, B_L1 + 6, B_L2)):
            t = c.DVE.mark(dve.tensor_tensor(gbias[:, k, 0:2], bias[:, b0:b0 + 2], bias[:, b0 + 3:b0 + 5], ALU.add))
            need(dve, t)
            t = c.DVE.mark(dve.tensor_scalar(gbias[:, k, 2:3], gbias[:, k, 1:2], -1.0, None, ALU.mult))
        t_gb = t
        need(act, t_gb)

        def gru(k, b0, ins, w_ih, w_hh, h, out, t_in, masked):
            res = []
            for ch in range(NCH):
                p4 = 4 * (ch % 2)
                for q in range(4):
                    need(pe, bank_free[p4 + q])
                need(pe, *t_in[ch])
                for q, parts in enumerate(((1, 1), (1, 1), (1, 0), (0, 1))):
                    f = slice(min(q, 2) * D, (min(q, 2) + 1) * D)
                    ops = [(w[:, f], s[:, cols(ch)]) for w, s in zip(w_ih, ins)] * parts[0] + [(w_hh[:, f], h[:, cols(ch)])] * parts[1]
                    for i, (w, s) in enumerate(ops):
                        mm = pe.matmul(ps[:, p4 + q, 0:CH], w, s, start=(i == 0), stop=(i == len(ops) - 1))
                t = c.PE.mark(mm)
                r, omz, hn, n, d = (tmp[:, ch % 2, i, :] for i in range(5))
                need(act, t, t_tmp[ch % 2])
                t_r = bank_free[p4] = c.ACT.mark(act.activation(r, ps[:, p4, 0:CH], ACT.Sigmoid, bias=gbias[:, k, 0:1]))
                t_z = bank_free[p4 + 1] = c.ACT.mark(act.activation(omz, ps[:, p4 + 1, 0:CH], ACT.Sigmoid, bias=gbias[:, k, 2:3], scale=-1.0))
                need(dve, t_r)
                t = bank_free[p4 + 3] = c.DVE.mark(dve.scalar_tensor_tensor(
                    out=hn, in0=ps[:, p4 + 3, 0:CH], scalar=bias[:, b0 + 5:b0 + 6], in1=r, op0=ALU.add, op1=ALU.mult))
                need(dve, t)
                t = bank_free[p4 + 2] = c.DVE.mark(dve.tensor_tensor(hn, hn, ps[:, p4 + 2, 0:CH], ALU.add))
                need(act, t)
                t_n = c.ACT.mark(act.activation(n, hn, ACT.Tanh, bias=bias[:, b0 + 2:b0 + 3]))
                need(dve, t_z)
                if masked:
                    t = c.DVE.mark(dve.scalar_tensor_tensor(out=omz, in0=degT[:, cols(ch)], scalar=1.0, in1=omz, op0=ALU.min, op1=ALU.mult))
                    need(dve, t)
                need(dve, t_n)
                t = c.DVE.mark(dve.tensor_tensor(d, n, h[:, cols(ch)], ALU.subtract))
                need(dve, t)
                t = c.DVE.mark(dve.tensor_tensor(d, d, omz, ALU.mult))
                need(dve, t)
                t_tmp[ch % 2] = c.DVE.mark(dve.tensor_tensor(out[:, cols(ch)], h[:, cols(ch)], d, ALU.add))
                res.append(t_tmp[ch % 2])
            return res

        h, t_h = resT, t_res
        for step in range(2):
            for ch in range(NCH):
                k7 = next_bank()
                need(pe, t_h[ch])
                for b in range(ch * BPC, (ch + 1) * BPC):
                    mm = pe.transpose(ps[0:W, k7, (b % BPC) * P:(b % BPC + 1) * P], h[:, block_cols(b)], ident[:, :])
                t = c.PE.mark(mm)
                need(act, t)
                bank_free[k7] = c.ACT.mark(act.activation(xn[0:W, ch * BPC:(ch + 1) * BPC, 0:D],
                                                          ps[0:W, k7, :].rearrange("p (b f) -> p b f", f=D), ACT.Copy))
                for b in range(BPC):
                    t_xn[ch * BPC + b] = bank_free[k7]
            t_ps = times_counts(0, W, t_xn)
            t_z = []
            for ch in range(NCH):
                need(act, t_ps[ch])
                bank_free[ch] = c.ACT.mark(act.activation(zT[:, cols(ch)], ps[:, ch, 0:CH], ACT.Copy))
                t_z.append(bank_free[ch])
            t_agg = []
            for ch in range(NCH):
                dh = tmp[:, ch % 2, 5, :]
                need(dve, t_h[ch], t_agg[ch - 2][0] if ch >= 2 else None)
                t_dh = c.DVE.mark(dve.tensor_tensor(dh, h[:, cols(ch)], degT[:, cols(ch)], ALU.mult))
                for half in range(2):
                    f = slice(half * D, (half + 1) * D)
                    k7 = next_bank()
                    need(pe, t_z[ch])
                    pe.matmul(ps[:, k7, 0:CH], l1_msg[:, step, 0, f], zT[:, cols(ch)], start=True, stop=False)
                    need(pe, t_dh)
                    pe.matmul(ps[:, k7, 0:CH], l1_msg[:, step, 1, f], dh, start=False, stop=False)
                    mm = pe.matmul(ps[:, k7, 0:CH], rowb[0:1, step * 2 * D + half * D:step * 2 * D + (half + 1) * D],
                                   degT[0:1, cols(ch)], start=False, stop=True)
                    t = c.PE.mark(mm)
                    need(act, t)
                    bank_free[k7] = c.ACT.mark(act.activation(wideT[:, half, cols(ch)], ps[:, k7, 0:CH], ACT.Copy))
                t_agg.append((bank_free[k7],))
            t_h = gru(step, B_L1 + 6 * step, [wideT[:, 0, :], wideT[:, 1, :]],
                      [l1_ih[:, step, 0, :], l1_ih[:, step, 1, :]], l1_hh[:, step, :], h, hT, t_agg, True)
            h = hT
        t_y = []
        for ch in range(NCH):
            need(dve, t_h[ch])
            t_y.append(c.DVE.mark(dve.tensor_tensor(zT[:, cols(ch)], hT[:, cols(ch)], resT[:, cols(ch)], ALU.add)))
        t_res = norm(zT, resT, t_y)

        need(act, t_ps[0])
        for b in range(NB):
            t_emb = s_emb.mark(act.dma_start(xn[W:W + NTYPE, b, 0:D], io["emb"]))

        def plain(k7, b, t):
            need(dve, t)
            return c.DVE.mark(dve.tensor_copy(xn[0:W, b, 0:D], ps[0:W, k7, 0:D]))

        t_xn = to_nodes([resT], [l2_msg[:, :]], D, [(t,) for t in t_res], plain, bias_row=rowb[0:1, 4 * D:5 * D])
        need(pe, t_emb)
        t_ps = times_counts(0, W + NTYPE, t_xn)
        t_z = []
        for ch in range(NCH):
            need(act, t_ps[ch])
            bank_free[ch] = c.ACT.mark(act.activation(zT[:, cols(ch)], ps[:, ch, 0:CH], ACT.Copy))
            t_z.append((bank_free[ch],))
        t_h = gru(2, B_L2, [zT], [l2_ih[:, :]], l2_hh[:, :], resT, hT, t_z, False)
        t_y = []
        for ch in range(NCH):
            need(dve, t_h[ch])
            t_y.append(c.DVE.mark(dve.tensor_tensor(zT[:, cols(ch)], hT[:, cols(ch)], resT[:, cols(ch)], ALU.add)))
        t_x3 = norm(zT, x3_out, t_y)
        return t_x3


def attention(c, recs, t_recs, bins, flags, lastslot, x3T, t_x3, out):
    nc, sp, act, dve, pool, pe, io = c.nc, c.sp, c.act, c.dve, c.pool, c.pe, c.io
    kv_d = c.dram("kv_d", (NP, 2 * D), F32)
    q_d = c.dram("q_d", (NP, QW), F32)
    sums_d = c.dram("sums_d", (NP, MW), F32)
    with ExitStack() as st:
        def sb(name, shape, dt=F32, where=None):
            return (where or st).enter_context(nc.sbuf_tensor(name, shape, dt))

        xs, x3n = sb("xs", [P, NB, D]), sb("x3n", [P, NB, D])
        wb = sb("wb", [P, 3, D])
        ident = sb("ident4", [P, P])
        eps = sb("eps4", [P, 1])
        iota_w = sb("iota_w4", [P, W])
        s_w, s_out = c.slot("s_w4"), c.slot("s_out")
        s_kv, s_q = c.slot("s_kvd"), c.slot("s_qd")

        t_i = c.POOL.mark(pool.memset(ident[:, :], 0.0))
        need(pool, t_i)
        t_ident = c.POOL.mark(pool.affine_select(out=ident[:, :], in_=ident[:, :], compare_op=ALU.not_equal, fill=1.0,
                                                 base=0, pattern=[[-1, P]], channel_multiplier=1))
        t_iota = c.POOL.mark(pool.iota(iota_w[:, :], [[1, W]], base=0, channel_multiplier=0, allow_small_or_imprecise_dtypes=True))
        t_eps = c.DVE.mark(dve.memset(eps[:, :], EPS_LN))

        with ExitStack() as st2:
            qn, kvn = sb("qn", [P, NB, QW], where=st2), sb("kvn", [P, NB, 2 * D], where=st2)
            qT = sb("qT", [P, CH], where=st2)
            w4, b4, we4, bq = (sb("w4", [P, 4 * D], where=st2), sb("b4", [1, 4 * D], where=st2),
                               sb("we4", [P, HEADS * DE], where=st2), sb("bq", [P, 1], where=st2))
            ones1 = sb("ones1", [1, P], where=st2)
            lastrec = sb("lastrec", [P, NB, REC], where=st2)
            lastkv = kvn
            prod, prod_e = sb("prod0", [P, NB, D], where=st2), sb("prod_e0", [P, NB, HEADS * DE], where=st2)
            sc, sc_e = sb("sc0", [P, NB * HEADS], where=st2), sb("sc_e0", [P, NB * HEADS], where=st2)
            ps = st2.enter_context(nc.psum_tensor("ps4", [P, 8, 512], F32))
            s_rec, s_lkv = c.slot("s_lrec"), c.slot("s_lkv")

            t_one = c.DVE.mark(dve.memset(ones1[:, :], 1.0))
            t_we = c.DVE.mark(dve.memset(we4[:, :], 0.0))
            need(act, t_we)
            for a, b in ((w4[:, :], io["qkvs"]), (b4[:, :], io["qkvs_b"]), (bq[:, :], io["bq"]),
                         (wb[:, :, :], io["wbeta"].rearrange("(o k) f -> o k f", o=1).to_broadcast([P, 3, D]))):
                s_w.mark(act.dma_start(a, b))
            for h in range(HEADS):
                t_w = s_w.mark(act.dma_start(we4[h * HD:(h + 1) * HD, h * DE:(h + 1) * DE], io["weT"][h * HD:(h + 1) * HD, :]))
            need(pool, lastslot["ready"])
            for b in range(NB):
                t_lrec = s_rec.mark(pool.indirect_dma_start(
                    lastrec[0:W, b, :], None, bins,
                    bass.IndirectOffsetOnAxis(ap=lastslot["i"][0:W, b:b + 1].bitcast(mybir.dt.uint32), axis=0)))

            need(pe, *t_x3)
            need(pe, t_w, t_one, t_ident)
            need(dve, t_w)
            need(act, t_w)
            bank_free = [None] * 8
            t_kvn, t_qn = [], []
            scale = 1.0 / HD ** 0.5
            for b in range(NB):
                k7, cols = b % 4, slice(b * W, (b + 1) * W)
                need(pe, *(bank_free[k7] or ()))
                pe.matmul(ps[0:W, k7, :], ones1[0:1, 0:W], b4[:, :], start=True, stop=False)
                t = c.PE.mark(pe.matmul(ps[0:W, k7, :], x3T[:, cols], w4[:, :], start=False, stop=True))
                need(act, t)
                t_k = c.ACT.mark(act.activation(kvn[0:W, b, :], ps[0:W, k7, D:3 * D], ACT.Copy))
                need(dve, t_k)
                c.DVE.mark(dve.tensor_scalar(qn[0:W, b, 0:D], ps[0:W, k7, 0:D], scale, None, ALU.mult))
                t_s = c.DVE.mark(dve.tensor_copy(xs[0:W, b, :], ps[0:W, k7, 3 * D:4 * D]))
                bank_free[k7] = (t_k, t_s)
                k7 = 4 + b % 2
                need(pe, *(bank_free[k7] or ()))
                t = c.PE.mark(pe.transpose(ps[0:W, k7, 0:P], x3T[:, cols], ident[:, :]))
                need(act, t)
                bank_free[k7] = (c.ACT.mark(act.activation(x3n[0:W, b, :], ps[0:W, k7, 0:P], ACT.Copy)),)
            t_x3n = bank_free[k7][0]
            need(sp, t_k)
            t_kvd = s_kv.mark(sp.dma_start(kv_d.rearrange("(b p) f -> p b f", p=W), kvn[0:W, :, :]))
            t_qe = None
            for ch in range(NCH):
                need(pe, *(bank_free[6] or ()))
                t = c.PE.mark(pe.matmul(ps[:, 6, 0:CH], w4[:, 0:D], x3T[:, ch * CH:(ch + 1) * CH], start=True, stop=True))
                need(dve, t, t_qe)
                t_qT = c.DVE.mark(dve.tensor_scalar(qT[:, :], ps[:, 6, 0:CH], bq[:, 0:1], scale, ALU.add, ALU.mult))
                bank_free[6] = (t_qT,)
                need(pe, t_qT, *(bank_free[7] or ()))
                for i in range(BPC):
                    mm = pe.matmul(ps[0:W, 7, i * HEADS * DE:(i + 1) * HEADS * DE], qT[:, i * W:(i + 1) * W], we4[:, :], start=True, stop=True)
                t_qe = c.PE.mark(mm)
                need(act, t_qe)
                t_q = c.ACT.mark(act.activation(qn[0:W, ch * BPC:(ch + 1) * BPC, D:D + HEADS * DE],
                                                ps[0:W, 7, 0:BPC * HEADS * DE].rearrange("p (b f) -> p b f", b=BPC), ACT.Copy))
                bank_free[7] = (t_q,)
            need(pool, t_kvd, t_lrec)
            for b in range(NB):
                t_lkv = s_lkv.mark(pool.indirect_dma_start(
                    lastkv[0:W, b, :], None, kv_d,
                    bass.IndirectOffsetOnAxis(ap=lastrec[0:W, b, R_DSTI:R_DSTI + 1].bitcast(mybir.dt.uint32), axis=0)))
            need(dve, t_lkv, t_q, t_lrec, t_s)
            t = c.DVE.mark(dve.tensor_tensor(prod[0:W, :, :], qn[0:W, :, 0:D], lastkv[0:W, :, 0:D], ALU.mult))
            t2 = c.DVE.mark(dve.tensor_tensor(prod_e[0:W, :, :].rearrange("p b (h d) -> p b h d", h=HEADS),
                                              qn[0:W, :, D:D + HEADS * DE].rearrange("p b (h d) -> p b h d", h=HEADS),
                                              lastrec[0:W, :, 0:DE].unsqueeze(2).to_broadcast([W, NB, HEADS, DE]), ALU.mult))
            need(dve, t2)
            c.DVE.mark(dve.tensor_reduce(sc[0:W, :], prod[0:W, :, :].rearrange("p b (h c) -> p (b h) c", h=HEADS), AX.X, ALU.add, negate=True))
            t = c.DVE.mark(dve.tensor_reduce(sc_e[0:W, :], prod_e[0:W, :, :].rearrange("p b (h c) -> p (b h) c", h=HEADS), AX.X, ALU.add))
            need(dve, t)
            t = c.DVE.mark(dve.tensor_tensor(qn[0:W, :, D + HEADS * DE:QW], sc[0:W, :].rearrange("p (b h) -> p b h", h=HEADS),
                                             sc_e[0:W, :].rearrange("p (b h) -> p b h", h=HEADS), ALU.subtract))
            need(sp, t)
            t_qd = s_q.mark(sp.dma_start(q_d.rearrange("(b p) f -> p b f", p=W), qn[0:W, :, :]))
            need(sp, t_qd, t_x3n)
            nc.all_engine_barrier()

        NKV, NQ, NS = 3, 3, 3
        with ExitStack() as st2:
            kv = sb("kv", [P, NKV, TG, 2 * D], where=st2)
            qb = sb("qb", [P, NQ, QW], where=st2)
            src1 = sb("src14", [P, NS, TG, W], where=st2)
            srcT = sb("srcT", [P, 2, GE], where=st2)
            prod, prod_e = sb("prod", [P, TG, D], where=st2), sb("prod_e", [P, TG, HEADS * DE], where=st2)
            sc, sc_e = sb("sc", [P, TG, HEADS], where=st2), sb("sc_e", [P, TG, HEADS], where=st2)
            msg = sb("msg", [P, 2, TG, MW], where=st2)
            acc = sb("acc4", [P, 2, MW], where=st2)
            psT = st2.enter_context(nc.psum_tensor("psT4", [P, 1024], F32))
            psQ = st2.enter_context(nc.psum_tensor("psQ", [P, 3, 512], F32))
            psO = st2.enter_context(nc.psum_tensor("psO", [P, 2, 512], F32))
            qrows = psQ[:, :, :].rearrange("p k (two f) -> p (k two) f", two=2)
            s_g = [c.slot(f"s_gather{i}") for i in range(NKV)]
            s_qb = [c.slot(f"s_qb{i}") for i in range(NQ)]
            s_st = [c.slot(f"s_sums{i}") for i in range(2)]

            need(dve, t_iota, t_recs)
            need(pool, t_recs)
            t_src1, t_T, t_Q, t_kv, t_qb, t_msgs, t_sum, t_prod, t_srcT, t_ex, t_acc = ([NOT_YET] * NG for _ in range(11))
            t_st = [None, None]
            blks = {}

            def sources(g):
                need(dve, t_sum[g - NS] if g >= NS else None)
                t_src1[g] = c.DVE.mark(dve.tensor_tensor(src1[:, g % NS, :, :], iota_w[:, :].unsqueeze(1).to_broadcast([P, TG, W]),
                                                         recs[:, g, :, R_SRC:R_SRC + 1].to_broadcast([P, TG, W]), ALU.is_equal))

            def fetch(g):
                need(pool, t_msgs[g - NKV] if g >= NKV else None)
                for t in range(TG):
                    t_kv[g] = s_g[g % NKV].mark(pool.indirect_dma_start(
                        kv[:, g % NKV, t, :], None, kv_d,
                        bass.IndirectOffsetOnAxis(ap=recs[:, g, t, R_DSTI:R_DSTI + 1].bitcast(mybir.dt.uint32), axis=0)))
                b = sp.value_load(flags["blki"][0:1, g:g + 1], min_val=0, max_val=NB - 1)
                need(sp, t_Q[g - NQ] if g >= NQ else None)
                t_qb[g] = s_qb[g % NQ].mark(sp.dma_start(qb[0:W, g % NQ, :], q_d[bass.ds(b * W, W), :]))

            def spread(g):
                need(pe, t_src1[g], t_srcT[g - 1] if g else None)
                for t in range(TG):
                    mm = pe.transpose(psT[0:W, t * P:(t + 1) * P], src1[:, g % NS, t, :], ident[:, :])
                t_T[g] = c.PE.mark(mm)
                need(act, t_T[g], t_Q[g - 2] if g >= 2 else None)
                t_srcT[g] = c.ACT.mark(act.activation(srcT[0:W, g % 2, :], psT[0:W, 0:GE], ACT.Copy))
                need(pe, t_srcT[g], t_qb[g], t_prod[g - 1] if g else None)
                for t in range(TG):
                    mm = pe.matmul(psQ[:, t // 2, (t % 2) * 256:(t % 2) * 256 + QW], srcT[0:W, g % 2, t * P:(t + 1) * P], qb[0:W, g % NQ, :],
                                   start=True, stop=True)
                t_Q[g] = c.PE.mark(mm)

            def scores(g):
                k = g % NKV
                need(dve, t_Q[g], t_kv[g])
                t1 = c.DVE.mark(dve.tensor_tensor(prod[:, :, :], qrows[:, :, 0:D], kv[:, k, :, 0:D], ALU.mult))
                t2 = c.DVE.mark(dve.tensor_tensor(prod_e[:, :, :].rearrange("p t (h d) -> p t h d", h=HEADS),
                                                  qrows[:, :, D:D + HEADS * DE].rearrange("p t (h d) -> p t h d", h=HEADS),
                                                  recs[:, g, :, 0:DE].unsqueeze(2).to_broadcast([P, TG, HEADS, DE]), ALU.mult))
                need(dve, t1)
                t1 = c.DVE.mark(dve.tensor_reduce(sc[:, :, :], prod[:, :, :].rearrange("p t (h c) -> p t h c", h=HEADS), AX.X, ALU.add))
                need(dve, t2)
                t2 = c.DVE.mark(dve.tensor_reduce(sc_e[:, :, :], prod_e[:, :, :].rearrange("p t (h c) -> p t h c", h=HEADS), AX.X, ALU.add))
                need(dve, t1)
                t1 = t_prod[g] = c.DVE.mark(dve.tensor_tensor(sc[:, :, :], sc[:, :, :], qrows[:, :, D + HEADS * DE:QW], ALU.add))
                need(dve, t1, t2)
                t1 = c.DVE.mark(dve.tensor_tensor(sc[:, :, :], sc[:, :, :], sc_e[:, :, :], ALU.add))
                need(act, t1, t_sum[g - 2] if g >= 2 else None)
                t_ex[g] = c.ACT.mark(act.activation(msg[:, g % 2, :, D:MW], sc[:, :, :], ACT.Exp))

            def messages(g):
                k = g % NKV
                if g + 2 < NG:
                    sources(g + 2)
                need(dve, t_ex[g])
                t_msgs[g] = c.DVE.mark(dve.tensor_tensor(
                    msg[:, g % 2, :, 0:D].rearrange("p t (h c) -> p t h c", h=HEADS),
                    kv[:, k, :, D:2 * D].rearrange("p t (h c) -> p t h c", h=HEADS),
                    msg[:, g % 2, :, D:MW].unsqueeze(3).to_broadcast([P, TG, HEADS, HD]), ALU.mult))
                need(pe, t_msgs[g], t_acc[g - 2] if g >= 2 else None)
                for t in range(TG):
                    mm = pe.matmul(psO[0:W, g % 2, 0:MW], src1[:, g % NS, t, :], msg[:, g % 2, t, :], start=(t == 0), stop=(t == TG - 1))
                t_sum[g] = c.PE.mark(mm)

            def accumulate(g):
                need(dve, t_sum[g], t_acc[g - 1] if g else None, t_st[g % 2])
                if g == 0:
                    ins = dve.tensor_copy(acc[0:W, 0, :], psO[0:W, 0, 0:MW])
                else:
                    ins = dve.scalar_tensor_tensor(out=acc[0:W, g % 2, :], in0=acc[0:W, (g - 1) % 2, :], scalar=flags["same"][0:W, g:g + 1],
                                                   in1=psO[0:W, g % 2, 0:MW], op0=ALU.mult, op1=ALU.add)
                t_acc[g] = c.DVE.mark(ins)
                b = sp.value_load(flags["blki"][0:1, g:g + 1], min_val=0, max_val=NB - 1)
                is_last = sp.value_load(flags["lasti"][0:1, g:g + 1], min_val=0, max_val=1)
                need(sp, t_acc[g])
                t_st[g % 2] = s_st[g % 2].mark(sp.dma_start(sums_d[bass.ds(b * W, W), :], acc[0:W, g % 2, :], cond=is_last))

            sources(0)
            sources(1)
            for g in range(2):
                fetch(g)
            spread(0)
            for g in range(NG):
                if g + 2 < NG:
                    fetch(g + 2)
                scores(g)
                if g + 1 < NG:
                    spread(g + 1)
                messages(g)
                if g:
                    accumulate(g - 1)
            accumulate(NG - 1)
            need(sp, *t_st)
            nc.all_engine_barrier()

        sums = sb("sums", [P, NB, MW])
        o, y, t_a = sb("o", [P, NB, D]), sb("y", [P, NB, D]), sb("t_a", [P, NB, D])
        rden, la, lb = sb("rden", [P, NB, HEADS]), sb("la", [P, NB]), sb("lb", [P, NB])
        s_sums = c.slot("s_sums_in")
        t = s_sums.mark(sp.dma_start(sums[0:W, :, :], sums_d.rearrange("(b p) f -> p b f", p=W)))

        def bc(a):
            return a[0:W, :].unsqueeze(2).to_broadcast([W, NB, D])

        def vec(ins):
            t = c.DVE.mark(ins)
            need(dve, t)
            return t

        need(dve, t, t_eps)
        vec(dve.tensor_scalar(rden[0:W, :, :], sums[0:W, :, D:MW], 1e-16, None, ALU.add))
        vec(dve.reciprocal(rden[0:W, :, :], rden[0:W, :, :]))
        vec(dve.tensor_tensor(o[0:W, :, :].rearrange("p b (h c) -> p b h c", h=HEADS), sums[0:W, :, 0:D].rearrange("p b (h c) -> p b h c", h=HEADS),
                              rden[0:W, :, :].unsqueeze(3).to_broadcast([W, NB, HEADS, HD]), ALU.mult))
        vec(dve.tensor_tensor(wb[0:W, 0, :], wb[0:W, 0, :], wb[0:W, 2, :], ALU.add))
        vec(dve.tensor_tensor(wb[0:W, 1, :], wb[0:W, 1, :], wb[0:W, 2, :], ALU.subtract))
        vec(dve.tensor_tensor(t_a[0:W, :, :], o[0:W, :, :], wb[0:W, 0:1, :].to_broadcast([W, NB, D]), ALU.mult))
        vec(dve.tensor_tensor(y[0:W, :, :], xs[0:W, :, :], wb[0:W, 1:2, :].to_broadcast([W, NB, D]), ALU.mult))
        vec(dve.tensor_tensor(y[0:W, :, :], y[0:W, :, :], t_a[0:W, :, :], ALU.add))
        t = vec(dve.tensor_reduce(la[0:W, :], y[0:W, :, :], AX.X, ALU.add))
        need(act, t)
        t = c.ACT.mark(act.activation(lb[0:W, :], la[0:W, :], ACT.Sigmoid))
        vec(dve.tensor_tensor(t_a[0:W, :, :], xs[0:W, :, :], o[0:W, :, :], ALU.subtract))
        need(dve, t)
        vec(dve.tensor_tensor(t_a[0:W, :, :], t_a[0:W, :, :], bc(lb), ALU.mult))
        vec(dve.tensor_tensor(o[0:W, :, :], o[0:W, :, :], x3n[0:W, :, :], ALU.add))
        vec(dve.tensor_tensor(y[0:W, :, :], o[0:W, :, :], t_a[0:W, :, :], ALU.add))
        vec(dve.tensor_reduce(la[0:W, :], y[0:W, :, :], AX.X, ALU.add))
        vec(dve.tensor_scalar(la[0:W, :], la[0:W, :], 1.0 / D, None, ALU.mult))
        t = vec(dve.tensor_tensor(y[0:W, :, :], y[0:W, :, :], bc(la), ALU.subtract))
        vec(dve.tensor_tensor(t_a[0:W, :, :], y[0:W, :, :], y[0:W, :, :], ALU.mult))
        t = vec(dve.tensor_reduce(lb[0:W, :], t_a[0:W, :, :], AX.X, ALU.add))
        need(act, t, t_eps)
        t = c.ACT.mark(act.activation(lb[0:W, :], lb[0:W, :], ACT.Sqrt, bias=eps[0:W, 0:1], scale=1.0 / D))
        need(dve, t)
        vec(dve.reciprocal(lb[0:W, :], lb[0:W, :]))
        t = vec(dve.tensor_tensor(y[0:W, :, :], y[0:W, :, :], bc(lb), ALU.mult))
        need(sp, t)
        s_out.mark(sp.dma_start(out[0:(NB - 1) * W, :].rearrange("(b p) f -> p b f", p=W), y[0:W, 0:NB - 1, :]))
        t = s_out.mark(sp.dma_start(out[(NB - 1) * W:N, :], y[0:LASTROWS, NB - 1, :]))
        need(sp, t)
        nc.all_engine_barrier()


def build(nc, io, out):
    with ExitStack() as ctx:
        c = Ctx(nc, ctx, io)

        def sb(name, shape, dt=F32):
            return ctx.enter_context(nc.sbuf_tensor(name, shape, dt))

        bins = c.dram("bins", (NG * GE, REC), F32)
        at = c.dram("at", (NB * P, NP), F32)
        lastslot = {"f": sb("lastslot_f", [P, NB]), "i": sb("lastslot_i", [P, NB], I32)}
        flags = {k: sb("group_" + k, [P, NG]) for k in ("blk", "same", "last")}
        flags["blki"], flags["lasti"] = sb("group_blki", [1, NG], I32), sb("group_lasti", [1, NG], I32)
        s_recs = c.slot("s_recs")

        def load_records(recs):
            return s_recs.mark(c.sp.dma_start(recs[:, :, :, :].rearrange("p g t r -> p g (t r)"),
                                              bins.rearrange("(g p t) r -> p g (t r)", p=P, t=TG)))

        t_scattered = sort_edges(c, bins, flags)
        need(c.sp, t_scattered)
        nc.all_engine_barrier()
        with nc.sbuf_tensor("recs", [P, NG, TG, REC], F32) as recs:
            t_at = build_counts(c, recs, flags, at, load_records(recs), lastslot)
            need(c.sp, *t_at)
            nc.all_engine_barrier()
        x3T = sb("x3T", [P, NP])
        t_x3 = layers(c, at, t_at, x3T)
        nc.all_engine_barrier()
        with nc.sbuf_tensor("recs4", [P, NG, TG, REC], F32) as recs:
            attention(c, recs, load_records(recs), bins, flags, lastslot, x3T, t_x3, out)


def kernel(**inputs):
    import concourse.bacc as bacc
    from concourse.bass_utils import run_bass_kernel_spmd

    nc = bacc.Bacc("TRN2", target_bir_lowering=False, num_devices=1)
    arrays, io = {}, {}
    for name, a in laid_out(inputs).items():
        arrays["in_" + name] = a
        io[name] = nc.dram_tensor("in_" + name, a.shape, mybir.dt.from_np(a.dtype), kind="ExternalInput").ap()
    out = nc.dram_tensor("out", (N, D), F32, kind="ExternalOutput").ap()
    build(nc, io, out)
    return run_bass_kernel_spmd(nc, [arrays], core_ids=[0]).results[0]["out"]


def laid_out(inputs):
    a = {k: np.asarray(v) for k, v in inputs.items()}
    columns = []
    for name in ("L0_gnn_b0", "L0_gnn_b1", "L0_gnn_b2"):
        columns += list(a[name].reshape(-1, D))
    for t in range(2):
        columns += list(a["L1_gnn_b_ih"][t].reshape(3, D)) + list(a["L1_gnn_b_hh"][t].reshape(3, D))
    columns += list(a["L2_gnn_b_ih"].reshape(3, D)) + list(a["L2_gnn_b_hh"].reshape(3, D))
    out = {
        "src": a["src"], "dst": a["dst"], "edge_type_9": a["edge_type_9"], "edge_attr_16": a["edge_attr_16"],
        "x": a["x"], "w0": a["L0_gnn_W0"], "w1": a["L0_gnn_W1"], "w2": a["L0_gnn_W2"],
        "l1_msg": a["L1_gnn_W_msg"].transpose(0, 2, 1), "l1_ih": a["L1_gnn_W_ih"].transpose(0, 2, 1),
        "l1_hh": a["L1_gnn_W_hh"].transpose(0, 2, 1),
        "l2_msg": a["L2_gnn_W_msg"].T, "l2_ih": a["L2_gnn_W_ih"].T, "l2_hh": a["L2_gnn_W_hh"].T,
        "emb": a["L2_gnn_edge_embed"],
        "bias": np.stack(columns, axis=1),
        "rowb": np.concatenate([a["L1_gnn_b_msg"].reshape(-1), a["L2_gnn_b_msg"]]).reshape(1, -1),
        "qkvs": np.concatenate([a["L3_gnn_W" + k] for k in ("q", "k", "v", "skip")], axis=1),
        "qkvs_b": np.concatenate([a["L3_gnn_b" + k] for k in ("q", "k", "v", "skip")]).reshape(1, -1),
        "bq": a["L3_gnn_bq"].reshape(D, 1),
        "weT": a["L3_gnn_We"].T, "wbeta": a["L3_gnn_Wbeta"].reshape(3, D),
    }
    return {k: np.ascontiguousarray(v) for k, v in out.items()}
```

```python
from contextlib import ExitStack

import concourse.bass as bass
import concourse.mybir as mybir
import numpy as np

ALU = mybir.AluOpType
ACT = mybir.ActivationFunctionType
AX = mybir.AxisListType
F32, BF16, F16 = mybir.dt.float32, mybir.dt.bfloat16, mybir.dt.float16
I32, U8 = mybir.dt.int32, mybir.dt.uint8

P = 128
N, E, D = 3125, 100000, 128
NTYPE = 9
DE = 16
W = 112
NB = -(-N // W)
NP = NB * W
LASTROWS = N - (NB - 1) * W
BPC = 4
CH = BPC * W
NCH = NP // CH
ECOLS = -(-E // P)
ETAIL = E - (P - 1) * ECOLS
TG = 3
GE = TG * P
NG = P * ECOLS // GE + NB
REC = 20
R_SRC, R_DSTI, R_DSTC, R_TYPE = 16, 17, 18, 19
NO_SRC, NO_TYPE, NO_DST = float(W + 3), 100.0, 1e4
CENTER = NP // 2
MAGIC = 1.5 * 2.0 ** 23
HEADS, HD = 4, 32
QW = D + HEADS * DE + HEADS
MW = D + HEADS
EPS_LN = 1e-5

B_L0_0, B_L0_1, B_L0_2 = 0, 2, 4
B_L1 = 5
B_L2 = 17
NBIAS = 23


class Progress:

    def __init__(self, sem):
        self.sem, self.n = sem, 0

    def mark(self, ins):
        self.n += 1
        ins.then_inc(self.sem, 1)
        return (self.sem, self.n)


class Slot:

    def __init__(self, sem):
        self.sem, self.n = sem, 0

    def mark(self, ins):
        self.n += 16
        ins.then_inc(self.sem, 16)
        return (self.sem, self.n)


NOT_YET = "not issued yet"


def need(engine, *tokens):
    for t in tokens:
        if t is not None:
            assert t is not NOT_YET, "the producer comes later in the program"
            engine.wait_ge(t[0], t[1])


class Ctx:

    def __init__(self, nc, ctx, io):
        self.nc, self.ctx, self.io = nc, ctx, io
        self.pe, self.dve, self.act, self.pool, self.sp = nc.tensor, nc.vector, nc.scalar, nc.gpsimd, nc.sync
        self.PE, self.DVE, self.ACT, self.POOL = (
            Progress(ctx.enter_context(nc.semaphore(n))) for n in ("pe_done", "dve_done", "act_done", "pool_done"))

    def slot(self, name):
        return Slot(self.ctx.enter_context(self.nc.semaphore(name)))

    def dram(self, name, shape, dt):
        return self.nc.dram_tensor(name, shape, dt, kind="Internal").ap()


def edge_rows(ap, cols=1):
    whole = ap[0:(P - 1) * ECOLS * cols].rearrange("(p j) -> p j", j=ECOLS * cols)
    tail = ap[(P - 1) * ECOLS * cols:E * cols].rearrange("(p j) -> p j", p=1)
    return [(0, 112, whole[0:112, :]), (112, P - 1, whole[112:P - 1, :]), (P - 1, P, tail)]


def sort_edges(c, bins, flags):
    nc, sp, act, dve, pool, pe = c.nc, c.sp, c.act, c.dve, c.pool, c.pe
    with ExitStack() as st:
        def sb(name, shape, dt=F32):
            return st.enter_context(nc.sbuf_tensor(name, shape, dt))

        rec = sb("rec", [P, ECOLS, REC])
        fill = sb("fill", [P, NG * TG, REC])
        EC = 98
        stage = sb("stage", [P, 2, EC * DE])
        srci, dsti, typi = (sb(n, [P, ECOLS], I32) for n in ("srci", "dsti", "typi"))
        srcf, blk, rank, pos, ones_e = (sb(n, [P, ECOLS]) for n in ("srcf", "blk", "rank", "pos", "ones_e"))
        posi = sb("posi", [P, ECOLS], I32)
        mask = sb("mask", [P, NB, ECOLS], U8)
        cnt, gcnt, gend, gstart, off = (sb(n, [P, NB]) for n in ("cnt", "gcnt", "gend", "gstart", "off"))
        ones_b = sb("ones_b", [P, NB])
        ones_pp, below = sb("ones_pp", [P, P]), sb("below", [P, P])
        iota_g = sb("iota_g", [P, NG])
        rounded = sb("rounded", [P, NB])
        tot = st.enter_context(nc.psum_tensor("tot", [P, NB], F32))
        pre = st.enter_context(nc.psum_tensor("pre", [P, NB], F32))
        s_int = [c.slot(f"s_int{i}") for i in range(3)]
        s_stage = [[c.slot(f"s_stage{i}_{k}") for k in range(3)] for i in range(2)]
        s_fill, s_scatter = c.slot("s_fill"), c.slot("s_scatter")

        t_f = c.POOL.mark(pool.memset(fill[:, :, :], 0.0))
        need(pool, t_f)
        c.POOL.mark(pool.memset(fill[:, :, R_SRC:R_SRC + 1], NO_SRC))
        c.POOL.mark(pool.memset(fill[:, :, R_DSTC:R_DSTC + 1], NO_DST))
        t_f = c.POOL.mark(pool.memset(fill[:, :, R_TYPE:R_TYPE + 1], NO_TYPE))
        need(sp, t_f)
        t_fill = s_fill.mark(sp.dma_start(bins.rearrange("(p s) r -> p s r", p=P), fill[:, :, :]))

        t_ints = []
        for tile, name, pad in ((srci, "src", NP + 3), (dsti, "dst", 0), (typi, "edge_type_9", 0)):
            t_pad = c.DVE.mark(dve.memset(tile[:, ETAIL:ECOLS], pad))
            need(act, t_pad)
            s = s_int[len(t_ints)]
            for a, b, piece in edge_rows(c.io[name]):
                t = s.mark(act.dma_start(tile[a:b, 0:piece.shape[1]], piece))
            t_ints.append(t)

        t_one = c.DVE.mark(dve.memset(ones_e[:, :], 1.0))
        t_one = c.DVE.mark(dve.memset(ones_b[:, :], 1.0))
        t_pp = c.DVE.mark(dve.memset(ones_pp[:, :], 1.0))
        t_io = c.POOL.mark(pool.iota(iota_g[:, :], [[1, NG]], base=0, channel_multiplier=0,
                                     allow_small_or_imprecise_dtypes=True))
        need(pool, t_pp)
        t_below = c.POOL.mark(pool.affine_select(out=below[:, :], in_=ones_pp[:, :], compare_op=ALU.is_gt, fill=0.0,
                                                 base=0, pattern=[[1, P]], channel_multiplier=-1))

        need(dve, t_ints[0])
        t = c.DVE.mark(dve.tensor_copy(srcf[:, :], srci[:, :]))
        need(dve, t)
        t = c.DVE.mark(dve.tensor_scalar(blk[:, :], srcf[:, :], -(W - 1) / 2, 1.0 / W, ALU.add, ALU.mult))
        need(dve, t)
        t = c.DVE.mark(dve.tensor_scalar(blk[:, :], blk[:, :], MAGIC, None, ALU.add))
        need(dve, t)
        t = c.DVE.mark(dve.tensor_scalar(blk[:, :], blk[:, :], -MAGIC, float(NB - 1), ALU.add, ALU.min))
        need(dve, t)
        for b in range(NB):
            t_cnt = c.DVE.mark(dve.tensor_scalar(mask[:, b, :], blk[:, :], float(b), None, ALU.is_equal, ALU.add,
                                                 accum_out=cnt[:, b:b + 1]))
        need(pe, t_cnt, t_pp, t_below)
        t_tot = c.PE.mark(pe.matmul(tot[:, :], ones_pp[:, :], cnt[:, :], start=True, stop=True))
        t_pre = c.PE.mark(pe.matmul(pre[:, :], below[:, :], cnt[:, :], start=True, stop=True))
        need(dve, t_tot)
        t = c.DVE.mark(dve.tensor_scalar(rounded[:, :], tot[:, :], -(GE - 1) / 2, 1.0 / GE, ALU.add, ALU.mult))
        need(dve, t)
        t = c.DVE.mark(dve.tensor_scalar(rounded[:, :], rounded[:, :], MAGIC, None, ALU.add))
        need(dve, t)
        t = c.DVE.mark(dve.tensor_scalar(gcnt[:, :], rounded[:, :], -MAGIC, 1.0, ALU.add, ALU.add))
        need(dve, t, t_one)
        t = c.DVE.mark(dve.tensor_tensor_scan(gend[:, :], ones_b[:, :], gcnt[:, :], 0.0, ALU.mult, ALU.add))
        need(dve, t)
        t = c.DVE.mark(dve.tensor_tensor(gstart[:, :], gend[:, :], gcnt[:, :], ALU.subtract))
        need(dve, t, t_pre)
        t = c.DVE.mark(dve.scalar_tensor_tensor(out=off[:, :], in0=gstart[:, :], scalar=float(GE), in1=pre[:, :],
                                                op0=ALU.mult, op1=ALU.add))
        need(dve, t)
        t = c.DVE.mark(dve.tensor_scalar(off[:, :], off[:, :], -1.0, None, ALU.add))
        need(dve, t)
        t_pos = None
        for b in range(NB):
            need(dve, t_pos)
            t = c.DVE.mark(dve.tensor_tensor_scan(rank[:, :], ones_e[:, :], mask[:, b, :], off[:, b:b + 1],
                                                  ALU.mult, ALU.add))
            need(dve, t)
            t_pos = c.DVE.mark(dve.copy_predicated(pos[:, :], mask[:, b, :], rank[:, :]))
        need(dve, t_pos)
        t_pos = c.DVE.mark(dve.tensor_copy(posi[:, :], pos[:, :]))

        need(dve, t_ints[1], t_ints[2], t_pos)
        t = c.DVE.mark(dve.scalar_tensor_tensor(out=rec[:, :, R_SRC], in0=blk[:, :], scalar=-float(W), in1=srcf[:, :],
                                                op0=ALU.mult, op1=ALU.add))
        t = c.DVE.mark(dve.tensor_copy(rec[:, :, R_DSTI].bitcast(I32), dsti[:, :]))
        t = c.DVE.mark(dve.tensor_scalar(rec[:, :, R_DSTC], dsti[:, :], -float(CENTER), None, ALU.add))
        t = c.DVE.mark(dve.tensor_scalar(pos[:, :], srcf[:, :], float(NP), NO_TYPE, ALU.is_ge, ALU.mult))
        t = c.DVE.mark(dve.tensor_scalar(rank[:, :], typi[:, :], 0.0, float(NTYPE - 1), ALU.max, ALU.min))
        need(dve, t)
        t_rec = c.DVE.mark(dve.tensor_tensor(rec[:, :, R_TYPE], rank[:, :], pos[:, :], ALU.add))

        need(dve, t_io)
        blkg, same, last = flags["blk"], flags["same"], flags["last"]
        t = c.DVE.mark(dve.memset(blkg[:, :], 0.0))
        for b in range(NB - 1):
            need(dve, t)
            t = c.DVE.mark(dve.scalar_tensor_tensor(out=blkg[:, :], in0=iota_g[:, :], scalar=gend[:, b:b + 1],
                                                    in1=blkg[:, :], op0=ALU.is_ge, op1=ALU.add))
        t_m = c.DVE.mark(dve.memset(same[:, 0:1], 0.0))
        t_m = c.DVE.mark(dve.memset(last[:, NG - 1:NG], 1.0))
        need(dve, t)
        c.DVE.mark(dve.tensor_tensor(same[:, 1:NG], blkg[:, 1:NG], blkg[:, 0:NG - 1], ALU.is_equal))
        t = c.DVE.mark(dve.tensor_tensor(last[:, 0:NG - 1], blkg[:, 1:NG], blkg[:, 0:NG - 1], ALU.not_equal))
        need(dve, t)
        c.DVE.mark(dve.tensor_copy(flags["blki"][:, :], blkg[0:1, :]))
        flags["ready"] = c.DVE.mark(dve.tensor_copy(flags["lasti"][:, :], last[0:1, :]))

        npieces = -(-ECOLS // EC)
        t_stage_pad = []
        for k in range(2):
            t_stage_pad.append(c.POOL.mark(pool.memset(stage[:, k, :], 0.0)))
        t_copied = [None, None]
        t_ea = []
        ea = c.io["edge_attr_16"].rearrange("e k -> (e k)")
        for k in range(npieces):
            j0, j1 = k * EC, min(ECOLS, (k + 1) * EC)
            need(sp, t_stage_pad[k % 2], t_copied[k % 2])
            for i, (a, b, piece) in enumerate(edge_rows(ea, DE)):
                end = min(j1 * DE, piece.shape[1])
                if end > j0 * DE:
                    t = s_stage[k % 2][i].mark(sp.dma_start(stage[a:b, k % 2, 0:end - j0 * DE],
                                                            piece[:, j0 * DE:end]))
                    need(act, t)
            t_copied[k % 2] = c.ACT.mark(act.activation(
                rec[:, j0:j1, 0:DE], stage[:, k % 2, 0:(j1 - j0) * DE].rearrange("p (j k) -> p j k", k=DE), ACT.Copy))
            t_ea.append(t_copied[k % 2])

        need(pool, t_fill, t_pos, t_rec)
        for j in range(ECOLS):
            if j % EC == 0:
                need(pool, t_ea[j // EC])
            t = s_scatter.mark(pool.indirect_dma_start(
                bins, bass.IndirectOffsetOnAxis(ap=posi[:, j:j + 1].bitcast(mybir.dt.uint32), axis=0),
                rec[:, j, :], None))
        return t


SPANS = [(0, 2), (2, 4), (4, 6), (6, NCH)]
ALL_SPANS = (1 << len(SPANS)) - 1
FIRST = 1 << len(SPANS)


def build_counts(c, recs, flags, at, t_recs, lastslot):
    nc, sp, act, dve, pool, pe = c.nc, c.sp, c.act, c.dve, c.pool, c.pe
    ND, NS = 3, 3
    with ExitStack() as st:
        def sb(name, shape, dt=F32):
            return st.enter_context(nc.sbuf_tensor(name, shape, dt))

        iota_w, iota_t = sb("iota_w", [P, W]), sb("iota_t", [P, NTYPE])
        iota_n = sb("iota_n", [P, NP], F16)
        order = sb("order", [P, TG, P])
        gbase = sb("gbase", [P, NG])
        ident = sb("ident_b", [P, P], BF16)
        ones = sb("ones_s", [P, P])
        in_span, touched = sb("in_span", [P, NG, TG]), sb("touched", [P, NG])
        code, codei = sb("code", [1, NG]), sb("codei", [1, NG], I32)
        src1 = sb("src1", [P, NS, TG, P], BF16)
        dst1 = sb("dst1", [P, ND, TG, NP], BF16)
        acc = sb("acc", [P, NP])
        lastg = sb("lastg", [P, NG])
        zeros = sb("zeros", [P, CH], BF16)
        junk = sb("junk", [P, max(GE, NG)])
        lastrun = sb("lastrun", [P, NG])
        seen = sb("seen", [P, NG])
        marker = sb("marker", [1, NG + 1])
        ps = st.enter_context(nc.psum_tensor("ps_cnt", [P, NCH, 512], F32))
        psT = st.enter_context(nc.psum_tensor("psT", [P, 1024], BF16))
        touched_ps = ps[:, 0, 0:NG]
        s_at = c.slot("s_at")

        t_ones = c.DVE.mark(dve.memset(ones[:, :], 1.0))
        t_zero = c.DVE.mark(dve.memset(zeros[:, :], 0.0))
        t_mark = c.DVE.mark(dve.memset(marker[:, :], 0.0))
        t_code = c.DVE.mark(dve.memset(code[:, :], 0.0))
        c.POOL.mark(pool.iota(iota_w[:, :], [[1, W]], base=0, channel_multiplier=0, allow_small_or_imprecise_dtypes=True))
        c.POOL.mark(pool.iota(iota_t[:, :], [[1, NTYPE]], base=0, channel_multiplier=0, allow_small_or_imprecise_dtypes=True))
        c.POOL.mark(pool.iota(iota_n[:, :], [[1, NP]], base=-CENTER, channel_multiplier=0, allow_small_or_imprecise_dtypes=True))
        c.POOL.mark(pool.iota(order[:, :, :], [[1, TG], [TG, P]], base=1, channel_multiplier=0, allow_small_or_imprecise_dtypes=True))
        c.POOL.mark(pool.iota(gbase[:, :], [[GE, NG]], base=0, channel_multiplier=0, allow_small_or_imprecise_dtypes=True))
        c.POOL.mark(pool.memset(src1[:, :, :, :], 0.0))
        t = c.POOL.mark(pool.memset(ident[:, :], 0.0))
        need(pool, t)
        t_cst = c.POOL.mark(pool.affine_select(out=ident[:, :], in_=ident[:, :], compare_op=ALU.not_equal, fill=1.0,
                                               base=0, pattern=[[-1, P]], channel_multiplier=1))
        need(dve, t_cst, t_recs)
        need(pe, t_cst, t_ones)
        need(act, t_mark)
        need(sp, flags["ready"])

        targets = recs[:, :, :, R_DSTC]
        t_touched = None
        for s, (c0, c1) in enumerate(SPANS):
            need(dve, t_touched)
            t = c.DVE.mark(dve.tensor_scalar(in_span[:, :, :], targets, float(c0 * CH - CENTER), None, ALU.is_ge))
            need(dve, t)
            t = c.DVE.mark(dve.scalar_tensor_tensor(out=in_span[:, :, :], in0=targets, scalar=float(c1 * CH - CENTER),
                                                    in1=in_span[:, :, :], op0=ALU.is_lt, op1=ALU.mult))
            need(dve, t)
            t = c.DVE.mark(dve.tensor_reduce(touched[:, :], in_span[:, :, :], AX.X, ALU.max))
            need(pe, t)
            t = c.PE.mark(pe.matmul(touched_ps, ones[:, :], touched[:, :], start=True, stop=True))
            need(dve, t)
            t_touched = c.DVE.mark(dve.tensor_scalar(seen[:, :], touched_ps, 0.0, float(1 << s), ALU.is_gt, ALU.mult))
            need(dve, t_touched, t_code)
            t_code = c.DVE.mark(dve.tensor_tensor(code[:, :], code[:, :], seen[0:1, :], ALU.add))
        t = c.DVE.mark(dve.tensor_scalar(lastg[0:1, :], flags["same"][0:1, :], -float(FIRST), float(FIRST), ALU.mult, ALU.add))
        need(dve, t)
        t = c.DVE.mark(dve.tensor_tensor(code[:, :], code[:, :], lastg[0:1, :], ALU.add))
        need(dve, t)
        t_code = c.DVE.mark(dve.tensor_copy(codei[:, :], code[:, :]))
        need(pe, t_code, t_touched, t_zero)
        need(dve, t_code)

        t_hot, t_src, t_used, t_order, t_at, t_evac = ([NOT_YET] * NG for _ in range(6))

        def flag(engine, tile, g, top):
            return engine.value_load(tile[0:1, g:g + 1], min_val=0, max_val=top)

        def targets_one_hot(g, c0, c1):
            for t in range(TG):
                dve.tensor_scalar(dst1[:, g % ND, t, c0 * CH:c1 * CH], iota_n[:, c0 * CH:c1 * CH],
                                  recs[:, g, t, R_DSTC:R_DSTC + 1], None, ALU.is_equal)

        def add_products(g, c0, c1):
            for t in range(TG):
                for ch in range(c0, c1):
                    pe.matmul(ps[:, ch, 0:CH], src1[:, g % NS, t, :], dst1[:, g % ND, t, ch * CH:(ch + 1) * CH],
                              start=False, stop=True, skip_group_check=True)

        def one_hots(g):
            spans = codes["dve"]
            if g + 1 < NG:
                codes["dve"] = flag(dve, codei, g + 1, FIRST + ALL_SPANS)
            free = t_used[g - ND] if g >= ND else None
            for s, (c0, c1) in enumerate(SPANS):
                with dve.If((spans >> s) & 1):
                    need(dve, free)
                    targets_one_hot(g, c0, c1)
            need(dve, free)
            dve.tensor_tensor(src1[:, g % NS, :, 0:W], iota_w[:, :].unsqueeze(1).to_broadcast([P, TG, W]),
                              recs[:, g, :, R_SRC:R_SRC + 1].to_broadcast([P, TG, W]), ALU.is_equal)
            t_hot[g] = c.DVE.mark(dve.tensor_tensor(src1[:, g % NS, :, W:W + NTYPE], iota_t[:, :].unsqueeze(1).to_broadcast([P, TG, NTYPE]),
                                                    recs[:, g, :, R_TYPE:R_TYPE + 1].to_broadcast([P, TG, NTYPE]), ALU.is_equal))

        def products(g):
            spans = codes["pe"]
            if g + 1 < NG:
                codes["pe"] = flag(pe, codei, g + 1, FIRST + ALL_SPANS)
            with pe.If(spans >= FIRST):
                need(pe, t_evac[g - 1] if g else None)
                for ch in range(NCH):
                    pe.matmul(ps[:, ch, 0:CH], ident[:, :], zeros[:, :], start=True, stop=True, skip_group_check=True)
            for s, (c0, c1) in enumerate(SPANS):
                with pe.If((spans >> s) & 1):
                    need(pe, t_hot[g])
                    add_products(g, c0, c1)
            need(pe, t_hot[g], t_order[g - 1] if g else None)
            for t in range(TG):
                tr = pe.transpose(psT[:, t * P:(t + 1) * P], src1[:, g % NS, t, :], ident[:, :])
            t_used[g] = c.PE.mark(tr)

        def evacuate(g):
            is_last = codes["act"]
            if g + 1 < NG:
                codes["act"] = flag(act, flags["lasti"], g + 1, 1)
            need(act, t_used[g])
            with act.If(is_last):
                need(act, t_at[g - 1] if g else None)
                for ch in range(NCH):
                    act.activation(acc[:, ch * CH:(ch + 1) * CH], ps[:, ch, 0:CH], ACT.Copy)
            t_evac[g] = c.ACT.mark(act.activation(marker[:, g + 1:g + 2], marker[:, 0:1], ACT.Copy))
            b = flag(sp, flags["blki"], g, NB - 1)
            is_last = flag(sp, flags["lasti"], g, 1)
            need(sp, t_evac[g])
            t_at[g] = s_at.mark(sp.dma_start(at[bass.ds(b * P, P), :], acc[:, :], cond=is_last))

        def last_slots(g):
            need(dve, t_used[g])
            t_order[g] = c.DVE.mark(dve.tensor_tensor_reduce(
                junk[:, 0:GE], psT[:, 0:GE], order[:, :, :].rearrange("p t k -> p (t k)"), 1.0, 0.0, ALU.mult, ALU.max, lastg[:, g:g + 1]))

        codes = {"dve": flag(dve, codei, 0, FIRST + ALL_SPANS), "pe": flag(pe, codei, 0, FIRST + ALL_SPANS),
                 "act": flag(act, flags["lasti"], 0, 1)}
        one_hots(0)
        one_hots(1)
        for g in range(NG):
            if g:
                last_slots(g - 1)
            if g + 2 < NG:
                one_hots(g + 2)
            products(g)
            evacuate(g)
        last_slots(NG - 1)

        need(dve, t_order[-1])
        t = c.DVE.mark(dve.tensor_scalar(seen[:, :], lastg[:, :], 0.0, None, ALU.is_gt))
        need(dve, t)
        t = c.DVE.mark(dve.tensor_tensor(seen[:, :], seen[:, :], gbase[:, :], ALU.mult))
        need(dve, t)
        t = c.DVE.mark(dve.tensor_tensor(lastg[:, :], lastg[:, :], seen[:, :], ALU.add))
        need(dve, t)
        t_run = c.DVE.mark(dve.tensor_tensor_scan(lastrun[:, :], flags["same"][:, :], lastg[:, :], 0.0, ALU.mult, ALU.max))
        need(dve, t_run)
        t_sel = c.DVE.mark(dve.tensor_tensor(lastrun[:, :], lastrun[:, :], flags["last"][:, :], ALU.mult))
        need(dve, t_sel)
        for b in range(NB):
            t = c.DVE.mark(dve.scalar_tensor_tensor(out=junk[:, 0:NG], in0=flags["blk"][:, :], scalar=float(b), in1=lastrun[:, :],
                                                    op0=ALU.is_equal, op1=ALU.mult))
            need(dve, t)
            t = c.DVE.mark(dve.tensor_reduce(lastslot["f"][:, b:b + 1], junk[:, 0:NG], AX.X, ALU.max))
            need(dve, t)
        t = c.DVE.mark(dve.tensor_scalar(lastslot["f"][:, :], lastslot["f"][:, :], -1.0, 0.0, ALU.add, ALU.max))
        need(dve, t)
        lastslot["ready"] = c.DVE.mark(dve.tensor_copy(lastslot["i"][:, :], lastslot["f"][:, :]))
        need(dve, lastslot["ready"])
        return [t_at[-1]]


def layers(c, at, t_at, x3_out):
    nc, sp, act, dve, pool, pe, io = c.nc, c.sp, c.act, c.dve, c.pool, c.pe, c.io
    NRING = 3
    with ExitStack() as st:
        def sb(name, shape, dt=F32):
            return st.enter_context(nc.sbuf_tensor(name, shape, dt))

        ps = st.enter_context(nc.psum_tensor("ps", [P, 8, 512], F32))
        ring = sb("ring", [P, NRING, NP])
        resT, degT, zT, hT = (sb(n, [P, NP]) for n in ("resT", "degT", "zT", "hT"))
        dinvT = x3_out
        wideT = sb("wideT", [P, 2, NP])
        xn = sb("xn", [P, NB, 2 * D])
        tmp = sb("tmp", [P, 2, 6, CH])
        dinvn = sb("dinvn", [P, NB])
        ident, ones, mean_w = sb("ident", [P, P]), sb("ones", [P, P]), sb("mean_w", [P, P])
        eps = sb("eps", [P, 1])
        bias = sb("bias", [P, NBIAS])
        gbias = sb("gbias", [P, 3, 4])
        w0, w1, w2 = sb("w0", [P, 2 * D]), sb("w1", [P, 2, 2 * D]), sb("w2", [P, 2, D])
        l1_msg, l1_ih, l1_hh = sb("l1_msg", [P, 2, 2, 2 * D]), sb("l1_ih", [P, 2, 2, 3 * D]), sb("l1_hh", [P, 2, 3 * D])
        l2_msg, l2_ih, l2_hh = sb("l2_msg", [P, D]), sb("l2_ih", [P, 3 * D]), sb("l2_hh", [P, 3 * D])
        rowb = sb("rowb", [1, 5 * D])

        s_w, s_x, s_types, s_emb = c.slot("s_w"), c.slot("s_x"), c.slot("s_types"), c.slot("s_emb")
        s_ring = [c.slot(f"s_ring{i}") for i in range(NRING)]

        for out, in_ in ((w0[:, :], io["w0"]), (w1[:, :, :], io["w1"].rearrange("(k p) n -> p k n", p=P)),
                         (w2[:, :, :], io["w2"].rearrange("(k p) n -> p k n", p=P)),
                         (l1_hh[:, :, :], io["l1_hh"].rearrange("t p n -> p t n")),
                         (l2_msg[:, :], io["l2_msg"]), (l2_ih[:, :], io["l2_ih"]), (l2_hh[:, :], io["l2_hh"]),
                         (bias[:, :], io["bias"]), (rowb[:, :], io["rowb"])):
            s_w.mark(act.dma_start(out, in_))
        for t in range(2):
            s_w.mark(act.dma_start(l1_msg[:, t, :, :], io["l1_msg"][t, :, :].rearrange("(k p) n -> p k n", p=P)))
            t_w = s_w.mark(act.dma_start(l1_ih[:, t, :, :], io["l1_ih"][t, :, :].rearrange("(k p) n -> p k n", p=P)))

        xin = xn[:, :, 0:D]
        t0 = c.DVE.mark(dve.memset(xn[:, NB - 1, :], 0.0))
        t1 = c.DVE.mark(dve.memset(ones[:, :], 1.0))
        t2 = c.DVE.mark(dve.memset(mean_w[:, :], 1.0 / D))
        t2 = c.DVE.mark(dve.memset(eps[:, :], EPS_LN))
        t3 = c.POOL.mark(pool.memset(ident[:, :], 0.0))
        need(pool, t3)
        t_ident = c.POOL.mark(pool.affine_select(out=ident[:, :], in_=ident[:, :], compare_op=ALU.not_equal, fill=1.0,
                                                 base=0, pattern=[[-1, P]], channel_multiplier=1))
        need(act, t0)
        s_x.mark(act.dma_start(xin[0:W, 0:NB - 1, :], io["x"][0:(NB - 1) * W, :].rearrange("(b p) f -> p b f", p=W)))
        t_x = s_x.mark(act.dma_start(xin[0:LASTROWS, NB - 1, :], io["x"][(NB - 1) * W:N, :]))

        HB = NB // 2
        need(sp, *t_at)
        for b in range(NB):
            r = (b % HB) * NTYPE
            t_ty = s_types.mark(sp.dma_start(ring[r:r + NTYPE, b // HB, :], at[b * P + W:b * P + W + NTYPE, :]))
        KT = HB * NTYPE

        bank_free = [None] * 8
        need(pe, t_ty, t1, t_ident, t_x, t_w)
        need(dve, t_w, t_x)
        need(act, t1, t2, t_w)

        def cols(ch):
            return slice(ch * CH, (ch + 1) * CH)

        def block_cols(b):
            return slice(b * W, (b + 1) * W)

        t_deg = []
        for ch in range(NCH):
            for h in range(2):
                mm = pe.matmul(ps[:, ch, 0:CH], ones[0:KT, :], ring[0:KT, h, cols(ch)], start=(h == 0), stop=(h == 1))
            t = c.PE.mark(mm)
            need(act, t)
            bank_free[ch] = c.ACT.mark(act.activation(degT[:, cols(ch)], ps[:, ch, 0:CH], ACT.Copy))
            t_deg.append(bank_free[ch])
        for b in range(NB):
            for h in range(2):
                mm = pe.matmul(ps[0:W, 7, b:b + 1], ring[0:KT, h, block_cols(b)], ones[0:KT, 0:1], start=(h == 0), stop=(h == 1))
        t_degn = c.PE.mark(mm)
        ring_free = [t_degn] * NRING

        def one_over_root(out, in_, *tokens):
            need(dve, *tokens)
            t = c.DVE.mark(dve.tensor_scalar(out, in_, 1.0, None, ALU.add))
            need(act, t)
            t = c.ACT.mark(act.activation(out, out, ACT.Sqrt))
            need(dve, t)
            return c.DVE.mark(dve.reciprocal(out, out))

        t_dinvn = bank_free[7] = one_over_root(dinvn[0:W, :], ps[0:W, 7, 0:NB], t_degn)
        t_dinv = [one_over_root(dinvT[:, cols(ch)], degT[:, cols(ch)], t_deg[ch]) for ch in range(NCH)]

        t_res = []
        for ch in range(NCH):
            need(pe, bank_free[ch])
            for b in range(ch * BPC, (ch + 1) * BPC):
                mm = pe.transpose(ps[:, ch, (b % BPC) * W:(b % BPC + 1) * W], xin[0:W, b, :], ident[0:W, 0:W])
            t = c.PE.mark(mm)
            need(act, t)
            bank_free[ch] = c.ACT.mark(act.activation(resT[:, cols(ch)], ps[:, ch, 0:CH], ACT.Copy))
            t_res.append(bank_free[ch])
        need(dve, t_res[-1], t_dinvn)
        t = c.DVE.mark(dve.tensor_tensor(xin[0:W, :, :], xin[0:W, :, :], dinvn[0:W, :].unsqueeze(2).to_broadcast([W, NB, D]), ALU.mult))
        t_xn = [t] * NB

        state = {"block": 0}

        def times_counts(f0, rows, t_xn, self_loops=False):
            for ch in range(NCH):
                need(pe, bank_free[ch])
            for b in range(NB):
                r = state["block"] % NRING
                state["block"] += 1
                need(sp, ring_free[r])
                t = s_ring[r].mark(sp.dma_start(ring[:, r, :], at[b * P:(b + 1) * P, :]))
                need(pe, t, t_xn[b])
                for ch in range(NCH):
                    mm = pe.matmul(ps[:, ch, 0:CH], xn[0:rows, b, f0:f0 + D], ring[0:rows, r, cols(ch)],
                                   start=(b == 0), stop=(b == NB - 1))
                ring_free[r] = c.PE.mark(mm)
                if b == NB - 2 and self_loops:
                    need(pe, t_xn[NB - 1])
                    for i in range(NB):
                        pe.matmul(ps[:, i // BPC, (i % BPC) * W:(i % BPC + 1) * W], xn[0:W, i, f0:f0 + D], ident[0:W, 0:W],
                                  start=False, stop=False, skip_group_check=True)
            return [ring_free[r]] * NCH

        bank_turn = {"n": 0}

        def next_bank():
            bank_turn["n"] = (bank_turn["n"] + 1) % 8
            need(pe, bank_free[bank_turn["n"]])
            return bank_turn["n"]

        def to_nodes(srcs, weights, width, t_src, evac, bias_row=None, rows_free=None):
            out = []
            for b in range(NB):
                k7 = next_bank()
                need(pe, *t_src[b // BPC])
                if bias_row is not None:
                    pe.matmul(ps[0:W, k7, 0:width], ones[0:1, 0:W], bias_row, start=True, stop=False)
                for k, (s, w) in enumerate(zip(srcs, weights)):
                    mm = pe.matmul(ps[0:W, k7, 0:width], s[:, block_cols(b)], w, start=(k == 0 and bias_row is None),
                                   stop=(k == len(srcs) - 1))
                t = c.PE.mark(mm)
                bank_free[k7] = evac(k7, b, t)
                out.append(bank_free[k7])
            return out

        def norm(y, out, t_y):
            res = []
            for ch in range(NCH):
                k7 = next_bank()
                need(pe, t_y[ch])
                t = c.PE.mark(pe.matmul(ps[:, k7, 0:CH], mean_w[:, :], y[:, cols(ch)], start=True, stop=True))
                need(dve, t)
                t_c = bank_free[k7] = c.DVE.mark(dve.tensor_tensor(y[:, cols(ch)], y[:, cols(ch)], ps[:, k7, 0:CH], ALU.subtract))
                sq = tmp[:, ch % 2, 0, :]
                need(act, t_c, t_tmp[ch % 2])
                t = c.ACT.mark(act.activation(sq, y[:, cols(ch)], ACT.Square))
                k7 = next_bank()
                need(pe, t)
                t = c.PE.mark(pe.matmul(ps[:, k7, 0:CH], mean_w[:, :], sq, start=True, stop=True))
                rstd = tmp[:, ch % 2, 1, :]
                need(act, t)
                t = bank_free[k7] = c.ACT.mark(act.activation(rstd, ps[:, k7, 0:CH], ACT.Sqrt, bias=eps[:, 0:1]))
                need(dve, t)
                t = c.DVE.mark(dve.reciprocal(rstd, rstd))
                need(dve, t)
                t_tmp[ch % 2] = c.DVE.mark(dve.tensor_tensor(out[:, cols(ch)], y[:, cols(ch)], rstd, ALU.mult))
                res.append(t_tmp[ch % 2])
            return res

        t_tmp = [None, None]

        t_ps = times_counts(0, W, t_xn, self_loops=True)
        t_z = []
        for ch in range(NCH):
            need(dve, t_ps[ch], t_dinv[ch])
            bank_free[ch] = c.DVE.mark(dve.tensor_tensor(zT[:, cols(ch)], ps[:, ch, 0:CH], dinvT[:, cols(ch)], ALU.mult))
            t_z.append(bank_free[ch])
        t_wide = []
        for ch in range(NCH):
            for half in range(2):
                k7 = next_bank()
                need(pe, t_z[ch])
                t = c.PE.mark(pe.matmul(ps[:, k7, 0:CH], w0[:, half * D:(half + 1) * D], zT[:, cols(ch)], start=True, stop=True))
                need(act, t)
                bank_free[k7] = c.ACT.mark(act.activation(wideT[:, half, cols(ch)], ps[:, k7, 0:CH], ACT.Relu,
                                                          bias=bias[:, B_L0_0 + half:B_L0_0 + half + 1]))
            t_wide.append((bank_free[k7],))

        def scaled(width):
            def evac(k7, b, t):
                need(dve, t)
                return c.DVE.mark(dve.tensor_scalar(xn[0:W, b, 0:width], ps[0:W, k7, 0:width], dinvn[0:W, b:b + 1], None, ALU.mult))
            return evac

        t_xn = to_nodes([wideT[:, 0, :], wideT[:, 1, :]], [w1[:, 0, :], w1[:, 1, :]], 2 * D, t_wide, scaled(2 * D))
        t_wide = [None] * NCH
        for half in range(2):
            t_ps = times_counts(half * D, W, t_xn, self_loops=True)
            for ch in range(NCH):
                need(dve, t_ps[ch])
                t = bank_free[ch] = c.DVE.mark(dve.tensor_tensor(wideT[:, half, cols(ch)], ps[:, ch, 0:CH], dinvT[:, cols(ch)], ALU.mult))
                need(act, t)
                t = c.ACT.mark(act.activation(wideT[:, half, cols(ch)], wideT[:, half, cols(ch)], ACT.Relu,
                                              bias=bias[:, B_L0_1 + half:B_L0_1 + half + 1]))
                t_wide[ch] = (t,)

        t_xn = to_nodes([wideT[:, 0, :], wideT[:, 1, :]], [w2[:, 0, :], w2[:, 1, :]], D, t_wide, scaled(D))
        t_ps = times_counts(0, W, t_xn, self_loops=True)
        t_y = []
        for ch in range(NCH):
            need(dve, t_ps[ch])
            t = bank_free[ch] = c.DVE.mark(dve.tensor_tensor(zT[:, cols(ch)], ps[:, ch, 0:CH], dinvT[:, cols(ch)], ALU.mult))
            need(dve, t)
            t_y.append(c.DVE.mark(dve.scalar_tensor_tensor(out=zT[:, cols(ch)], in0=zT[:, cols(ch)], scalar=bias[:, B_L0_2:B_L0_2 + 1],
                                                           in1=resT[:, cols(ch)], op0=ALU.add, op1=ALU.add)))
        t_res = norm(zT, resT, t_y)

        for k, b0 in enumerate((B_L1, B_L1 + 6, B_L2)):
            t = c.DVE.mark(dve.tensor_tensor(gbias[:, k, 0:2], bias[:, b0:b0 + 2], bias[:, b0 + 3:b0 + 5], ALU.add))
            need(dve, t)
            t = c.DVE.mark(dve.tensor_scalar(gbias[:, k, 2:3], gbias[:, k, 1:2], -1.0, None, ALU.mult))
        t_gb = t
        need(act, t_gb)

        def gru(k, b0, ins, w_ih, w_hh, h, out, t_in, masked):
            res = []
            for ch in range(NCH):
                p4 = 4 * (ch % 2)
                for q in range(4):
                    need(pe, bank_free[p4 + q])
                need(pe, *t_in[ch])
                for q, parts in enumerate(((1, 1), (1, 1), (1, 0), (0, 1))):
                    f = slice(min(q, 2) * D, (min(q, 2) + 1) * D)
                    ops = [(w[:, f], s[:, cols(ch)]) for w, s in zip(w_ih, ins)] * parts[0] + [(w_hh[:, f], h[:, cols(ch)])] * parts[1]
                    for i, (w, s) in enumerate(ops):
                        mm = pe.matmul(ps[:, p4 + q, 0:CH], w, s, start=(i == 0), stop=(i == len(ops) - 1))
                t = c.PE.mark(mm)
                r, omz, hn, n, d = (tmp[:, ch % 2, i, :] for i in range(5))
                need(act, t, t_tmp[ch % 2])
                t_r = bank_free[p4] = c.ACT.mark(act.activation(r, ps[:, p4, 0:CH], ACT.Sigmoid, bias=gbias[:, k, 0:1]))
                t_z = bank_free[p4 + 1] = c.ACT.mark(act.activation(omz, ps[:, p4 + 1, 0:CH], ACT.Sigmoid, bias=gbias[:, k, 2:3], scale=-1.0))
                need(dve, t_r)
                t = bank_free[p4 + 3] = c.DVE.mark(dve.scalar_tensor_tensor(
                    out=hn, in0=ps[:, p4 + 3, 0:CH], scalar=bias[:, b0 + 5:b0 + 6], in1=r, op0=ALU.add, op1=ALU.mult))
                need(dve, t)
                t = bank_free[p4 + 2] = c.DVE.mark(dve.tensor_tensor(hn, hn, ps[:, p4 + 2, 0:CH], ALU.add))
                need(act, t)
                t_n = c.ACT.mark(act.activation(n, hn, ACT.Tanh, bias=bias[:, b0 + 2:b0 + 3]))
                need(dve, t_z)
                if masked:
                    t = c.DVE.mark(dve.scalar_tensor_tensor(out=omz, in0=degT[:, cols(ch)], scalar=1.0, in1=omz, op0=ALU.min, op1=ALU.mult))
                    need(dve, t)
                need(dve, t_n)
                t = c.DVE.mark(dve.tensor_tensor(d, n, h[:, cols(ch)], ALU.subtract))
                need(dve, t)
                t = c.DVE.mark(dve.tensor_tensor(d, d, omz, ALU.mult))
                need(dve, t)
                t_tmp[ch % 2] = c.DVE.mark(dve.tensor_tensor(out[:, cols(ch)], h[:, cols(ch)], d, ALU.add))
                res.append(t_tmp[ch % 2])
            return res

        h, t_h = resT, t_res
        for step in range(2):
            for ch in range(NCH):
                k7 = next_bank()
                need(pe, t_h[ch])
                for b in range(ch * BPC, (ch + 1) * BPC):
                    mm = pe.transpose(ps[0:W, k7, (b % BPC) * P:(b % BPC + 1) * P], h[:, block_cols(b)], ident[:, :])
                t = c.PE.mark(mm)
                need(act, t)
                bank_free[k7] = c.ACT.mark(act.activation(xn[0:W, ch * BPC:(ch + 1) * BPC, 0:D],
                                                          ps[0:W, k7, :].rearrange("p (b f) -> p b f", f=D), ACT.Copy))
                for b in range(BPC):
                    t_xn[ch * BPC + b] = bank_free[k7]
            t_ps = times_counts(0, W, t_xn)
            t_z = []
            for ch in range(NCH):
                need(act, t_ps[ch])
                bank_free[ch] = c.ACT.mark(act.activation(zT[:, cols(ch)], ps[:, ch, 0:CH], ACT.Copy))
                t_z.append(bank_free[ch])
            t_agg = []
            for ch in range(NCH):
                dh = tmp[:, ch % 2, 5, :]
                need(dve, t_h[ch], t_agg[ch - 2][0] if ch >= 2 else None)
                t_dh = c.DVE.mark(dve.tensor_tensor(dh, h[:, cols(ch)], degT[:, cols(ch)], ALU.mult))
                for half in range(2):
                    f = slice(half * D, (half + 1) * D)
                    k7 = next_bank()
                    need(pe, t_z[ch])
                    pe.matmul(ps[:, k7, 0:CH], l1_msg[:, step, 0, f], zT[:, cols(ch)], start=True, stop=False)
                    need(pe, t_dh)
                    pe.matmul(ps[:, k7, 0:CH], l1_msg[:, step, 1, f], dh, start=False, stop=False)
                    mm = pe.matmul(ps[:, k7, 0:CH], rowb[0:1, step * 2 * D + half * D:step * 2 * D + (half + 1) * D],
                                   degT[0:1, cols(ch)], start=False, stop=True)
                    t = c.PE.mark(mm)
                    need(act, t)
                    bank_free[k7] = c.ACT.mark(act.activation(wideT[:, half, cols(ch)], ps[:, k7, 0:CH], ACT.Copy))
                t_agg.append((bank_free[k7],))
            t_h = gru(step, B_L1 + 6 * step, [wideT[:, 0, :], wideT[:, 1, :]],
                      [l1_ih[:, step, 0, :], l1_ih[:, step, 1, :]], l1_hh[:, step, :], h, hT, t_agg, True)
            h = hT
        t_y = []
        for ch in range(NCH):
            need(dve, t_h[ch])
            t_y.append(c.DVE.mark(dve.tensor_tensor(zT[:, cols(ch)], hT[:, cols(ch)], resT[:, cols(ch)], ALU.add)))
        t_res = norm(zT, resT, t_y)

        need(act, t_ps[0])
        for b in range(NB):
            t_emb = s_emb.mark(act.dma_start(xn[W:W + NTYPE, b, 0:D], io["emb"]))

        def plain(k7, b, t):
            need(dve, t)
            return c.DVE.mark(dve.tensor_copy(xn[0:W, b, 0:D], ps[0:W, k7, 0:D]))

        t_xn = to_nodes([resT], [l2_msg[:, :]], D, [(t,) for t in t_res], plain, bias_row=rowb[0:1, 4 * D:5 * D])
        need(pe, t_emb)
        t_ps = times_counts(0, W + NTYPE, t_xn)
        t_z = []
        for ch in range(NCH):
            need(act, t_ps[ch])
            bank_free[ch] = c.ACT.mark(act.activation(zT[:, cols(ch)], ps[:, ch, 0:CH], ACT.Copy))
            t_z.append((bank_free[ch],))
        t_h = gru(2, B_L2, [zT], [l2_ih[:, :]], l2_hh[:, :], resT, hT, t_z, False)
        t_y = []
        for ch in range(NCH):
            need(dve, t_h[ch])
            t_y.append(c.DVE.mark(dve.tensor_tensor(zT[:, cols(ch)], hT[:, cols(ch)], resT[:, cols(ch)], ALU.add)))
        t_x3 = norm(zT, x3_out, t_y)
        return t_x3


def attention(c, recs, t_recs, bins, flags, lastslot, x3T, t_x3, out):
    nc, sp, act, dve, pool, pe, io = c.nc, c.sp, c.act, c.dve, c.pool, c.pe, c.io
    kv_d = c.dram("kv_d", (NP, 2 * D), F32)
    q_d = c.dram("q_d", (NP, QW), F32)
    sums_d = c.dram("sums_d", (NP, MW), F32)
    with ExitStack() as st:
        def sb(name, shape, dt=F32, where=None):
            return (where or st).enter_context(nc.sbuf_tensor(name, shape, dt))

        xs, x3n = sb("xs", [P, NB, D]), sb("x3n", [P, NB, D])
        wb = sb("wb", [P, 3, D])
        ident = sb("ident4", [P, P])
        eps = sb("eps4", [P, 1])
        iota_w = sb("iota_w4", [P, W])
        s_w, s_out = c.slot("s_w4"), c.slot("s_out")
        s_kv, s_q = c.slot("s_kvd"), c.slot("s_qd")

        t_i = c.POOL.mark(pool.memset(ident[:, :], 0.0))
        need(pool, t_i)
        t_ident = c.POOL.mark(pool.affine_select(out=ident[:, :], in_=ident[:, :], compare_op=ALU.not_equal, fill=1.0,
                                                 base=0, pattern=[[-1, P]], channel_multiplier=1))
        t_iota = c.POOL.mark(pool.iota(iota_w[:, :], [[1, W]], base=0, channel_multiplier=0, allow_small_or_imprecise_dtypes=True))
        t_eps = c.DVE.mark(dve.memset(eps[:, :], EPS_LN))

        with ExitStack() as st2:
            qn, kvn = sb("qn", [P, NB, QW], where=st2), sb("kvn", [P, NB, 2 * D], where=st2)
            qT = sb("qT", [P, CH], where=st2)
            w4, b4, we4, bq = (sb("w4", [P, 4 * D], where=st2), sb("b4", [1, 4 * D], where=st2),
                               sb("we4", [P, HEADS * DE], where=st2), sb("bq", [P, 1], where=st2))
            ones1 = sb("ones1", [1, P], where=st2)
            lastrec = sb("lastrec", [P, NB, REC], where=st2)
            lastkv = kvn
            prod, prod_e = sb("prod0", [P, NB, D], where=st2), sb("prod_e0", [P, NB, HEADS * DE], where=st2)
            sc, sc_e = sb("sc0", [P, NB * HEADS], where=st2), sb("sc_e0", [P, NB * HEADS], where=st2)
            ps = st2.enter_context(nc.psum_tensor("ps4", [P, 8, 512], F32))
            s_rec, s_lkv = c.slot("s_lrec"), c.slot("s_lkv")

            t_one = c.DVE.mark(dve.memset(ones1[:, :], 1.0))
            t_we = c.DVE.mark(dve.memset(we4[:, :], 0.0))
            need(act, t_we)
            for a, b in ((w4[:, :], io["qkvs"]), (b4[:, :], io["qkvs_b"]), (bq[:, :], io["bq"]),
                         (wb[:, :, :], io["wbeta"].rearrange("(o k) f -> o k f", o=1).to_broadcast([P, 3, D]))):
                s_w.mark(act.dma_start(a, b))
            for h in range(HEADS):
                t_w = s_w.mark(act.dma_start(we4[h * HD:(h + 1) * HD, h * DE:(h + 1) * DE], io["weT"][h * HD:(h + 1) * HD, :]))
            need(pool, lastslot["ready"])
            for b in range(NB):
                t_lrec = s_rec.mark(pool.indirect_dma_start(
                    lastrec[0:W, b, :], None, bins,
                    bass.IndirectOffsetOnAxis(ap=lastslot["i"][0:W, b:b + 1].bitcast(mybir.dt.uint32), axis=0)))

            need(pe, *t_x3)
            need(pe, t_w, t_one, t_ident)
            need(dve, t_w)
            need(act, t_w)
            bank_free = [None] * 8
            t_kvn, t_qn = [], []
            scale = 1.0 / HD ** 0.5
            for b in range(NB):
                k7, cols = b % 4, slice(b * W, (b + 1) * W)
                need(pe, *(bank_free[k7] or ()))
                pe.matmul(ps[0:W, k7, :], ones1[0:1, 0:W], b4[:, :], start=True, stop=False)
                t = c.PE.mark(pe.matmul(ps[0:W, k7, :], x3T[:, cols], w4[:, :], start=False, stop=True))
                need(act, t)
                t_k = c.ACT.mark(act.activation(kvn[0:W, b, :], ps[0:W, k7, D:3 * D], ACT.Copy))
                need(dve, t_k)
                c.DVE.mark(dve.tensor_scalar(qn[0:W, b, 0:D], ps[0:W, k7, 0:D], scale, None, ALU.mult))
                t_s = c.DVE.mark(dve.tensor_copy(xs[0:W, b, :], ps[0:W, k7, 3 * D:4 * D]))
                bank_free[k7] = (t_k, t_s)
                k7 = 4 + b % 2
                need(pe, *(bank_free[k7] or ()))
                t = c.PE.mark(pe.transpose(ps[0:W, k7, 0:P], x3T[:, cols], ident[:, :]))
                need(act, t)
                bank_free[k7] = (c.ACT.mark(act.activation(x3n[0:W, b, :], ps[0:W, k7, 0:P], ACT.Copy)),)
            t_x3n = bank_free[k7][0]
            need(sp, t_k)
            t_kvd = s_kv.mark(sp.dma_start(kv_d.rearrange("(b p) f -> p b f", p=W), kvn[0:W, :, :]))
            t_qe = None
            for ch in range(NCH):
                need(pe, *(bank_free[6] or ()))
                t = c.PE.mark(pe.matmul(ps[:, 6, 0:CH], w4[:, 0:D], x3T[:, ch * CH:(ch + 1) * CH], start=True, stop=True))
                need(dve, t, t_qe)
                t_qT = c.DVE.mark(dve.tensor_scalar(qT[:, :], ps[:, 6, 0:CH], bq[:, 0:1], scale, ALU.add, ALU.mult))
                bank_free[6] = (t_qT,)
                need(pe, t_qT, *(bank_free[7] or ()))
                for i in range(BPC):
                    mm = pe.matmul(ps[0:W, 7, i * HEADS * DE:(i + 1) * HEADS * DE], qT[:, i * W:(i + 1) * W], we4[:, :], start=True, stop=True)
                t_qe = c.PE.mark(mm)
                need(act, t_qe)
                t_q = c.ACT.mark(act.activation(qn[0:W, ch * BPC:(ch + 1) * BPC, D:D + HEADS * DE],
                                                ps[0:W, 7, 0:BPC * HEADS * DE].rearrange("p (b f) -> p b f", b=BPC), ACT.Copy))
                bank_free[7] = (t_q,)
            need(pool, t_kvd, t_lrec)
            for b in range(NB):
                t_lkv = s_lkv.mark(pool.indirect_dma_start(
                    lastkv[0:W, b, :], None, kv_d,
                    bass.IndirectOffsetOnAxis(ap=lastrec[0:W, b, R_DSTI:R_DSTI + 1].bitcast(mybir.dt.uint32), axis=0)))
            need(dve, t_lkv, t_q, t_lrec, t_s)
            t = c.DVE.mark(dve.tensor_tensor(prod[0:W, :, :], qn[0:W, :, 0:D], lastkv[0:W, :, 0:D], ALU.mult))
            t2 = c.DVE.mark(dve.tensor_tensor(prod_e[0:W, :, :].rearrange("p b (h d) -> p b h d", h=HEADS),
                                              qn[0:W, :, D:D + HEADS * DE].rearrange("p b (h d) -> p b h d", h=HEADS),
                                              lastrec[0:W, :, 0:DE].unsqueeze(2).to_broadcast([W, NB, HEADS, DE]), ALU.mult))
            need(dve, t2)
            c.DVE.mark(dve.tensor_reduce(sc[0:W, :], prod[0:W, :, :].rearrange("p b (h c) -> p (b h) c", h=HEADS), AX.X, ALU.add, negate=True))
            t = c.DVE.mark(dve.tensor_reduce(sc_e[0:W, :], prod_e[0:W, :, :].rearrange("p b (h c) -> p (b h) c", h=HEADS), AX.X, ALU.add))
            need(dve, t)
            t = c.DVE.mark(dve.tensor_tensor(qn[0:W, :, D + HEADS * DE:QW], sc[0:W, :].rearrange("p (b h) -> p b h", h=HEADS),
                                             sc_e[0:W, :].rearrange("p (b h) -> p b h", h=HEADS), ALU.subtract))
            need(sp, t)
            t_qd = s_q.mark(sp.dma_start(q_d.rearrange("(b p) f -> p b f", p=W), qn[0:W, :, :]))
            need(sp, t_qd, t_x3n)
            nc.all_engine_barrier()

        NKV, NQ, NS = 4, 3, 4
        with ExitStack() as st2:
            kv = sb("kv", [P, NKV, TG, 2 * D], where=st2)
            qb = sb("qb", [P, NQ, QW], where=st2)
            src1 = sb("src14", [P, NS, TG, W], where=st2)
            srcT = sb("srcT", [P, 3, GE], where=st2)
            prod, prod_e = sb("prod", [P, TG, D], where=st2), sb("prod_e", [P, TG, HEADS * DE], where=st2)
            sc, sc_e = sb("sc", [P, TG, HEADS], where=st2), sb("sc_e", [P, TG, HEADS], where=st2)
            msg = sb("msg", [P, 2, TG, MW], where=st2)
            acc = sb("acc4", [P, 2, MW], where=st2)
            psT = st2.enter_context(nc.psum_tensor("psT4", [P, 2, 512], F32))
            psQ = st2.enter_context(nc.psum_tensor("psQ", [P, 2, -(-TG // 2), 512], F32))
            psO = st2.enter_context(nc.psum_tensor("psO", [P, 2, 512], F32))
            qrows = psQ[:, :, :, :].rearrange("p i k (two f) -> p i (k two) f", two=2)[:, :, 0:TG, :]
            s_g = [c.slot(f"s_gather{i}") for i in range(NKV)]
            s_qb = [c.slot(f"s_qb{i}") for i in range(NQ)]
            s_st = [c.slot(f"s_sums{i}") for i in range(2)]

            need(dve, t_iota, t_recs)
            need(pool, t_recs)
            t_src1, t_T, t_Q, t_kv, t_qb, t_msgs, t_sum, t_prod, t_srcT, t_ex, t_acc = ([NOT_YET] * NG for _ in range(11))
            t_st = [None, None]
            blks = {}

            def sources(g):
                need(dve, t_sum[g - NS] if g >= NS else None)
                t_src1[g] = c.DVE.mark(dve.tensor_tensor(src1[:, g % NS, :, :], iota_w[:, :].unsqueeze(1).to_broadcast([P, TG, W]),
                                                         recs[:, g, :, R_SRC:R_SRC + 1].to_broadcast([P, TG, W]), ALU.is_equal))

            def fetch(g):
                need(pool, t_msgs[g - NKV] if g >= NKV else None)
                for t in range(TG):
                    t_kv[g] = s_g[g % NKV].mark(pool.indirect_dma_start(
                        kv[:, g % NKV, t, :], None, kv_d,
                        bass.IndirectOffsetOnAxis(ap=recs[:, g, t, R_DSTI:R_DSTI + 1].bitcast(mybir.dt.uint32), axis=0)))
                b = sp.value_load(flags["blki"][0:1, g:g + 1], min_val=0, max_val=NB - 1)
                need(sp, t_Q[g - NQ] if g >= NQ else None)
                t_qb[g] = s_qb[g % NQ].mark(sp.dma_start(qb[0:W, g % NQ, :], q_d[bass.ds(b * W, W), :]))

            def turn(g):
                need(pe, t_src1[g], t_srcT[g - 2] if g >= 2 else None)
                for t in range(TG):
                    mm = pe.transpose(psT[0:W, g % 2, t * P:(t + 1) * P], src1[:, g % NS, t, :], ident[:, :])
                t_T[g] = c.PE.mark(mm)
                need(act, t_T[g], t_Q[g - 3] if g >= 3 else None)
                t_srcT[g] = c.ACT.mark(act.activation(srcT[0:W, g % 3, :], psT[0:W, g % 2, 0:GE], ACT.Copy))

            def spread(g):
                need(pe, t_srcT[g], t_qb[g], t_prod[g - 2] if g >= 2 else None)
                for t in range(TG):
                    mm = pe.matmul(psQ[:, g % 2, t // 2, (t % 2) * 256:(t % 2) * 256 + QW], srcT[0:W, g % 3, t * P:(t + 1) * P],
                                   qb[0:W, g % NQ, :], start=True, stop=True)
                t_Q[g] = c.PE.mark(mm)

            def scores(g):
                k = g % NKV
                need(dve, t_Q[g], t_kv[g])
                t1 = c.DVE.mark(dve.tensor_tensor(prod[:, :, :], qrows[:, g % 2, :, 0:D], kv[:, k, :, 0:D], ALU.mult))
                t2 = c.DVE.mark(dve.tensor_tensor(prod_e[:, :, :].rearrange("p t (h d) -> p t h d", h=HEADS),
                                                  qrows[:, g % 2, :, D:D + HEADS * DE].rearrange("p t (h d) -> p t h d", h=HEADS),
                                                  recs[:, g, :, 0:DE].unsqueeze(2).to_broadcast([P, TG, HEADS, DE]), ALU.mult))
                need(dve, t1)
                t1 = c.DVE.mark(dve.tensor_reduce(sc[:, :, :], prod[:, :, :].rearrange("p t (h c) -> p t h c", h=HEADS), AX.X, ALU.add))
                need(dve, t2)
                t2 = c.DVE.mark(dve.tensor_reduce(sc_e[:, :, :], prod_e[:, :, :].rearrange("p t (h c) -> p t h c", h=HEADS), AX.X, ALU.add))
                need(dve, t1)
                t1 = t_prod[g] = c.DVE.mark(dve.tensor_tensor(sc[:, :, :], sc[:, :, :], qrows[:, g % 2, :, D + HEADS * DE:QW], ALU.add))
                need(dve, t1, t2)
                t1 = c.DVE.mark(dve.tensor_tensor(sc[:, :, :], sc[:, :, :], sc_e[:, :, :], ALU.add))
                need(act, t1, t_sum[g - 2] if g >= 2 else None)
                t_ex[g] = c.ACT.mark(act.activation(msg[:, g % 2, :, D:MW], sc[:, :, :], ACT.Exp))

            def messages(g):
                k = g % NKV
                if g + 3 < NG:
                    sources(g + 3)
                need(dve, t_ex[g])
                t_msgs[g] = c.DVE.mark(dve.tensor_tensor(
                    msg[:, g % 2, :, 0:D].rearrange("p t (h c) -> p t h c", h=HEADS),
                    kv[:, k, :, D:2 * D].rearrange("p t (h c) -> p t h c", h=HEADS),
                    msg[:, g % 2, :, D:MW].unsqueeze(3).to_broadcast([P, TG, HEADS, HD]), ALU.mult))
                need(pe, t_msgs[g], t_acc[g - 2] if g >= 2 else None)
                for t in range(TG):
                    mm = pe.matmul(psO[0:W, g % 2, 0:MW], src1[:, g % NS, t, :], msg[:, g % 2, t, :], start=(t == 0), stop=(t == TG - 1))
                t_sum[g] = c.PE.mark(mm)

            def accumulate(g):
                need(dve, t_sum[g], t_acc[g - 1] if g else None, t_st[g % 2])
                if g == 0:
                    ins = dve.tensor_copy(acc[0:W, 0, :], psO[0:W, 0, 0:MW])
                else:
                    ins = dve.scalar_tensor_tensor(out=acc[0:W, g % 2, :], in0=acc[0:W, (g - 1) % 2, :], scalar=flags["same"][0:W, g:g + 1],
                                                   in1=psO[0:W, g % 2, 0:MW], op0=ALU.mult, op1=ALU.add)
                t_acc[g] = c.DVE.mark(ins)
                b = sp.value_load(flags["blki"][0:1, g:g + 1], min_val=0, max_val=NB - 1)
                is_last = sp.value_load(flags["lasti"][0:1, g:g + 1], min_val=0, max_val=1)
                need(sp, t_acc[g])
                t_st[g % 2] = s_st[g % 2].mark(sp.dma_start(sums_d[bass.ds(b * W, W), :], acc[0:W, g % 2, :], cond=is_last))

            for g in range(3):
                sources(g)
                fetch(g)
            turn(0)
            turn(1)
            spread(0)
            for g in range(NG):
                if g + 3 < NG:
                    fetch(g + 3)
                if g + 2 < NG:
                    turn(g + 2)
                scores(g)
                if g + 1 < NG:
                    spread(g + 1)
                messages(g)
                if g:
                    accumulate(g - 1)
            accumulate(NG - 1)
            need(sp, *t_st)
            nc.all_engine_barrier()

        sums = sb("sums", [P, NB, MW])
        o, y, t_a = sb("o", [P, NB, D]), sb("y", [P, NB, D]), sb("t_a", [P, NB, D])
        rden, la, lb = sb("rden", [P, NB, HEADS]), sb("la", [P, NB]), sb("lb", [P, NB])
        s_sums = c.slot("s_sums_in")
        t = s_sums.mark(sp.dma_start(sums[0:W, :, :], sums_d.rearrange("(b p) f -> p b f", p=W)))

        def bc(a):
            return a[0:W, :].unsqueeze(2).to_broadcast([W, NB, D])

        def vec(ins):
            t = c.DVE.mark(ins)
            need(dve, t)
            return t

        need(dve, t, t_eps)
        vec(dve.tensor_scalar(rden[0:W, :, :], sums[0:W, :, D:MW], 1e-16, None, ALU.add))
        vec(dve.reciprocal(rden[0:W, :, :], rden[0:W, :, :]))
        vec(dve.tensor_tensor(o[0:W, :, :].rearrange("p b (h c) -> p b h c", h=HEADS), sums[0:W, :, 0:D].rearrange("p b (h c) -> p b h c", h=HEADS),
                              rden[0:W, :, :].unsqueeze(3).to_broadcast([W, NB, HEADS, HD]), ALU.mult))
        vec(dve.tensor_tensor(wb[0:W, 0, :], wb[0:W, 0, :], wb[0:W, 2, :], ALU.add))
        vec(dve.tensor_tensor(wb[0:W, 1, :], wb[0:W, 1, :], wb[0:W, 2, :], ALU.subtract))
        vec(dve.tensor_tensor(t_a[0:W, :, :], o[0:W, :, :], wb[0:W, 0:1, :].to_broadcast([W, NB, D]), ALU.mult))
        vec(dve.tensor_tensor(y[0:W, :, :], xs[0:W, :, :], wb[0:W, 1:2, :].to_broadcast([W, NB, D]), ALU.mult))
        vec(dve.tensor_tensor(y[0:W, :, :], y[0:W, :, :], t_a[0:W, :, :], ALU.add))
        t = vec(dve.tensor_reduce(la[0:W, :], y[0:W, :, :], AX.X, ALU.add))
        need(act, t)
        t = c.ACT.mark(act.activation(lb[0:W, :], la[0:W, :], ACT.Sigmoid))
        vec(dve.tensor_tensor(t_a[0:W, :, :], xs[0:W, :, :], o[0:W, :, :], ALU.subtract))
        need(dve, t)
        vec(dve.tensor_tensor(t_a[0:W, :, :], t_a[0:W, :, :], bc(lb), ALU.mult))
        vec(dve.tensor_tensor(o[0:W, :, :], o[0:W, :, :], x3n[0:W, :, :], ALU.add))
        vec(dve.tensor_tensor(y[0:W, :, :], o[0:W, :, :], t_a[0:W, :, :], ALU.add))
        vec(dve.tensor_reduce(la[0:W, :], y[0:W, :, :], AX.X, ALU.add))
        vec(dve.tensor_scalar(la[0:W, :], la[0:W, :], 1.0 / D, None, ALU.mult))
        t = vec(dve.tensor_tensor(y[0:W, :, :], y[0:W, :, :], bc(la), ALU.subtract))
        vec(dve.tensor_tensor(t_a[0:W, :, :], y[0:W, :, :], y[0:W, :, :], ALU.mult))
        t = vec(dve.tensor_reduce(lb[0:W, :], t_a[0:W, :, :], AX.X, ALU.add))
        need(act, t, t_eps)
        t = c.ACT.mark(act.activation(lb[0:W, :], lb[0:W, :], ACT.Sqrt, bias=eps[0:W, 0:1], scale=1.0 / D))
        need(dve, t)
        vec(dve.reciprocal(lb[0:W, :], lb[0:W, :]))
        t = vec(dve.tensor_tensor(y[0:W, :, :], y[0:W, :, :], bc(lb), ALU.mult))
        need(sp, t)
        s_out.mark(sp.dma_start(out[0:(NB - 1) * W, :].rearrange("(b p) f -> p b f", p=W), y[0:W, 0:NB - 1, :]))
        t = s_out.mark(sp.dma_start(out[(NB - 1) * W:N, :], y[0:LASTROWS, NB - 1, :]))
        need(sp, t)
        nc.all_engine_barrier()


def build(nc, io, out):
    with ExitStack() as ctx:
        c = Ctx(nc, ctx, io)

        def sb(name, shape, dt=F32):
            return ctx.enter_context(nc.sbuf_tensor(name, shape, dt))

        bins = c.dram("bins", (NG * GE, REC), F32)
        at = c.dram("at", (NB * P, NP), F32)
        lastslot = {"f": sb("lastslot_f", [P, NB]), "i": sb("lastslot_i", [P, NB], I32)}
        flags = {k: sb("group_" + k, [P, NG]) for k in ("blk", "same", "last")}
        flags["blki"], flags["lasti"] = sb("group_blki", [1, NG], I32), sb("group_lasti", [1, NG], I32)
        s_recs = c.slot("s_recs")

        def load_records(recs):
            return s_recs.mark(c.sp.dma_start(recs[:, :, :, :].rearrange("p g t r -> p g (t r)"),
                                              bins.rearrange("(g p t) r -> p g (t r)", p=P, t=TG)))

        t_scattered = sort_edges(c, bins, flags)
        need(c.sp, t_scattered)
        nc.all_engine_barrier()
        with nc.sbuf_tensor("recs", [P, NG, TG, REC], F32) as recs:
            t_at = build_counts(c, recs, flags, at, load_records(recs), lastslot)
            need(c.sp, *t_at)
            nc.all_engine_barrier()
        x3T = sb("x3T", [P, NP])
        t_x3 = layers(c, at, t_at, x3T)
        nc.all_engine_barrier()
        with nc.sbuf_tensor("recs4", [P, NG, TG, REC], F32) as recs:
            attention(c, recs, load_records(recs), bins, flags, lastslot, x3T, t_x3, out)


def kernel(**inputs):
    import concourse.bacc as bacc
    from concourse.bass_utils import run_bass_kernel_spmd

    nc = bacc.Bacc("TRN2", target_bir_lowering=False, num_devices=1)
    arrays, io = {}, {}
    for name, a in laid_out(inputs).items():
        arrays["in_" + name] = a
        io[name] = nc.dram_tensor("in_" + name, a.shape, mybir.dt.from_np(a.dtype), kind="ExternalInput").ap()
    out = nc.dram_tensor("out", (N, D), F32, kind="ExternalOutput").ap()
    build(nc, io, out)
    return run_bass_kernel_spmd(nc, [arrays], core_ids=[0]).results[0]["out"]


def laid_out(inputs):
    a = {k: np.asarray(v) for k, v in inputs.items()}
    columns = []
    for name in ("L0_gnn_b0", "L0_gnn_b1", "L0_gnn_b2"):
        columns += list(a[name].reshape(-1, D))
    for t in range(2):
        columns += list(a["L1_gnn_b_ih"][t].reshape(3, D)) + list(a["L1_gnn_b_hh"][t].reshape(3, D))
    columns += list(a["L2_gnn_b_ih"].reshape(3, D)) + list(a["L2_gnn_b_hh"].reshape(3, D))
    out = {
        "src": a["src"], "dst": a["dst"], "edge_type_9": a["edge_type_9"], "edge_attr_16": a["edge_attr_16"],
        "x": a["x"], "w0": a["L0_gnn_W0"], "w1": a["L0_gnn_W1"], "w2": a["L0_gnn_W2"],
        "l1_msg": a["L1_gnn_W_msg"].transpose(0, 2, 1), "l1_ih": a["L1_gnn_W_ih"].transpose(0, 2, 1),
        "l1_hh": a["L1_gnn_W_hh"].transpose(0, 2, 1),
        "l2_msg": a["L2_gnn_W_msg"].T, "l2_ih": a["L2_gnn_W_ih"].T, "l2_hh": a["L2_gnn_W_hh"].T,
        "emb": a["L2_gnn_edge_embed"],
        "bias": np.stack(columns, axis=1),
        "rowb": np.concatenate([a["L1_gnn_b_msg"].reshape(-1), a["L2_gnn_b_msg"]]).reshape(1, -1),
        "qkvs": np.concatenate([a["L3_gnn_W" + k] for k in ("q", "k", "v", "skip")], axis=1),
        "qkvs_b": np.concatenate([a["L3_gnn_b" + k] for k in ("q", "k", "v", "skip")]).reshape(1, -1),
        "bq": a["L3_gnn_bq"].reshape(D, 1),
        "weT": a["L3_gnn_We"].T, "wbeta": a["L3_gnn_Wbeta"].reshape(3, D),
    }
    return {k: np.ascontiguousarray(v) for k, v in out.items()}
```

```python
from contextlib import ExitStack

import concourse.bass as bass
import concourse.mybir as mybir
import numpy as np

ALU = mybir.AluOpType
ACT = mybir.ActivationFunctionType
AX = mybir.AxisListType
F32, BF16, F16 = mybir.dt.float32, mybir.dt.bfloat16, mybir.dt.float16
I32, U8 = mybir.dt.int32, mybir.dt.uint8

P = 128
N, E, D = 3125, 100000, 128
NTYPE = 9
DE = 16
W = 112
NB = -(-N // W)
NP = NB * W
LASTROWS = N - (NB - 1) * W
BPC = 4
CH = BPC * W
NCH = NP // CH
ECOLS = -(-E // P)
ETAIL = E - (P - 1) * ECOLS
TG = 4
GE = TG * P
NG = P * ECOLS // GE + NB
REC = 20
R_SRC, R_DSTI, R_DSTC, R_TYPE = 16, 17, 18, 19
NO_SRC, NO_TYPE, NO_DST = float(W + 3), 100.0, 1e4
CENTER = NP // 2
MAGIC = 1.5 * 2.0 ** 23
HEADS, HD = 4, 32
QW = D + HEADS * DE + HEADS
MW = D + HEADS
EPS_LN = 1e-5

B_L0_0, B_L0_1, B_L0_2 = 0, 2, 4
B_L1 = 5
B_L2 = 17
NBIAS = 23


class Progress:

    def __init__(self, sem):
        self.sem, self.n = sem, 0

    def mark(self, ins):
        self.n += 1
        ins.then_inc(self.sem, 1)
        return (self.sem, self.n)


class Slot:

    def __init__(self, sem):
        self.sem, self.n = sem, 0

    def mark(self, ins):
        self.n += 16
        ins.then_inc(self.sem, 16)
        return (self.sem, self.n)


NOT_YET = "not issued yet"


def need(engine, *tokens):
    for t in tokens:
        if t is not None:
            assert t is not NOT_YET, "the producer comes later in the program"
            engine.wait_ge(t[0], t[1])


class Ctx:

    def __init__(self, nc, ctx, io):
        self.nc, self.ctx, self.io = nc, ctx, io
        self.pe, self.dve, self.act, self.pool, self.sp = nc.tensor, nc.vector, nc.scalar, nc.gpsimd, nc.sync
        self.PE, self.DVE, self.ACT, self.POOL = (
            Progress(ctx.enter_context(nc.semaphore(n))) for n in ("pe_done", "dve_done", "act_done", "pool_done"))

    def slot(self, name):
        return Slot(self.ctx.enter_context(self.nc.semaphore(name)))

    def dram(self, name, shape, dt):
        return self.nc.dram_tensor(name, shape, dt, kind="Internal").ap()


def edge_rows(ap, cols=1):
    whole = ap[0:(P - 1) * ECOLS * cols].rearrange("(p j) -> p j", j=ECOLS * cols)
    tail = ap[(P - 1) * ECOLS * cols:E * cols].rearrange("(p j) -> p j", p=1)
    return [(0, 112, whole[0:112, :]), (112, P - 1, whole[112:P - 1, :]), (P - 1, P, tail)]


def sort_edges(c, bins, flags):
    nc, sp, act, dve, pool, pe = c.nc, c.sp, c.act, c.dve, c.pool, c.pe
    with ExitStack() as st:
        def sb(name, shape, dt=F32):
            return st.enter_context(nc.sbuf_tensor(name, shape, dt))

        rec = sb("rec", [P, ECOLS, REC])
        fill = sb("fill", [P, NG * TG, REC])
        EC = 98
        stage = sb("stage", [P, 2, EC * DE])
        srci, dsti, typi = (sb(n, [P, ECOLS], I32) for n in ("srci", "dsti", "typi"))
        srcf, blk, rank, pos, ones_e = (sb(n, [P, ECOLS]) for n in ("srcf", "blk", "rank", "pos", "ones_e"))
        posi = sb("posi", [P, ECOLS], I32)
        mask = sb("mask", [P, NB, ECOLS], U8)
        cnt, gcnt, gend, gstart, off = (sb(n, [P, NB]) for n in ("cnt", "gcnt", "gend", "gstart", "off"))
        ones_b = sb("ones_b", [P, NB])
        ones_pp, below = sb("ones_pp", [P, P]), sb("below", [P, P])
        iota_g = sb("iota_g", [P, NG])
        rounded = sb("rounded", [P, NB])
        tot = st.enter_context(nc.psum_tensor("tot", [P, NB], F32))
        pre = st.enter_context(nc.psum_tensor("pre", [P, NB], F32))
        s_int = [c.slot(f"s_int{i}") for i in range(3)]
        s_stage = [[c.slot(f"s_stage{i}_{k}") for k in range(3)] for i in range(2)]
        s_fill, s_scatter = c.slot("s_fill"), c.slot("s_scatter")

        t_f = c.POOL.mark(pool.memset(fill[:, :, :], 0.0))
        need(pool, t_f)
        c.POOL.mark(pool.memset(fill[:, :, R_SRC:R_SRC + 1], NO_SRC))
        c.POOL.mark(pool.memset(fill[:, :, R_DSTC:R_DSTC + 1], NO_DST))
        t_f = c.POOL.mark(pool.memset(fill[:, :, R_TYPE:R_TYPE + 1], NO_TYPE))
        need(sp, t_f)
        t_fill = s_fill.mark(sp.dma_start(bins.rearrange("(p s) r -> p s r", p=P), fill[:, :, :]))

        t_ints = []
        for tile, name, pad in ((srci, "src", NP + 3), (dsti, "dst", 0), (typi, "edge_type_9", 0)):
            t_pad = c.DVE.mark(dve.memset(tile[:, ETAIL:ECOLS], pad))
            need(act, t_pad)
            s = s_int[len(t_ints)]
            for a, b, piece in edge_rows(c.io[name]):
                t = s.mark(act.dma_start(tile[a:b, 0:piece.shape[1]], piece))
            t_ints.append(t)

        t_one = c.DVE.mark(dve.memset(ones_e[:, :], 1.0))
        t_one = c.DVE.mark(dve.memset(ones_b[:, :], 1.0))
        t_pp = c.DVE.mark(dve.memset(ones_pp[:, :], 1.0))
        t_io = c.POOL.mark(pool.iota(iota_g[:, :], [[1, NG]], base=0, channel_multiplier=0,
                                     allow_small_or_imprecise_dtypes=True))
        need(pool, t_pp)
        t_below = c.POOL.mark(pool.affine_select(out=below[:, :], in_=ones_pp[:, :], compare_op=ALU.is_gt, fill=0.0,
                                                 base=0, pattern=[[1, P]], channel_multiplier=-1))

        need(dve, t_ints[0])
        t = c.DVE.mark(dve.tensor_copy(srcf[:, :], srci[:, :]))
        need(dve, t)
        t = c.DVE.mark(dve.tensor_scalar(blk[:, :], srcf[:, :], -(W - 1) / 2, 1.0 / W, ALU.add, ALU.mult))
        need(dve, t)
        t = c.DVE.mark(dve.tensor_scalar(blk[:, :], blk[:, :], MAGIC, None, ALU.add))
        need(dve, t)
        t = c.DVE.mark(dve.tensor_scalar(blk[:, :], blk[:, :], -MAGIC, float(NB - 1), ALU.add, ALU.min))
        need(dve, t)
        for b in range(NB):
            t_cnt = c.DVE.mark(dve.tensor_scalar(mask[:, b, :], blk[:, :], float(b), None, ALU.is_equal, ALU.add,
                                                 accum_out=cnt[:, b:b + 1]))
        need(pe, t_cnt, t_pp, t_below)
        t_tot = c.PE.mark(pe.matmul(tot[:, :], ones_pp[:, :], cnt[:, :], start=True, stop=True))
        t_pre = c.PE.mark(pe.matmul(pre[:, :], below[:, :], cnt[:, :], start=True, stop=True))
        need(dve, t_tot)
        t = c.DVE.mark(dve.tensor_scalar(rounded[:, :], tot[:, :], -(GE - 1) / 2, 1.0 / GE, ALU.add, ALU.mult))
        need(dve, t)
        t = c.DVE.mark(dve.tensor_scalar(rounded[:, :], rounded[:, :], MAGIC, None, ALU.add))
        need(dve, t)
        t = c.DVE.mark(dve.tensor_scalar(gcnt[:, :], rounded[:, :], -MAGIC, 1.0, ALU.add, ALU.add))
        need(dve, t, t_one)
        t = c.DVE.mark(dve.tensor_tensor_scan(gend[:, :], ones_b[:, :], gcnt[:, :], 0.0, ALU.mult, ALU.add))
        need(dve, t)
        t = c.DVE.mark(dve.tensor_tensor(gstart[:, :], gend[:, :], gcnt[:, :], ALU.subtract))
        need(dve, t, t_pre)
        t = c.DVE.mark(dve.scalar_tensor_tensor(out=off[:, :], in0=gstart[:, :], scalar=float(GE), in1=pre[:, :],
                                                op0=ALU.mult, op1=ALU.add))
        need(dve, t)
        t = c.DVE.mark(dve.tensor_scalar(off[:, :], off[:, :], -1.0, None, ALU.add))
        need(dve, t)
        t_pos = None
        for b in range(NB):
            need(dve, t_pos)
            t = c.DVE.mark(dve.tensor_tensor_scan(rank[:, :], ones_e[:, :], mask[:, b, :], off[:, b:b + 1],
                                                  ALU.mult, ALU.add))
            need(dve, t)
            t_pos = c.DVE.mark(dve.copy_predicated(pos[:, :], mask[:, b, :], rank[:, :]))
        need(dve, t_pos)
        t_pos = c.DVE.mark(dve.tensor_copy(posi[:, :], pos[:, :]))

        need(dve, t_ints[1], t_ints[2], t_pos)
        t = c.DVE.mark(dve.scalar_tensor_tensor(out=rec[:, :, R_SRC], in0=blk[:, :], scalar=-float(W), in1=srcf[:, :],
                                                op0=ALU.mult, op1=ALU.add))
        t = c.DVE.mark(dve.tensor_copy(rec[:, :, R_DSTI].bitcast(I32), dsti[:, :]))
        t = c.DVE.mark(dve.tensor_scalar(rec[:, :, R_DSTC], dsti[:, :], -float(CENTER), None, ALU.add))
        t = c.DVE.mark(dve.tensor_scalar(pos[:, :], srcf[:, :], float(NP), NO_TYPE, ALU.is_ge, ALU.mult))
        t = c.DVE.mark(dve.tensor_scalar(rank[:, :], typi[:, :], 0.0, float(NTYPE - 1), ALU.max, ALU.min))
        need(dve, t)
        t_rec = c.DVE.mark(dve.tensor_tensor(rec[:, :, R_TYPE], rank[:, :], pos[:, :], ALU.add))

        need(dve, t_io)
        blkg, same, last = flags["blk"], flags["same"], flags["last"]
        t = c.DVE.mark(dve.memset(blkg[:, :], 0.0))
        for b in range(NB - 1):
            need(dve, t)
            t = c.DVE.mark(dve.scalar_tensor_tensor(out=blkg[:, :], in0=iota_g[:, :], scalar=gend[:, b:b + 1],
                                                    in1=blkg[:, :], op0=ALU.is_ge, op1=ALU.add))
        t_m = c.DVE.mark(dve.memset(same[:, 0:1], 0.0))
        t_m = c.DVE.mark(dve.memset(last[:, NG - 1:NG], 1.0))
        need(dve, t)
        c.DVE.mark(dve.tensor_tensor(same[:, 1:NG], blkg[:, 1:NG], blkg[:, 0:NG - 1], ALU.is_equal))
        t = c.DVE.mark(dve.tensor_tensor(last[:, 0:NG - 1], blkg[:, 1:NG], blkg[:, 0:NG - 1], ALU.not_equal))
        need(dve, t)
        c.DVE.mark(dve.tensor_copy(flags["blki"][:, :], blkg[0:1, :]))
        flags["ready"] = c.DVE.mark(dve.tensor_copy(flags["lasti"][:, :], last[0:1, :]))

        npieces = -(-ECOLS // EC)
        t_stage_pad = []
        for k in range(2):
            t_stage_pad.append(c.POOL.mark(pool.memset(stage[:, k, :], 0.0)))
        t_copied = [None, None]
        t_ea = []
        ea = c.io["edge_attr_16"].rearrange("e k -> (e k)")
        for k in range(npieces):
            j0, j1 = k * EC, min(ECOLS, (k + 1) * EC)
            need(sp, t_stage_pad[k % 2], t_copied[k % 2])
            for i, (a, b, piece) in enumerate(edge_rows(ea, DE)):
                end = min(j1 * DE, piece.shape[1])
                if end > j0 * DE:
                    t = s_stage[k % 2][i].mark(sp.dma_start(stage[a:b, k % 2, 0:end - j0 * DE],
                                                            piece[:, j0 * DE:end]))
                    need(act, t)
            t_copied[k % 2] = c.ACT.mark(act.activation(
                rec[:, j0:j1, 0:DE], stage[:, k % 2, 0:(j1 - j0) * DE].rearrange("p (j k) -> p j k", k=DE), ACT.Copy))
            t_ea.append(t_copied[k % 2])

        need(pool, t_fill, t_pos, t_rec)
        for j in range(ECOLS):
            if j % EC == 0:
                need(pool, t_ea[j // EC])
            t = s_scatter.mark(pool.indirect_dma_start(
                bins, bass.IndirectOffsetOnAxis(ap=posi[:, j:j + 1].bitcast(mybir.dt.uint32), axis=0),
                rec[:, j, :], None))
        return t


SPANS = [(0, 2), (2, 4), (4, 6), (6, NCH)]
ALL_SPANS = (1 << len(SPANS)) - 1
FIRST = 1 << len(SPANS)


def build_counts(c, recs, flags, at, t_recs, lastslot):
    nc, sp, act, dve, pool, pe = c.nc, c.sp, c.act, c.dve, c.pool, c.pe
    ND, NS = 3, 3
    with ExitStack() as st:
        def sb(name, shape, dt=F32):
            return st.enter_context(nc.sbuf_tensor(name, shape, dt))

        iota_w, iota_t = sb("iota_w", [P, W]), sb("iota_t", [P, NTYPE])
        iota_n = sb("iota_n", [P, NP], F16)
        order = sb("order", [P, TG, P])
        gbase = sb("gbase", [P, NG])
        ident = sb("ident_b", [P, P], BF16)
        ones = sb("ones_s", [P, P])
        in_span, touched = sb("in_span", [P, NG, TG]), sb("touched", [P, NG])
        code, codei = sb("code", [1, NG]), sb("codei", [1, NG], I32)
        src1 = sb("src1", [P, NS, TG, P], BF16)
        dst1 = sb("dst1", [P, ND, TG, NP], BF16)
        acc = sb("acc", [P, NP])
        lastg = sb("lastg", [P, NG])
        zeros = sb("zeros", [P, CH], BF16)
        junk = sb("junk", [P, max(GE, NG)])
        lastrun = sb("lastrun", [P, NG])
        seen = sb("seen", [P, NG])
        marker, marker2, marker3 = sb("marker", [1, NG + 1]), sb("marker2", [1, 2 * NG]), sb("marker3", [1, NG])
        hi, lo = sb("hi", [P, NP], BF16), sb("lo", [P, NP], BF16)
        squares = sb("squares", [P, NG])
        ps = st.enter_context(nc.psum_tensor("ps_cnt", [P, NCH, 512], F32))
        psT = st.enter_context(nc.psum_tensor("psT", [P, 1024], BF16))
        touched_ps = ps[:, 0, 0:NG]
        s_at = c.slot("s_at")

        t_ones = c.DVE.mark(dve.memset(ones[:, :], 1.0))
        t_zero = c.DVE.mark(dve.memset(zeros[:, :], 0.0))
        t_sq0 = c.DVE.mark(dve.memset(squares[:, :], 0.0))
        t_mark = c.DVE.mark(dve.memset(marker[:, :], 0.0))
        t_code = c.DVE.mark(dve.memset(code[:, :], 0.0))
        c.POOL.mark(pool.iota(iota_w[:, :], [[1, W]], base=0, channel_multiplier=0, allow_small_or_imprecise_dtypes=True))
        c.POOL.mark(pool.iota(iota_t[:, :], [[1, NTYPE]], base=0, channel_multiplier=0, allow_small_or_imprecise_dtypes=True))
        c.POOL.mark(pool.iota(iota_n[:, :], [[1, NP]], base=-CENTER, channel_multiplier=0, allow_small_or_imprecise_dtypes=True))
        c.POOL.mark(pool.iota(order[:, :, :], [[1, TG], [TG, P]], base=1, channel_multiplier=0, allow_small_or_imprecise_dtypes=True))
        c.POOL.mark(pool.iota(gbase[:, :], [[GE, NG]], base=0, channel_multiplier=0, allow_small_or_imprecise_dtypes=True))
        c.POOL.mark(pool.memset(src1[:, :, :, :], 0.0))
        t = c.POOL.mark(pool.memset(ident[:, :], 0.0))
        need(pool, t)
        t_cst = c.POOL.mark(pool.affine_select(out=ident[:, :], in_=ident[:, :], compare_op=ALU.not_equal, fill=1.0,
                                               base=0, pattern=[[-1, P]], channel_multiplier=1))
        need(dve, t_cst, t_recs)
        need(pe, t_cst, t_ones)
        need(act, t_mark, t_sq0)
        need(pool, flags["ready"])
        need(sp, flags["ready"])

        targets = recs[:, :, :, R_DSTC]
        t_touched = None
        for s, (c0, c1) in enumerate(SPANS):
            need(dve, t_touched)
            t = c.DVE.mark(dve.tensor_scalar(in_span[:, :, :], targets, float(c0 * CH - CENTER), None, ALU.is_ge))
            need(dve, t)
            t = c.DVE.mark(dve.scalar_tensor_tensor(out=in_span[:, :, :], in0=targets, scalar=float(c1 * CH - CENTER),
                                                    in1=in_span[:, :, :], op0=ALU.is_lt, op1=ALU.mult))
            need(dve, t)
            t = c.DVE.mark(dve.tensor_reduce(touched[:, :], in_span[:, :, :], AX.X, ALU.max))
            need(pe, t)
            t = c.PE.mark(pe.matmul(touched_ps, ones[:, :], touched[:, :], start=True, stop=True))
            need(dve, t)
            t_touched = c.DVE.mark(dve.tensor_scalar(seen[:, :], touched_ps, 0.0, float(1 << s), ALU.is_gt, ALU.mult))
            need(dve, t_touched, t_code)
            t_code = c.DVE.mark(dve.tensor_tensor(code[:, :], code[:, :], seen[0:1, :], ALU.add))
        t = c.DVE.mark(dve.tensor_scalar(lastg[0:1, :], flags["same"][0:1, :], -float(FIRST), float(FIRST), ALU.mult, ALU.add))
        need(dve, t)
        t = c.DVE.mark(dve.tensor_tensor(code[:, :], code[:, :], lastg[0:1, :], ALU.add))
        need(dve, t)
        t_code = c.DVE.mark(dve.tensor_copy(codei[:, :], code[:, :]))
        need(pe, t_code, t_touched, t_zero)
        need(dve, t_code)

        t_hot, t_used, t_order, t_at, t_evac, t_hi, t_lo, t_sq = ([NOT_YET] * NG for _ in range(8))

        def flag(engine, tile, g, top):
            return engine.value_load(tile[0:1, g:g + 1], min_val=0, max_val=top)

        def targets_one_hot(g, c0, c1):
            for t in range(TG):
                dve.tensor_scalar(dst1[:, g % ND, t, c0 * CH:c1 * CH], iota_n[:, c0 * CH:c1 * CH],
                                  recs[:, g, t, R_DSTC:R_DSTC + 1], None, ALU.is_equal)

        def add_products(g, c0, c1):
            for t in range(TG):
                for ch in range(c0, c1):
                    pe.matmul(ps[:, ch, 0:CH], src1[:, g % NS, t, :], dst1[:, g % ND, t, ch * CH:(ch + 1) * CH],
                              start=False, stop=True, skip_group_check=True)

        def one_hots(g):
            spans = codes["dve"]
            if g + 1 < NG:
                codes["dve"] = flag(dve, codei, g + 1, FIRST + ALL_SPANS)
            free = t_used[g - ND] if g >= ND else None
            for s, (c0, c1) in enumerate(SPANS):
                with dve.If((spans >> s) & 1):
                    need(dve, free)
                    targets_one_hot(g, c0, c1)
            need(dve, free)
            dve.tensor_tensor(src1[:, g % NS, :, 0:W], iota_w[:, :].unsqueeze(1).to_broadcast([P, TG, W]),
                              recs[:, g, :, R_SRC:R_SRC + 1].to_broadcast([P, TG, W]), ALU.is_equal)
            t_hot[g] = c.DVE.mark(dve.tensor_tensor(src1[:, g % NS, :, W:W + NTYPE], iota_t[:, :].unsqueeze(1).to_broadcast([P, TG, NTYPE]),
                                                    recs[:, g, :, R_TYPE:R_TYPE + 1].to_broadcast([P, TG, NTYPE]), ALU.is_equal))

        def products(g):
            spans = codes["pe"]
            if g + 1 < NG:
                codes["pe"] = flag(pe, codei, g + 1, FIRST + ALL_SPANS)
            with pe.If(spans >= FIRST):
                need(pe, t_evac[g - 1] if g else None)
                for ch in range(NCH):
                    pe.matmul(ps[:, ch, 0:CH], ident[:, :], zeros[:, :], start=True, stop=True, skip_group_check=True)
            for s, (c0, c1) in enumerate(SPANS):
                with pe.If((spans >> s) & 1):
                    need(pe, t_hot[g])
                    add_products(g, c0, c1)
            need(pe, t_hot[g], t_order[g - 1] if g else None)
            for t in range(TG):
                tr = pe.transpose(psT[:, t * P:(t + 1) * P], src1[:, g % NS, t, :], ident[:, :])
            t_used[g] = c.PE.mark(tr)

        def evacuate(g):
            is_last = codes["act"]
            if g + 1 < NG:
                codes["act"] = flag(act, flags["lasti"], g + 1, 1)
            need(act, t_used[g])
            with act.If(is_last):
                need(act, t_sq[g - 1] if g else None)
                for ch in range(NCH):
                    act.activation(acc[:, ch * CH:(ch + 1) * CH], ps[:, ch, 0:CH], ACT.Copy)
            t_evac[g] = c.ACT.mark(act.activation(marker[:, g + 1:g + 2], marker[:, 0:1], ACT.Copy))
            with act.If(is_last):
                need(act, t_evac[g], t_at[g - 1] if g else None)
                act.activation(hi[:, :], acc[:, :], ACT.Copy)
            spent = is_last
            t_hi[g] = c.ACT.mark(act.activation(marker2[:, g:g + 1], marker[:, 0:1], ACT.Copy))
            is_last = codes["pool"]
            if g + 1 < NG:
                codes["pool"] = flag(pool, flags["lasti"], g + 1, 1)
            with pool.If(is_last):
                need(pool, t_hi[g], *((t_at[g - 1], t_lo[g - 1]) if g else ()))
                pool.tensor_tensor(lo[:, :], acc[:, :], hi[:, :], ALU.subtract)
            t_lo[g] = c.POOL.mark(pool.memset(marker3[:, g:g + 1], 0.0))
            with act.If(spent):
                need(act, t_lo[g])
                act.activation(acc[:, :], lo[:, :], ACT.Square, accum_out=squares[:, g:g + 1])
            t_sq[g] = c.ACT.mark(act.activation(marker2[:, NG + g:NG + g + 1], marker[:, 0:1], ACT.Copy))
            b = flag(sp, flags["blki"], g, NB - 1)
            is_last = flag(sp, flags["lasti"], g, 1)
            need(sp, t_hi[g], t_lo[g])
            s_at.mark(sp.dma_start(at[0, bass.ds(b * P, P), :], hi[:, :], cond=is_last))
            t_at[g] = s_at.mark(sp.dma_start(at[1, bass.ds(b * P, P), :], lo[:, :], cond=is_last))

        def last_slots(g):
            need(dve, t_used[g])
            t_order[g] = c.DVE.mark(dve.tensor_tensor_reduce(
                junk[:, 0:GE], psT[:, 0:GE], order[:, :, :].rearrange("p t k -> p (t k)"), 1.0, 0.0, ALU.mult, ALU.max, lastg[:, g:g + 1]))

        codes = {"dve": flag(dve, codei, 0, FIRST + ALL_SPANS), "pe": flag(pe, codei, 0, FIRST + ALL_SPANS),
                 "act": flag(act, flags["lasti"], 0, 1), "pool": flag(pool, flags["lasti"], 0, 1)}
        one_hots(0)
        one_hots(1)
        for g in range(NG):
            if g:
                last_slots(g - 1)
            if g + 2 < NG:
                one_hots(g + 2)
            products(g)
            evacuate(g)
        last_slots(NG - 1)

        need(dve, t_sq[-1], t_lo[-1], t_order[-1])
        t = c.DVE.mark(dve.tensor_reduce(junk[:, 0:1], squares[:, :], AX.X, ALU.max))
        need(dve, t)
        t = c.DVE.mark(dve.tensor_scalar(junk[:, 1:2], junk[:, 0:1], 0.0, None, ALU.is_gt))
        need(pe, t, t_evac[-1])
        t = c.PE.mark(pe.matmul(ps[:, 0, 0:1], ones[:, :], junk[:, 1:2], start=True, stop=True))
        need(dve, t, t_order[-1])
        t = c.DVE.mark(dve.tensor_scalar(marker3[0:1, 0:1], ps[0:1, 0, 0:1], 0.0, None, ALU.is_gt))
        need(dve, t)
        flags["big_ready"] = t = c.DVE.mark(dve.tensor_copy(flags["big"][:, :], marker3[0:1, 0:1]))
        need(dve, t)

        need(dve, t_order[-1])
        t = c.DVE.mark(dve.tensor_scalar(seen[:, :], lastg[:, :], 0.0, None, ALU.is_gt))
        need(dve, t)
        t = c.DVE.mark(dve.tensor_tensor(seen[:, :], seen[:, :], gbase[:, :], ALU.mult))
        need(dve, t)
        t = c.DVE.mark(dve.tensor_tensor(lastg[:, :], lastg[:, :], seen[:, :], ALU.add))
        need(dve, t)
        t_run = c.DVE.mark(dve.tensor_tensor_scan(lastrun[:, :], flags["same"][:, :], lastg[:, :], 0.0, ALU.mult, ALU.max))
        need(dve, t_run)
        t_sel = c.DVE.mark(dve.tensor_tensor(lastrun[:, :], lastrun[:, :], flags["last"][:, :], ALU.mult))
        need(dve, t_sel)
        for b in range(NB):
            t = c.DVE.mark(dve.scalar_tensor_tensor(out=junk[:, 0:NG], in0=flags["blk"][:, :], scalar=float(b), in1=lastrun[:, :],
                                                    op0=ALU.is_equal, op1=ALU.mult))
            need(dve, t)
            t = c.DVE.mark(dve.tensor_reduce(lastslot["f"][:, b:b + 1], junk[:, 0:NG], AX.X, ALU.max))
            need(dve, t)
        t = c.DVE.mark(dve.tensor_scalar(lastslot["f"][:, :], lastslot["f"][:, :], -1.0, 0.0, ALU.add, ALU.max))
        need(dve, t)
        lastslot["ready"] = c.DVE.mark(dve.tensor_copy(lastslot["i"][:, :], lastslot["f"][:, :]))
        need(dve, lastslot["ready"])
        return [t_at[-1]]


def layers(c, at, t_at, flags, x3_out):
    nc, sp, act, dve, pool, pe, io = c.nc, c.sp, c.act, c.dve, c.pool, c.pe, c.io
    NRING, NLO = 3, 2
    with ExitStack() as st:
        def sb(name, shape, dt=F32):
            return st.enter_context(nc.sbuf_tensor(name, shape, dt))

        ps = st.enter_context(nc.psum_tensor("ps", [P, 8, 512], F32))
        ring = sb("ring", [P, NRING, NP], BF16)
        ring_lo = sb("ring_lo", [P, NLO, NP], BF16)
        resT, degT, zT, hT = (sb(n, [P, NP]) for n in ("resT", "degT", "zT", "hT"))
        dinvT = x3_out
        wideT = sb("wideT", [P, 2, NP])
        xn = sb("xn", [P, NB, D])
        xp = sb("xp", [P, 3, NB, D], BF16)
        tmp = sb("tmp", [P, 2, 6, CH])
        dinvn = sb("dinvn", [P, NB])
        ident, ones, mean_w = sb("ident", [P, P]), sb("ones", [P, P]), sb("mean_w", [P, P])
        ident_h, ones_h = sb("ident_h", [P, P], BF16), sb("ones_h", [P, P], BF16)
        eps = sb("eps", [P, 1])
        bias = sb("bias", [P, NBIAS])
        gbias = sb("gbias", [P, 3, 4])
        w0, w1, w2 = sb("w0", [P, 2 * D]), sb("w1", [P, 2, 2 * D]), sb("w2", [P, 2, D])
        l1_msg, l1_ih, l1_hh = sb("l1_msg", [P, 2, 2, 2 * D]), sb("l1_ih", [P, 2, 2, 3 * D]), sb("l1_hh", [P, 2, 3 * D])
        l2_msg, l2_ih, l2_hh = sb("l2_msg", [P, D]), sb("l2_ih", [P, 3 * D]), sb("l2_hh", [P, 3 * D])
        rowb = sb("rowb", [1, 5 * D])

        s_w, s_x, s_types, s_emb = c.slot("s_w"), c.slot("s_x"), c.slot("s_types"), c.slot("s_emb")
        s_ring = [c.slot(f"s_ring{i}") for i in range(NRING)]
        s_lo = [c.slot(f"s_ring_lo{i}") for i in range(NLO)]
        need(pe, flags["big_ready"])
        need(sp, flags["big_ready"])
        big = {e: e.value_load(flags["big"][0:1, 0:1], min_val=0, max_val=1) for e in (pe, sp)}

        for out, in_ in ((w0[:, :], io["w0"]), (w1[:, :, :], io["w1"].rearrange("(k p) n -> p k n", p=P)),
                         (w2[:, :, :], io["w2"].rearrange("(k p) n -> p k n", p=P)),
                         (l1_hh[:, :, :], io["l1_hh"].rearrange("t p n -> p t n")),
                         (l2_msg[:, :], io["l2_msg"]), (l2_ih[:, :], io["l2_ih"]), (l2_hh[:, :], io["l2_hh"]),
                         (bias[:, :], io["bias"]), (rowb[:, :], io["rowb"])):
            s_w.mark(act.dma_start(out, in_))
        for t in range(2):
            s_w.mark(act.dma_start(l1_msg[:, t, :, :], io["l1_msg"][t, :, :].rearrange("(k p) n -> p k n", p=P)))
            t_w = s_w.mark(act.dma_start(l1_ih[:, t, :, :], io["l1_ih"][t, :, :].rearrange("(k p) n -> p k n", p=P)))

        xin = xn
        t0 = c.DVE.mark(dve.memset(xn[:, NB - 1, :], 0.0))
        c.DVE.mark(dve.memset(ones[:, :], 1.0))
        t1 = c.DVE.mark(dve.memset(ones_h[:, :], 1.0))
        t2 = c.DVE.mark(dve.memset(mean_w[:, :], 1.0 / D))
        t2 = c.DVE.mark(dve.memset(eps[:, :], EPS_LN))
        t3 = c.POOL.mark(pool.memset(ident[:, :], 0.0))
        need(pool, t3)
        t_ident = c.POOL.mark(pool.affine_select(out=ident[:, :], in_=ident[:, :], compare_op=ALU.not_equal, fill=1.0,
                                                 base=0, pattern=[[-1, P]], channel_multiplier=1))
        need(pool, t_ident)
        t_ident = c.POOL.mark(pool.tensor_copy(ident_h[:, :], ident[:, :]))
        need(act, t0)
        s_x.mark(act.dma_start(xin[0:W, 0:NB - 1, :], io["x"][0:(NB - 1) * W, :].rearrange("(b p) f -> p b f", p=W)))
        t_x = s_x.mark(act.dma_start(xin[0:LASTROWS, NB - 1, :], io["x"][(NB - 1) * W:N, :]))

        HB = NB // 2
        need(sp, *t_at)
        for b in range(NB):
            r = (b % HB) * NTYPE
            for plane, tile in enumerate((ring, ring_lo)):
                t_ty = s_types.mark(sp.dma_start(tile[r:r + NTYPE, b // HB, :], at[plane, b * P + W:b * P + W + NTYPE, :]))
        KT = HB * NTYPE

        bank_free = [None] * 8
        need(pe, t_ty, t1, t_ident, t_x, t_w)
        need(dve, t_w, t_x)
        need(act, t1, t2, t_w)

        def cols(ch):
            return slice(ch * CH, (ch + 1) * CH)

        def block_cols(b):
            return slice(b * W, (b + 1) * W)

        type_tiles = [(tile, h) for tile in (ring, ring_lo) for h in range(2)]
        t_deg = []
        for ch in range(NCH):
            for i, (tile, h) in enumerate(type_tiles):
                mm = pe.matmul(ps[:, ch, 0:CH], ones_h[0:KT, :], tile[0:KT, h, cols(ch)], start=(i == 0), stop=(i == 3))
            t = c.PE.mark(mm)
            need(act, t)
            bank_free[ch] = c.ACT.mark(act.activation(degT[:, cols(ch)], ps[:, ch, 0:CH], ACT.Copy))
            t_deg.append(bank_free[ch])
        for b in range(NB):
            for i, (tile, h) in enumerate(type_tiles):
                mm = pe.matmul(ps[0:W, 7, b:b + 1], tile[0:KT, h, block_cols(b)], ones_h[0:KT, 0:1], start=(i == 0), stop=(i == 3))
        t_degn = c.PE.mark(mm)
        ring_free, lo_free = [t_degn] * NRING, [t_degn] * NLO

        def one_over_root(out, in_, *tokens):
            need(dve, *tokens)
            t = c.DVE.mark(dve.tensor_scalar(out, in_, 1.0, None, ALU.add))
            need(act, t)
            t = c.ACT.mark(act.activation(out, out, ACT.Sqrt))
            need(dve, t)
            return c.DVE.mark(dve.reciprocal(out, out))

        t_dinvn = bank_free[7] = one_over_root(dinvn[0:W, :], ps[0:W, 7, 0:NB], t_degn)
        t_dinv = [one_over_root(dinvT[:, cols(ch)], degT[:, cols(ch)], t_deg[ch]) for ch in range(NCH)]

        t_res = []
        for ch in range(NCH):
            need(pe, bank_free[ch])
            for b in range(ch * BPC, (ch + 1) * BPC):
                mm = pe.transpose(ps[:, ch, (b % BPC) * W:(b % BPC + 1) * W], xin[0:W, b, :], ident[0:W, 0:W])
            t = c.PE.mark(mm)
            need(act, t)
            bank_free[ch] = c.ACT.mark(act.activation(resT[:, cols(ch)], ps[:, ch, 0:CH], ACT.Copy))
            t_res.append(bank_free[ch])
        need(dve, t_res[-1], t_dinvn)
        t = c.DVE.mark(dve.tensor_tensor(xin[0:W, :, :], xin[0:W, :, :], dinvn[0:W, :].unsqueeze(2).to_broadcast([W, NB, D]), ALU.mult))
        t_xn = [t] * NB

        state = {"block": 0, "parts_free": None}

        def split(rows, t_xn):
            out = []
            for k in range(NCH):
                bs = slice(k * BPC, (k + 1) * BPC)
                x, parts = xn[0:rows, bs, :], [xp[0:rows, i, bs, :] for i in range(3)]
                for i in range(3):
                    if i == 0:
                        need(act, state["parts_free"], *t_xn[bs])
                        need(dve, state["parts_free"])
                    if i < 2:
                        need(act, t if i else None)
                        t = c.ACT.mark(act.activation(parts[i], x, ACT.Copy))
                        need(dve, t)
                        t = c.DVE.mark(dve.tensor_tensor(x, x, parts[i], ALU.subtract))
                    else:
                        need(dve, t)
                        t = c.DVE.mark(dve.tensor_copy(parts[i], x))
                out += [t] * BPC
            return out

        def times_counts(rows, t_xn, self_loops=False):
            t_xn = split(rows, t_xn)
            for ch in range(NCH):
                need(pe, bank_free[ch])
            for b in range(NB):
                r, rl = state["block"] % NRING, state["block"] % NLO
                state["block"] += 1
                need(sp, ring_free[r])
                t = s_ring[r].mark(sp.dma_start(ring[:, r, :], at[0, b * P:(b + 1) * P, :]))
                need(sp, lo_free[rl])
                t_lo = s_lo[rl].mark(sp.dma_start(ring_lo[:, rl, :], at[1, b * P:(b + 1) * P, :], cond=big[sp]))
                need(pe, t, t_lo, t_xn[b])

                def hi_products():
                    for i in range(3):
                        for ch in range(NCH):
                            mm = pe.matmul(ps[:, ch, 0:CH], xp[0:rows, i, b, :], ring[0:rows, r, cols(ch)],
                                           start=(b == 0 and i == 0), stop=(b == NB - 1 and i == 2))
                    return mm

                if b < NB - 1:
                    hi_products()
                if b == NB - 2 and self_loops:
                    need(pe, t_xn[NB - 1])
                    for i in range(NB):
                        for part in range(3):
                            pe.matmul(ps[:, i // BPC, (i % BPC) * W:(i % BPC + 1) * W], xp[0:W, part, i, :], ident_h[0:W, 0:W],
                                      start=False, stop=False, skip_group_check=True)
                with pe.If(big[pe]):
                    for i in range(3):
                        for ch in range(NCH):
                            pe.matmul(ps[:, ch, 0:CH], xp[0:rows, i, b, :], ring_lo[0:rows, rl, cols(ch)],
                                      start=False, stop=False, skip_group_check=True)
                if b == NB - 1:
                    mm = hi_products()
                else:
                    mm = pe.matmul(ps[:, NCH, 0:1], ident_h[:, :], ident_h[:, 0:1], start=True, stop=True)
                ring_free[r] = lo_free[rl] = c.PE.mark(mm)
            state["parts_free"] = ring_free[r]
            return [ring_free[r]] * NCH

        bank_turn = {"n": 0}

        def next_bank():
            bank_turn["n"] = (bank_turn["n"] + 1) % 8
            need(pe, bank_free[bank_turn["n"]])
            return bank_turn["n"]

        def to_nodes(srcs, weights, width, t_src, evac, bias_row=None):
            out = []
            for b in range(NB):
                k7 = next_bank()
                need(pe, *t_src[b // BPC])
                if bias_row is not None:
                    pe.matmul(ps[0:W, k7, 0:width], ones[0:1, 0:W], bias_row, start=True, stop=False)
                for k, (s, w) in enumerate(zip(srcs, weights)):
                    mm = pe.matmul(ps[0:W, k7, 0:width], s[:, block_cols(b)], w, start=(k == 0 and bias_row is None),
                                   stop=(k == len(srcs) - 1))
                t = c.PE.mark(mm)
                bank_free[k7] = evac(k7, b, t)
                out.append(bank_free[k7])
            return out

        def norm(y, out, t_y):
            t_sq, res = [None] * NCH, []

            def centre(ch):
                k7 = next_bank()
                need(pe, t_y[ch])
                t = c.PE.mark(pe.matmul(ps[:, k7, 0:CH], mean_w[:, :], y[:, cols(ch)], start=True, stop=True))
                need(dve, t)
                t_c = bank_free[k7] = c.DVE.mark(dve.tensor_tensor(y[:, cols(ch)], y[:, cols(ch)], ps[:, k7, 0:CH], ALU.subtract))
                need(act, t_c, t_tmp[ch % 2])
                t_sq[ch] = c.ACT.mark(act.activation(tmp[:, ch % 2, 0, :], y[:, cols(ch)], ACT.Square))

            def divide(ch):
                k7 = next_bank()
                need(pe, t_sq[ch])
                t = c.PE.mark(pe.matmul(ps[:, k7, 0:CH], mean_w[:, :], tmp[:, ch % 2, 0, :], start=True, stop=True))
                rstd = tmp[:, ch % 2, 1, :]
                need(act, t)
                t = bank_free[k7] = c.ACT.mark(act.activation(rstd, ps[:, k7, 0:CH], ACT.Sqrt, bias=eps[:, 0:1]))
                need(dve, t)
                t = c.DVE.mark(dve.reciprocal(rstd, rstd))
                need(dve, t)
                t_tmp[ch % 2] = c.DVE.mark(dve.tensor_tensor(out[:, cols(ch)], y[:, cols(ch)], rstd, ALU.mult))
                res.append(t_tmp[ch % 2])

            centre(0)
            for ch in range(NCH):
                if ch + 1 < NCH:
                    centre(ch + 1)
                divide(ch)
            return res

        t_tmp = [None, None]

        t_ps = times_counts(W, t_xn, self_loops=True)
        t_z = []
        for ch in range(NCH):
            need(dve, t_ps[ch], t_dinv[ch])
            bank_free[ch] = c.DVE.mark(dve.tensor_tensor(zT[:, cols(ch)], ps[:, ch, 0:CH], dinvT[:, cols(ch)], ALU.mult))
            t_z.append(bank_free[ch])
        t_wide = []
        for ch in range(NCH):
            for half in range(2):
                k7 = next_bank()
                need(pe, t_z[ch])
                t = c.PE.mark(pe.matmul(ps[:, k7, 0:CH], w0[:, half * D:(half + 1) * D], zT[:, cols(ch)], start=True, stop=True))
                need(act, t)
                bank_free[k7] = c.ACT.mark(act.activation(wideT[:, half, cols(ch)], ps[:, k7, 0:CH], ACT.Relu,
                                                          bias=bias[:, B_L0_0 + half:B_L0_0 + half + 1]))
            t_wide.append((bank_free[k7],))

        def scaled(width):
            def evac(k7, b, t):
                need(dve, t)
                return c.DVE.mark(dve.tensor_scalar(xn[0:W, b, 0:width], ps[0:W, k7, 0:width], dinvn[0:W, b:b + 1], None, ALU.mult))
            return evac

        t_in, t_wide = t_wide, [None] * NCH
        for half in range(2):
            f, result = slice(half * D, (half + 1) * D), (hT, wideT[:, 0, :])[half]
            t_xn = to_nodes([wideT[:, 0, :], wideT[:, 1, :]], [w1[:, 0, f], w1[:, 1, f]], D, t_in, scaled(D))
            t_ps = times_counts(W, t_xn, self_loops=True)
            for ch in range(NCH):
                need(dve, t_ps[ch])
                t = bank_free[ch] = c.DVE.mark(dve.tensor_tensor(result[:, cols(ch)], ps[:, ch, 0:CH], dinvT[:, cols(ch)], ALU.mult))
                need(act, t)
                t = c.ACT.mark(act.activation(result[:, cols(ch)], result[:, cols(ch)], ACT.Relu,
                                              bias=bias[:, B_L0_1 + half:B_L0_1 + half + 1]))
                t_wide[ch] = (t,)

        t_xn = to_nodes([hT, wideT[:, 0, :]], [w2[:, 0, :], w2[:, 1, :]], D, t_wide, scaled(D))
        t_ps = times_counts(W, t_xn, self_loops=True)
        t_y = []
        for ch in range(NCH):
            need(dve, t_ps[ch])
            t = bank_free[ch] = c.DVE.mark(dve.tensor_tensor(zT[:, cols(ch)], ps[:, ch, 0:CH], dinvT[:, cols(ch)], ALU.mult))
            need(dve, t)
            t_y.append(c.DVE.mark(dve.scalar_tensor_tensor(out=zT[:, cols(ch)], in0=zT[:, cols(ch)], scalar=bias[:, B_L0_2:B_L0_2 + 1],
                                                           in1=resT[:, cols(ch)], op0=ALU.add, op1=ALU.add)))
        t_res = norm(zT, resT, t_y)

        for k, b0 in enumerate((B_L1, B_L1 + 6, B_L2)):
            t = c.DVE.mark(dve.tensor_tensor(gbias[:, k, 0:2], bias[:, b0:b0 + 2], bias[:, b0 + 3:b0 + 5], ALU.add))
            need(dve, t)
            t = c.DVE.mark(dve.tensor_scalar(gbias[:, k, 2:3], gbias[:, k, 1:2], -1.0, None, ALU.mult))
        t_gb = t
        need(act, t_gb)

        def gru(k, b0, ins, w_ih, w_hh, h, out, t_in, masked):
            res = []
            for ch in range(NCH):
                p4 = 4 * (ch % 2)
                for q in range(4):
                    need(pe, bank_free[p4 + q])
                need(pe, *t_in[ch])
                for q, parts in enumerate(((1, 1), (1, 1), (1, 0), (0, 1))):
                    f = slice(min(q, 2) * D, (min(q, 2) + 1) * D)
                    ops = [(w[:, f], s[:, cols(ch)]) for w, s in zip(w_ih, ins)] * parts[0] + [(w_hh[:, f], h[:, cols(ch)])] * parts[1]
                    for i, (w, s) in enumerate(ops):
                        mm = pe.matmul(ps[:, p4 + q, 0:CH], w, s, start=(i == 0), stop=(i == len(ops) - 1))
                t = c.PE.mark(mm)
                r, omz, hn, n, d = (tmp[:, ch % 2, i, :] for i in range(5))
                need(act, t, t_tmp[ch % 2])
                t_r = bank_free[p4] = c.ACT.mark(act.activation(r, ps[:, p4, 0:CH], ACT.Sigmoid, bias=gbias[:, k, 0:1]))
                t_z = bank_free[p4 + 1] = c.ACT.mark(act.activation(omz, ps[:, p4 + 1, 0:CH], ACT.Sigmoid, bias=gbias[:, k, 2:3], scale=-1.0))
                need(dve, t_r)
                t = bank_free[p4 + 3] = c.DVE.mark(dve.scalar_tensor_tensor(
                    out=hn, in0=ps[:, p4 + 3, 0:CH], scalar=bias[:, b0 + 5:b0 + 6], in1=r, op0=ALU.add, op1=ALU.mult))
                need(dve, t)
                t = bank_free[p4 + 2] = c.DVE.mark(dve.tensor_tensor(hn, hn, ps[:, p4 + 2, 0:CH], ALU.add))
                need(act, t)
                t_n = c.ACT.mark(act.activation(n, hn, ACT.Tanh, bias=bias[:, b0 + 2:b0 + 3]))
                need(dve, t_z)
                if masked:
                    t = c.DVE.mark(dve.scalar_tensor_tensor(out=omz, in0=degT[:, cols(ch)], scalar=1.0, in1=omz, op0=ALU.min, op1=ALU.mult))
                    need(dve, t)
                need(dve, t_n)
                t = c.DVE.mark(dve.tensor_tensor(d, n, h[:, cols(ch)], ALU.subtract))
                need(dve, t)
                t = c.DVE.mark(dve.tensor_tensor(d, d, omz, ALU.mult))
                need(dve, t)
                t_tmp[ch % 2] = c.DVE.mark(dve.tensor_tensor(out[:, cols(ch)], h[:, cols(ch)], d, ALU.add))
                res.append(t_tmp[ch % 2])
            return res

        h, t_h = resT, t_res
        for step in range(2):
            for ch in range(NCH):
                k7 = next_bank()
                need(pe, t_h[ch])
                for b in range(ch * BPC, (ch + 1) * BPC):
                    mm = pe.transpose(ps[0:W, k7, (b % BPC) * P:(b % BPC + 1) * P], h[:, block_cols(b)], ident[:, :])
                t = c.PE.mark(mm)
                need(act, t)
                bank_free[k7] = c.ACT.mark(act.activation(xn[0:W, ch * BPC:(ch + 1) * BPC, 0:D],
                                                          ps[0:W, k7, :].rearrange("p (b f) -> p b f", f=D), ACT.Copy))
                for b in range(BPC):
                    t_xn[ch * BPC + b] = bank_free[k7]
            t_ps = times_counts(W, t_xn)
            t_z = []
            for ch in range(NCH):
                need(act, t_ps[ch])
                bank_free[ch] = c.ACT.mark(act.activation(zT[:, cols(ch)], ps[:, ch, 0:CH], ACT.Copy))
                t_z.append(bank_free[ch])
            t_agg = []
            for ch in range(NCH):
                dh = tmp[:, ch % 2, 5, :]
                need(dve, t_h[ch], t_agg[ch - 2][0] if ch >= 2 else None)
                t_dh = c.DVE.mark(dve.tensor_tensor(dh, h[:, cols(ch)], degT[:, cols(ch)], ALU.mult))
                for half in range(2):
                    f = slice(half * D, (half + 1) * D)
                    k7 = next_bank()
                    need(pe, t_z[ch])
                    pe.matmul(ps[:, k7, 0:CH], l1_msg[:, step, 0, f], zT[:, cols(ch)], start=True, stop=False)
                    need(pe, t_dh)
                    pe.matmul(ps[:, k7, 0:CH], l1_msg[:, step, 1, f], dh, start=False, stop=False)
                    mm = pe.matmul(ps[:, k7, 0:CH], rowb[0:1, step * 2 * D + half * D:step * 2 * D + (half + 1) * D],
                                   degT[0:1, cols(ch)], start=False, stop=True)
                    t = c.PE.mark(mm)
                    need(act, t)
                    bank_free[k7] = c.ACT.mark(act.activation(wideT[:, half, cols(ch)], ps[:, k7, 0:CH], ACT.Copy))
                t_agg.append((bank_free[k7],))
            t_h = gru(step, B_L1 + 6 * step, [wideT[:, 0, :], wideT[:, 1, :]],
                      [l1_ih[:, step, 0, :], l1_ih[:, step, 1, :]], l1_hh[:, step, :], h, hT, t_agg, True)
            h = hT
        t_y = []
        for ch in range(NCH):
            need(dve, t_h[ch])
            t_y.append(c.DVE.mark(dve.tensor_tensor(zT[:, cols(ch)], hT[:, cols(ch)], resT[:, cols(ch)], ALU.add)))
        t_res = norm(zT, resT, t_y)

        need(act, t_ps[0])
        for b in range(NB):
            t_emb = s_emb.mark(act.dma_start(xn[W:W + NTYPE, b, 0:D], io["emb"]))

        def plain(k7, b, t):
            need(dve, t)
            return c.DVE.mark(dve.tensor_copy(xn[0:W, b, 0:D], ps[0:W, k7, 0:D]))

        t_xn = to_nodes([resT], [l2_msg[:, :]], D, [(t,) for t in t_res], plain, bias_row=rowb[0:1, 4 * D:5 * D])
        need(act, t_emb)
        need(dve, t_emb)
        t_ps = times_counts(W + NTYPE, t_xn)
        t_z = []
        for ch in range(NCH):
            need(act, t_ps[ch])
            bank_free[ch] = c.ACT.mark(act.activation(zT[:, cols(ch)], ps[:, ch, 0:CH], ACT.Copy))
            t_z.append((bank_free[ch],))
        t_h = gru(2, B_L2, [zT], [l2_ih[:, :]], l2_hh[:, :], resT, hT, t_z, False)
        t_y = []
        for ch in range(NCH):
            need(dve, t_h[ch])
            t_y.append(c.DVE.mark(dve.tensor_tensor(zT[:, cols(ch)], hT[:, cols(ch)], resT[:, cols(ch)], ALU.add)))
        t_x3 = norm(zT, x3_out, t_y)
        return t_x3


def attention(c, recs, load_records, bins, flags, lastslot, x3T, t_x3, out):
    nc, sp, act, dve, pool, pe, io = c.nc, c.sp, c.act, c.dve, c.pool, c.pe, c.io
    kv_d = c.dram("kv_d", (NP, 2 * D), F32)
    q_d = c.dram("q_d", (NP, QW), F32)
    sums_d = c.dram("sums_d", (NP, MW), F32)
    with ExitStack() as st:
        def sb(name, shape, dt=F32, where=None):
            return (where or st).enter_context(nc.sbuf_tensor(name, shape, dt))

        xs, x3n = sb("xs", [P, NB, D]), sb("x3n", [P, NB, D])
        wb = sb("wb", [P, 3, D])
        ident = sb("ident4", [P, P])
        eps = sb("eps4", [P, 1])
        iota_w = sb("iota_w4", [P, W])
        s_w, s_out = c.slot("s_w4"), c.slot("s_out")
        s_kv, s_q = c.slot("s_kvd"), c.slot("s_qd")

        t_i = c.POOL.mark(pool.memset(ident[:, :], 0.0))
        need(pool, t_i)
        t_ident = c.POOL.mark(pool.affine_select(out=ident[:, :], in_=ident[:, :], compare_op=ALU.not_equal, fill=1.0,
                                                 base=0, pattern=[[-1, P]], channel_multiplier=1))
        t_iota = c.POOL.mark(pool.iota(iota_w[:, :], [[1, W]], base=0, channel_multiplier=0, allow_small_or_imprecise_dtypes=True))
        t_eps = c.DVE.mark(dve.memset(eps[:, :], EPS_LN))

        with ExitStack() as st2:
            qn, kvn = sb("qn", [P, NB, QW], where=st2), sb("kvn", [P, NB, 2 * D], where=st2)
            qT = sb("qT", [P, 2, CH], where=st2)
            w4, b4, we4, bq = (sb("w4", [P, 4 * D], where=st2), sb("b4", [P, 4 * D], where=st2),
                               sb("we4", [P, HEADS * DE], where=st2), sb("bq", [P, 1], where=st2))
            lastrec = sb("lastrec", [P, NB, REC], where=st2)
            lastkv = kvn
            prod, prod_e = sb("prod0", [P, NB, D], where=st2), sb("prod_e0", [P, NB, HEADS * DE], where=st2)
            sc, sc_e = sb("sc0", [P, NB * HEADS], where=st2), sb("sc_e0", [P, NB * HEADS], where=st2)
            ps = st2.enter_context(nc.psum_tensor("ps4", [P, 8, 512], F32))
            s_rec, s_lkv = c.slot("s_lrec"), [c.slot(f"s_lkv{i}") for i in range(NCH)]

            t_we = c.DVE.mark(dve.memset(we4[:, :], 0.0))
            need(act, t_we)
            for a, b in ((w4[:, :], io["qkvs"]), (b4[:, :], io["qkvs_b"].to_broadcast([P, 4 * D])), (bq[:, :], io["bq"]),
                         (wb[:, :, :], io["wbeta"].rearrange("(o k) f -> o k f", o=1).to_broadcast([P, 3, D]))):
                s_w.mark(act.dma_start(a, b))
            for h in range(HEADS):
                t_w = s_w.mark(act.dma_start(we4[h * HD:(h + 1) * HD, h * DE:(h + 1) * DE], io["weT"][h * HD:(h + 1) * HD, :]))
            need(sp, t_w)
            t_recs = load_records()
            need(pool, lastslot["ready"])
            for b in range(NB):
                t_lrec = s_rec.mark(pool.indirect_dma_start(
                    lastrec[0:W, b, :], None, bins,
                    bass.IndirectOffsetOnAxis(ap=lastslot["i"][0:W, b:b + 1].bitcast(mybir.dt.uint32), axis=0)))

            need(pe, *t_x3)
            need(pe, t_w, t_ident)
            need(dve, t_w)
            need(act, t_w)
            bank_free = [None] * 8
            t_qT, t_prodq, t_q = [None] * NCH, [None] * NCH, [None] * NCH
            scale = 1.0 / HD ** 0.5

            def project(b):
                k7, cols = b % 3, slice(b * W, (b + 1) * W)
                need(pe, bank_free[k7])
                t = c.PE.mark(pe.matmul(ps[0:W, k7, :], x3T[:, cols], w4[:, :], start=True, stop=True))
                need(dve, t)
                c.DVE.mark(dve.tensor_tensor(kvn[0:W, b, :], ps[0:W, k7, D:3 * D], b4[0:W, D:3 * D], ALU.add))
                c.DVE.mark(dve.tensor_tensor(xs[0:W, b, :], ps[0:W, k7, 3 * D:4 * D], b4[0:W, 3 * D:4 * D], ALU.add))
                bank_free[k7] = c.DVE.mark(dve.tensor_tensor(qn[0:W, b, 0:D], ps[0:W, k7, 0:D], b4[0:W, 0:D], ALU.add))
                k7 = 3 + b % 2
                need(pe, bank_free[k7])
                t = c.PE.mark(pe.transpose(ps[0:W, k7, 0:P], x3T[:, cols], ident[:, :]))
                need(act, t)
                bank_free[k7] = c.ACT.mark(act.activation(x3n[0:W, b, :], ps[0:W, k7, 0:P], ACT.Copy))
                return bank_free[b % 3]

            def q_feature_major(ch):
                need(pe, bank_free[5])
                t = c.PE.mark(pe.matmul(ps[:, 5, 0:CH], w4[:, 0:D], x3T[:, ch * CH:(ch + 1) * CH], start=True, stop=True))
                need(act, t, t_prodq[ch - 2] if ch >= 2 else None)
                bank_free[5] = t_qT[ch] = c.ACT.mark(act.activation(qT[:, ch % 2, :], ps[:, 5, 0:CH], ACT.Identity, bias=bq[:, 0:1]))

            def q_times_we(ch):
                bank = 6 + ch % 2
                need(pe, t_qT[ch], bank_free[bank])
                for i in range(BPC):
                    mm = pe.matmul(ps[0:W, bank, i * HEADS * DE:(i + 1) * HEADS * DE], qT[:, ch % 2, i * W:(i + 1) * W], we4[:, :], start=True, stop=True)
                t_prodq[ch] = c.PE.mark(mm)
                need(act, t_prodq[ch])
                bank_free[bank] = t_q[ch] = c.ACT.mark(act.activation(
                    qn[0:W, ch * BPC:(ch + 1) * BPC, D:D + HEADS * DE],
                    ps[0:W, bank, 0:BPC * HEADS * DE].rearrange("p (b f) -> p b f", b=BPC), ACT.Copy, scale=scale))

            for ch in range(NCH):
                q_feature_major(ch)
                for b in range(ch * BPC, (ch + 1) * BPC):
                    t_block = project(b)
                q_times_we(ch)
                need(dve, t_block)
                t_s = c.DVE.mark(dve.tensor_scalar(qn[0:W, ch * BPC:(ch + 1) * BPC, 0:D], qn[0:W, ch * BPC:(ch + 1) * BPC, 0:D], scale, None, ALU.mult))
                need(sp, t_block)
                nodes = slice(ch * CH, (ch + 1) * CH)
                t_kvd = s_kv.mark(sp.dma_start(kv_d[nodes, :].rearrange("(b p) f -> p b f", p=W), kvn[0:W, ch * BPC:(ch + 1) * BPC, :]))
            t_x3n, t_q = bank_free[3 + (NB - 1) % 2], t_q[-1]
            need(pool, t_kvd, t_lrec)
            need(dve, t_q, t_lrec, t_s)
            for ch in range(NCH):
                bs = slice(ch * BPC, (ch + 1) * BPC)
                nodes = slice(ch * CH, (ch + 1) * CH)
                for b in range(ch * BPC, (ch + 1) * BPC):
                    t_lkv = s_lkv[ch].mark(pool.indirect_dma_start(
                        lastkv[0:W, b, :], None, kv_d,
                        bass.IndirectOffsetOnAxis(ap=lastrec[0:W, b, R_DSTI:R_DSTI + 1].bitcast(mybir.dt.uint32), axis=0)))
                p, pe_ = prod[0:W, bs, :], prod_e[0:W, bs, :]
                s1, s2 = (x[0:W, ch * BPC * HEADS:(ch + 1) * BPC * HEADS] for x in (sc, sc_e))
                t2 = c.DVE.mark(dve.tensor_tensor(pe_.rearrange("p b (h d) -> p b h d", h=HEADS),
                                                  qn[0:W, bs, D:D + HEADS * DE].rearrange("p b (h d) -> p b h d", h=HEADS),
                                                  lastrec[0:W, bs, 0:DE].unsqueeze(2).to_broadcast([W, BPC, HEADS, DE]), ALU.mult))
                need(dve, t_lkv)
                t = c.DVE.mark(dve.tensor_tensor(p, qn[0:W, bs, 0:D], lastkv[0:W, bs, 0:D], ALU.mult))
                need(dve, t2)
                t2 = c.DVE.mark(dve.tensor_reduce(s2, pe_.rearrange("p b (h c) -> p (b h) c", h=HEADS), AX.X, ALU.add))
                need(dve, t)
                t = c.DVE.mark(dve.tensor_reduce(s1, p.rearrange("p b (h c) -> p (b h) c", h=HEADS), AX.X, ALU.add, negate=True))
                need(dve, t)
                t = c.DVE.mark(dve.tensor_tensor(qn[0:W, bs, D + HEADS * DE:QW], s1.rearrange("p (b h) -> p b h", h=HEADS),
                                                 s2.rearrange("p (b h) -> p b h", h=HEADS), ALU.subtract))
                need(sp, t)
                t_qd = s_q.mark(sp.dma_start(q_d[nodes, :].rearrange("(b p) f -> p b f", p=W), qn[0:W, bs, :]))
            need(sp, t_qd, t_x3n)
            nc.all_engine_barrier()

        NKV, NQ, NS = 4, 3, 4
        with ExitStack() as st2:
            kv = sb("kv", [P, NKV, TG, 2 * D], where=st2)
            qb = sb("qb", [P, NQ, QW], where=st2)
            src1 = sb("src14", [P, NS, TG, W], where=st2)
            srcT = sb("srcT", [P, 3, GE], where=st2)
            prod, prod_e = sb("prod", [P, TG, D], where=st2), sb("prod_e", [P, TG, HEADS * DE], where=st2)
            sc, sc_e = sb("sc", [P, TG, HEADS], where=st2), sb("sc_e", [P, TG, HEADS], where=st2)
            msg = sb("msg", [P, 2, TG, MW], where=st2)
            acc = sb("acc4", [P, 2, MW], where=st2)
            psT = st2.enter_context(nc.psum_tensor("psT4", [P, 2, 512], F32))
            psQ = st2.enter_context(nc.psum_tensor("psQ", [P, 2, -(-TG // 2), 512], F32))
            psO = st2.enter_context(nc.psum_tensor("psO", [P, 2, 512], F32))
            qrows = psQ[:, :, :, :].rearrange("p i k (two f) -> p i (k two) f", two=2)[:, :, 0:TG, :]
            s_g = [c.slot(f"s_gather{i}") for i in range(NKV)]
            s_qb = [c.slot(f"s_qb{i}") for i in range(NQ)]
            s_st = [c.slot(f"s_sums{i}") for i in range(2)]

            need(dve, t_iota, t_recs)
            need(pool, t_recs)
            t_src1, t_T, t_Q, t_kv, t_qb, t_msgs, t_sum, t_prod, t_srcT, t_ex, t_acc = ([NOT_YET] * NG for _ in range(11))
            t_st = [None, None]
            blks = {}

            def sources(g):
                need(dve, t_sum[g - NS] if g >= NS else None)
                t_src1[g] = c.DVE.mark(dve.tensor_tensor(src1[:, g % NS, :, :], iota_w[:, :].unsqueeze(1).to_broadcast([P, TG, W]),
                                                         recs[:, g, :, R_SRC:R_SRC + 1].to_broadcast([P, TG, W]), ALU.is_equal))

            def fetch(g):
                need(pool, t_msgs[g - NKV] if g >= NKV else None)
                for t in range(TG):
                    t_kv[g] = s_g[g % NKV].mark(pool.indirect_dma_start(
                        kv[:, g % NKV, t, :], None, kv_d,
                        bass.IndirectOffsetOnAxis(ap=recs[:, g, t, R_DSTI:R_DSTI + 1].bitcast(mybir.dt.uint32), axis=0)))
                b = sp.value_load(flags["blki"][0:1, g:g + 1], min_val=0, max_val=NB - 1)
                need(sp, t_Q[g - NQ] if g >= NQ else None)
                t_qb[g] = s_qb[g % NQ].mark(sp.dma_start(qb[0:W, g % NQ, :], q_d[bass.ds(b * W, W), :]))

            def turn(g):
                need(pe, t_src1[g], t_srcT[g - 2] if g >= 2 else None)
                for t in range(TG):
                    mm = pe.transpose(psT[0:W, g % 2, t * P:(t + 1) * P], src1[:, g % NS, t, :], ident[:, :])
                t_T[g] = c.PE.mark(mm)
                need(act, t_T[g], t_Q[g - 3] if g >= 3 else None)
                t_srcT[g] = c.ACT.mark(act.activation(srcT[0:W, g % 3, :], psT[0:W, g % 2, 0:GE], ACT.Copy))

            def spread(g):
                need(pe, t_srcT[g], t_qb[g], t_prod[g - 2] if g >= 2 else None)
                for t in range(TG):
                    mm = pe.matmul(psQ[:, g % 2, t // 2, (t % 2) * 256:(t % 2) * 256 + QW], srcT[0:W, g % 3, t * P:(t + 1) * P],
                                   qb[0:W, g % NQ, :], start=True, stop=True)
                t_Q[g] = c.PE.mark(mm)

            def scores(g):
                k = g % NKV
                need(dve, t_Q[g], t_kv[g])
                t1 = c.DVE.mark(dve.tensor_tensor(prod[:, :, :], qrows[:, g % 2, :, 0:D], kv[:, k, :, 0:D], ALU.mult))
                t2 = c.DVE.mark(dve.tensor_tensor(prod_e[:, :, :].rearrange("p t (h d) -> p t h d", h=HEADS),
                                                  qrows[:, g % 2, :, D:D + HEADS * DE].rearrange("p t (h d) -> p t h d", h=HEADS),
                                                  recs[:, g, :, 0:DE].unsqueeze(2).to_broadcast([P, TG, HEADS, DE]), ALU.mult))
                need(dve, t1)
                t1 = c.DVE.mark(dve.tensor_reduce(sc[:, :, :], prod[:, :, :].rearrange("p t (h c) -> p t h c", h=HEADS), AX.X, ALU.add))
                need(dve, t2)
                t2 = c.DVE.mark(dve.tensor_reduce(sc_e[:, :, :], prod_e[:, :, :].rearrange("p t (h c) -> p t h c", h=HEADS), AX.X, ALU.add))
                need(dve, t1)
                t1 = t_prod[g] = c.DVE.mark(dve.tensor_tensor(sc[:, :, :], sc[:, :, :], qrows[:, g % 2, :, D + HEADS * DE:QW], ALU.add))
                need(dve, t1, t2)
                t1 = c.DVE.mark(dve.tensor_tensor(sc[:, :, :], sc[:, :, :], sc_e[:, :, :], ALU.add))
                need(act, t1, t_sum[g - 2] if g >= 2 else None)
                t_ex[g] = c.ACT.mark(act.activation(msg[:, g % 2, :, D:MW], sc[:, :, :], ACT.Exp))

            def messages(g):
                k = g % NKV
                if g + 3 < NG:
                    sources(g + 3)
                need(dve, t_ex[g])
                t_msgs[g] = c.DVE.mark(dve.tensor_tensor(
                    msg[:, g % 2, :, 0:D].rearrange("p t (h c) -> p t h c", h=HEADS),
                    kv[:, k, :, D:2 * D].rearrange("p t (h c) -> p t h c", h=HEADS),
                    msg[:, g % 2, :, D:MW].unsqueeze(3).to_broadcast([P, TG, HEADS, HD]), ALU.mult))
                need(pe, t_msgs[g], t_acc[g - 2] if g >= 2 else None)
                for t in range(TG):
                    mm = pe.matmul(psO[0:W, g % 2, 0:MW], src1[:, g % NS, t, :], msg[:, g % 2, t, :], start=(t == 0), stop=(t == TG - 1))
                t_sum[g] = c.PE.mark(mm)

            def accumulate(g):
                need(dve, t_sum[g], t_acc[g - 1] if g else None, t_st[g % 2])
                if g == 0:
                    ins = dve.tensor_copy(acc[0:W, 0, :], psO[0:W, 0, 0:MW])
                else:
                    ins = dve.scalar_tensor_tensor(out=acc[0:W, g % 2, :], in0=acc[0:W, (g - 1) % 2, :], scalar=flags["same"][0:W, g:g + 1],
                                                   in1=psO[0:W, g % 2, 0:MW], op0=ALU.mult, op1=ALU.add)
                t_acc[g] = c.DVE.mark(ins)
                b = sp.value_load(flags["blki"][0:1, g:g + 1], min_val=0, max_val=NB - 1)
                is_last = sp.value_load(flags["lasti"][0:1, g:g + 1], min_val=0, max_val=1)
                need(sp, t_acc[g])
                t_st[g % 2] = s_st[g % 2].mark(sp.dma_start(sums_d[bass.ds(b * W, W), :], acc[0:W, g % 2, :], cond=is_last))

            for g in range(3):
                sources(g)
                fetch(g)
            turn(0)
            turn(1)
            spread(0)
            for g in range(NG):
                if g + 3 < NG:
                    fetch(g + 3)
                if g + 2 < NG:
                    turn(g + 2)
                scores(g)
                if g + 1 < NG:
                    spread(g + 1)
                messages(g)
                if g:
                    accumulate(g - 1)
            accumulate(NG - 1)
            need(sp, *t_st)
            nc.all_engine_barrier()

        sums = sb("sums", [P, NB, MW])
        o, y, t_a = sb("o", [P, NB, D]), sb("y", [P, NB, D]), sb("t_a", [P, NB, D])
        rden, gate, la, lb = sb("rden", [P, NB, HEADS]), sb("gate", [P, NB]), sb("la", [P, NB]), sb("lb", [P, NB])
        NPIECE = 4
        BPP = NB // NPIECE
        s_sums = [c.slot(f"s_sums_in{i}") for i in range(NPIECE)]
        t_sums = [s_sums[i].mark(sp.dma_start(sums[0:W, i * BPP:(i + 1) * BPP, :],
                                              sums_d[i * BPP * W:(i + 1) * BPP * W, :].rearrange("(b p) f -> p b f", p=W)))
                  for i in range(NPIECE)]

        dv = c.DVE.mark

        def piece(i):
            bs = slice(i * BPP, (i + 1) * BPP)
            v = lambda x: x[0:W, bs, :]
            row = lambda k: wb[0:W, k:k + 1, :].to_broadcast([W, BPP, D])
            bc = lambda x: x[0:W, bs].unsqueeze(2).to_broadcast([W, BPP, D])
            heads = lambda x: x.rearrange("p b (h c) -> p b h c", h=HEADS)
            t_y = c.POOL.mark(pool.tensor_tensor(v(y), v(xs), row(1), ALU.mult))
            yield t_sums[i]
            yield dv(dve.tensor_scalar(v(rden), sums[0:W, bs, D:MW], 1e-16, None, ALU.add))
            yield dv(dve.reciprocal(v(rden), v(rden)))
            t = dv(dve.tensor_tensor(heads(v(o)), heads(sums[0:W, bs, 0:D]), v(rden).unsqueeze(3).to_broadcast([W, BPP, HEADS, HD]), ALU.mult))
            need(pool, t)
            t_o = c.POOL.mark(pool.tensor_tensor(v(x3n), v(x3n), v(o), ALU.add))
            yield t
            t = dv(dve.tensor_tensor(v(t_a), v(o), row(0), ALU.mult))
            need(dve, t_y)
            yield t
            yield dv(dve.tensor_tensor(v(y), v(y), v(t_a), ALU.add))
            t = dv(dve.tensor_reduce(la[0:W, bs], v(y), AX.X, ALU.add))
            need(act, t)
            t_g = c.ACT.mark(act.activation(gate[0:W, bs], la[0:W, bs], ACT.Sigmoid))
            yield dv(dve.tensor_tensor(v(t_a), v(xs), v(o), ALU.subtract))
            need(dve, t_g)
            yield dv(dve.tensor_tensor(v(t_a), v(t_a), bc(gate), ALU.mult))
            need(dve, t_o)
            yield dv(dve.tensor_tensor(v(y), v(x3n), v(t_a), ALU.add))
            yield dv(dve.tensor_reduce(la[0:W, bs], v(y), AX.X, ALU.add))
            yield dv(dve.tensor_scalar(la[0:W, bs], la[0:W, bs], 1.0 / D, None, ALU.mult))
            t = dv(dve.tensor_tensor(v(y), v(y), bc(la), ALU.subtract))
            need(act, t)
            yield c.ACT.mark(act.activation(v(t_a), v(y), ACT.Square))
            t = dv(dve.tensor_reduce(lb[0:W, bs], v(t_a), AX.X, ALU.add))
            need(act, t)
            yield c.ACT.mark(act.activation(lb[0:W, bs], lb[0:W, bs], ACT.Sqrt, bias=eps[0:W, 0:1], scale=1.0 / D))
            yield dv(dve.reciprocal(lb[0:W, bs], lb[0:W, bs]))
            t = dv(dve.tensor_tensor(v(y), v(y), bc(lb), ALU.mult))
            need(sp, t)
            full = BPP if i < NPIECE - 1 else BPP - 1
            first = i * BPP
            s_out.mark(sp.dma_start(out[first * W:(first + full) * W, :].rearrange("(b p) f -> p b f", p=W), y[0:W, first:first + full, :]))
            yield None

        t = dv(dve.tensor_tensor(wb[0:W, 0, :], wb[0:W, 0, :], wb[0:W, 2, :], ALU.add))
        t = dv(dve.tensor_tensor(wb[0:W, 1, :], wb[0:W, 1, :], wb[0:W, 2, :], ALU.subtract))
        need(pool, t)
        need(dve, t)
        need(act, t_eps)
        chains = [piece(i) for i in range(NPIECE)]
        waits = [next(ch) for ch in chains]
        while chains:
            for k in range(len(chains)):
                need(dve, waits[k])
                waits[k] = next(chains[k], "done")
            chains, waits = [ch for ch, w in zip(chains, waits) if w != "done"], [w for w in waits if w != "done"]
        t = s_out.mark(sp.dma_start(out[(NB - 1) * W:N, :], y[0:LASTROWS, NB - 1, :]))
        need(sp, t)
        nc.all_engine_barrier()


def build(nc, io, out):
    with ExitStack() as ctx:
        c = Ctx(nc, ctx, io)

        def sb(name, shape, dt=F32):
            return ctx.enter_context(nc.sbuf_tensor(name, shape, dt))

        bins = c.dram("bins", (NG * GE, REC), F32)
        at = c.dram("at", (2, NB * P, NP), BF16)
        lastslot = {"f": sb("lastslot_f", [P, NB]), "i": sb("lastslot_i", [P, NB], I32)}
        flags = {k: sb("group_" + k, [P, NG]) for k in ("blk", "same", "last")}
        flags["blki"], flags["lasti"] = sb("group_blki", [1, NG], I32), sb("group_lasti", [1, NG], I32)
        flags["big"] = sb("counts_big", [1, 1], I32)
        s_recs = c.slot("s_recs")

        def load_records(recs):
            return s_recs.mark(c.sp.dma_start(recs[:, :, :, :].rearrange("p g t r -> p g (t r)"),
                                              bins.rearrange("(g p t) r -> p g (t r)", p=P, t=TG)))

        t_scattered = sort_edges(c, bins, flags)
        need(c.sp, t_scattered)
        nc.all_engine_barrier()
        with nc.sbuf_tensor("recs", [P, NG, TG, REC], F32) as recs:
            t_at = build_counts(c, recs, flags, at, load_records(recs), lastslot)
            need(c.sp, *t_at)
            nc.all_engine_barrier()
        x3T = sb("x3T", [P, NP])
        t_x3 = layers(c, at, t_at, flags, x3T)
        nc.all_engine_barrier()
        with nc.sbuf_tensor("recs4", [P, NG, TG, REC], F32) as recs:
            attention(c, recs, lambda: load_records(recs), bins, flags, lastslot, x3T, t_x3, out)


def kernel(**inputs):
    import concourse.bacc as bacc
    from concourse.bass_utils import run_bass_kernel_spmd

    nc = bacc.Bacc("TRN2", target_bir_lowering=False, num_devices=1)
    arrays, io = {}, {}
    for name, a in laid_out(inputs).items():
        arrays["in_" + name] = a
        io[name] = nc.dram_tensor("in_" + name, a.shape, mybir.dt.from_np(a.dtype), kind="ExternalInput").ap()
    out = nc.dram_tensor("out", (N, D), F32, kind="ExternalOutput").ap()
    build(nc, io, out)
    return run_bass_kernel_spmd(nc, [arrays], core_ids=[0]).results[0]["out"]


def laid_out(inputs):
    a = {k: np.asarray(v) for k, v in inputs.items()}
    columns = []
    for name in ("L0_gnn_b0", "L0_gnn_b1", "L0_gnn_b2"):
        columns += list(a[name].reshape(-1, D))
    for t in range(2):
        columns += list(a["L1_gnn_b_ih"][t].reshape(3, D)) + list(a["L1_gnn_b_hh"][t].reshape(3, D))
    columns += list(a["L2_gnn_b_ih"].reshape(3, D)) + list(a["L2_gnn_b_hh"].reshape(3, D))
    out = {
        "src": a["src"], "dst": a["dst"], "edge_type_9": a["edge_type_9"], "edge_attr_16": a["edge_attr_16"],
        "x": a["x"], "w0": a["L0_gnn_W0"], "w1": a["L0_gnn_W1"], "w2": a["L0_gnn_W2"],
        "l1_msg": a["L1_gnn_W_msg"].transpose(0, 2, 1), "l1_ih": a["L1_gnn_W_ih"].transpose(0, 2, 1),
        "l1_hh": a["L1_gnn_W_hh"].transpose(0, 2, 1),
        "l2_msg": a["L2_gnn_W_msg"].T, "l2_ih": a["L2_gnn_W_ih"].T, "l2_hh": a["L2_gnn_W_hh"].T,
        "emb": a["L2_gnn_edge_embed"],
        "bias": np.stack(columns, axis=1),
        "rowb": np.concatenate([a["L1_gnn_b_msg"].reshape(-1), a["L2_gnn_b_msg"]]).reshape(1, -1),
        "qkvs": np.concatenate([a["L3_gnn_W" + k] for k in ("q", "k", "v", "skip")], axis=1),
        "qkvs_b": np.concatenate([a["L3_gnn_b" + k] for k in ("q", "k", "v", "skip")]).reshape(1, -1),
        "bq": a["L3_gnn_bq"].reshape(D, 1),
        "weT": a["L3_gnn_We"].T, "wbeta": a["L3_gnn_Wbeta"].reshape(3, D),
    }
    return {k: np.ascontiguousarray(v) for k, v in out.items()}
```
